# Optimizing a Trainium2 kernel written in Bass

```python
import numpy as np
import jax
import jax.numpy as jnp

def _softmax(x, axis=-1):
    return jax.nn.softmax(x, axis=axis)

def _gelu(x):
    return jax.nn.gelu(x, approximate=True)

def _silu(x):
    return jax.nn.silu(x)

def _sigmoid(x):
    return jax.nn.sigmoid(x)

def _layernorm(x, axis=-1, eps=1e-05):
    m = jnp.mean(x, axis=axis, keepdims=True)
    v = jnp.var(x, axis=axis, keepdims=True)
    return (x - m) / jnp.sqrt(v + eps)

def _scatter_add(tgt, idx, src, axis=0):
    return tgt.at[idx].add(src)

def _segment_sum(src, seg, n):
    return jax.ops.segment_sum(src, seg, n)
kernel_name = 'mk_decoder_preln_d1_seqx_r8_7b2801'

def setup_inputs(seed: int=0):
    np.random.seed(seed)
    _w = jnp.asarray

    def _rec_inputs():
        import jax
        import jax.numpy as jnp
        _rk = jax.random.key(seed)
        x = -0.0002928 + 1 * jax.random.normal(jax.random.fold_in(_rk, 1), (128, 64, 128), jnp.float32)
        _lenS = 64 - jax.random.randint(jax.random.fold_in(_rk, 7), (128,), 0, max(1, 64 // 4) + 1, jnp.int32)
        _lenS2 = 64 - jax.random.randint(jax.random.fold_in(_rk, 8), (128,), 0, max(1, 64 // 4) + 1, jnp.int32)
        _ctx_1024P = jax.random.normal(jax.random.fold_in(_rk, 11), (128, 16, 128), jnp.float32)
        _ctx_1024c = jax.random.dirichlet(jax.random.fold_in(_rk, 511), 0.3 * jnp.ones((16,), jnp.float32), (128, 64))
        _ctx_1024t = jnp.einsum('bsk,bkd->bsd', _ctx_1024c, _ctx_1024P)
        _ctx_1024t = _ctx_1024t * jax.lax.rsqrt(jnp.mean(jnp.square(_ctx_1024t)) + 1e-12) * 0.953939
        ctx_1024 = 2.81802e-05 + 1.00001 * (_ctx_1024t + 0.3 * jax.random.normal(jax.random.fold_in(_rk, 611), (128, 64, 128), jnp.float32))
        return (x, ctx_1024)
    x, ctx_1024 = _rec_inputs()

    def _L0_attn_setup():
        import jax, jax.numpy as jnp
        import numpy as np
        DIM_IN, DIM_K, DIM_V, NH = (128, 128, 128, 16)
        DK, DV = (DIM_K // NH, DIM_V // NH)
        key = jax.random.key(seed)
        kx, kq, kk, kv = jax.random.split(key, 4)
        x = jax.random.normal(kx, (4, 256, DIM_IN), dtype=jnp.float32)
        Wq = jax.random.normal(kq, (DIM_K, DIM_IN), dtype=jnp.float32) / np.sqrt(DIM_IN)
        Wk = jax.random.normal(kk, (DK, DIM_IN), dtype=jnp.float32) / np.sqrt(DIM_IN)
        Wv = jax.random.normal(kv, (DV, DIM_IN), dtype=jnp.float32) / np.sqrt(DIM_IN)
        return {'x': x, 'Wq': Wq, 'Wk': Wk, 'Wv': Wv}
    _L0_attn_all = _L0_attn_setup()
    _L0_attn_in = {k: v for k, v in _L0_attn_all.items() if k in ('Wq', 'Wk', 'Wv')}
    del _L0_attn_all

    def _L0_xattn_setup():
        import jax, jax.numpy as jnp
        import numpy as np
        B, T, S, DIN, H = (64, 64, 32, 128, 128)
        SCALE = 0.02

        def _lstm_cell(x, h, c, Wi, Wh, bi, bh):
            g = x @ Wi.T + bi + h @ Wh.T + bh
            i, f, gg, o = jnp.split(g, 4, axis=-1)
            c2 = jax.nn.sigmoid(f) * c + jax.nn.sigmoid(i) * jnp.tanh(gg)
            h2 = jax.nn.sigmoid(o) * jnp.tanh(c2)
            return (h2, c2)
        key = jax.random.key(seed)
        ks = jax.random.split(key, 12)
        n = jax.random.normal
        return {'inputs': n(ks[0], (B, T, DIN), jnp.float32), 'context': n(ks[1], (B, S, H), jnp.float32), 'Wi0': n(ks[2], (4 * H, DIN + H), jnp.float32) * SCALE, 'Wh0': n(ks[3], (4 * H, H), jnp.float32) * SCALE, 'bi0': jnp.zeros((4 * H,), jnp.float32), 'bh0': jnp.zeros((4 * H,), jnp.float32), 'Wi1': n(ks[4], (4 * H, H), jnp.float32) * SCALE, 'Wh1': n(ks[5], (4 * H, H), jnp.float32) * SCALE, 'bi1': jnp.zeros((4 * H,), jnp.float32), 'bh1': jnp.zeros((4 * H,), jnp.float32), 'Wq': n(ks[6], (H, H), jnp.float32) * SCALE, 'Wo': n(ks[7], (H, 2 * H), jnp.float32) * SCALE, 'bo': jnp.zeros((H,), jnp.float32)}
    _L0_xattn_all = _L0_xattn_setup()
    _L0_xattn_in = {k: v for k, v in _L0_xattn_all.items() if k in ('Wi0', 'Wh0', 'bi0', 'bh0', 'Wi1', 'Wh1', 'bi1', 'bh1', 'Wq', 'Wo', 'bo')}
    del _L0_xattn_all

    def _L0_ffn_setup():
        import jax, jax.numpy as jnp
        import numpy as np
        D_MODEL = 128
        D_FF = 512
        N_EXPERTS = 8
        INIT_SCALE = 0.1

        def _trunc_normal(key, shape, std):
            return std * jax.random.truncated_normal(key, -2.0, 2.0, shape, dtype=jnp.float32)
        key = jax.random.key(seed)
        ks = jax.random.split(key, 5)
        x = jax.random.normal(ks[0], (4, 128, D_MODEL), dtype=jnp.float32)
        router_W = _trunc_normal(ks[1], (D_MODEL, N_EXPERTS), INIT_SCALE / np.sqrt(D_MODEL))
        router_b = jnp.zeros((N_EXPERTS,), dtype=jnp.float32)
        W1 = _trunc_normal(ks[2], (N_EXPERTS, D_MODEL, D_FF), INIT_SCALE / np.sqrt(D_MODEL))
        b1 = jnp.zeros((N_EXPERTS, D_FF), dtype=jnp.float32)
        W2 = _trunc_normal(ks[3], (N_EXPERTS, D_FF, D_MODEL), INIT_SCALE / np.sqrt(D_FF))
        b2 = jnp.zeros((N_EXPERTS, D_MODEL), dtype=jnp.float32)
        return {'x': x, 'router_W': router_W, 'router_b': router_b, 'W1': W1, 'b1': b1, 'W2': W2, 'b2': b2}
    _L0_ffn_all = _L0_ffn_setup()
    _L0_ffn_in = {k: v for k, v in _L0_ffn_all.items() if k in ('router_W', 'router_b', 'W1', 'b1', 'W2', 'b2')}
    del _L0_ffn_all
    return {'x': x, 'ctx_1024': ctx_1024, 'L0_attn_Wq': _L0_attn_in['Wq'], 'L0_attn_Wk': _L0_attn_in['Wk'], 'L0_attn_Wv': _L0_attn_in['Wv'], 'L0_xattn_Wi0': _L0_xattn_in['Wi0'], 'L0_xattn_Wh0': _L0_xattn_in['Wh0'], 'L0_xattn_bi0': _L0_xattn_in['bi0'], 'L0_xattn_bh0': _L0_xattn_in['bh0'], 'L0_xattn_Wi1': _L0_xattn_in['Wi1'], 'L0_xattn_Wh1': _L0_xattn_in['Wh1'], 'L0_xattn_bi1': _L0_xattn_in['bi1'], 'L0_xattn_bh1': _L0_xattn_in['bh1'], 'L0_xattn_Wq': _L0_xattn_in['Wq'], 'L0_xattn_Wo': _L0_xattn_in['Wo'], 'L0_xattn_bo': _L0_xattn_in['bo'], 'L0_ffn_router_W': _L0_ffn_in['router_W'], 'L0_ffn_router_b': _L0_ffn_in['router_b'], 'L0_ffn_W1': _L0_ffn_in['W1'], 'L0_ffn_b1': _L0_ffn_in['b1'], 'L0_ffn_W2': _L0_ffn_in['W2'], 'L0_ffn_b2': _L0_ffn_in['b2']}

def reference(x, ctx_1024, L0_attn_Wq, L0_attn_Wk, L0_attn_Wv, L0_xattn_Wi0, L0_xattn_Wh0, L0_xattn_bi0, L0_xattn_bh0, L0_xattn_Wi1, L0_xattn_Wh1, L0_xattn_bi1, L0_xattn_bh1, L0_xattn_Wq, L0_xattn_Wo, L0_xattn_bo, L0_ffn_router_W, L0_ffn_router_b, L0_ffn_W1, L0_ffn_b1, L0_ffn_W2, L0_ffn_b2):
    import jax
    import jax.numpy as jnp

    def _L0_attn_ref(x, Wq, Wk, Wv):
        import jax, jax.numpy as jnp
        import numpy as np
        DIM_IN, DIM_K, DIM_V, NH = (128, 128, 128, 16)
        DK, DV = (DIM_K // NH, DIM_V // NH)
        B, S, _ = x.shape
        scale = 1.0 / np.sqrt(DK)
        q = (x @ Wq.T).reshape(B, S, NH, DK).transpose(0, 2, 1, 3)
        k = x @ Wk.T
        v = x @ Wv.T
        dist = jnp.einsum('bhqd,bkd->bhqk', q, k) * scale
        dist = jax.nn.softmax(dist, axis=-1)
        att = jnp.einsum('bhqk,bkd->bhqd', dist, v)
        return att.transpose(0, 2, 1, 3).reshape(B, S, DIM_V)

    def _L0_xattn_ref(inputs, context, Wi0, Wh0, bi0, bh0, Wi1, Wh1, bi1, bh1, Wq, Wo, bo):
        import jax, jax.numpy as jnp
        import numpy as np
        B, T, S, DIN, H = (64, 64, 32, 128, 128)
        SCALE = 0.02

        def _lstm_cell(x, h, c, Wi, Wh, bi, bh):
            g = x @ Wi.T + bi + h @ Wh.T + bh
            i, f, gg, o = jnp.split(g, 4, axis=-1)
            c2 = jax.nn.sigmoid(f) * c + jax.nn.sigmoid(i) * jnp.tanh(gg)
            h2 = jax.nn.sigmoid(o) * jnp.tanh(c2)
            return (h2, c2)
        b, t, _ = inputs.shape
        h = Wh0.shape[1]

        def step(carry, x_t):
            h0, c0, h1, c1, a = carry
            xin = jnp.concatenate([x_t, a], axis=-1)
            h0, c0 = _lstm_cell(xin, h0, c0, Wi0, Wh0, bi0, bh0)
            h1, c1 = _lstm_cell(h0, h1, c1, Wi1, Wh1, bi1, bh1)
            q = h1 @ Wq.T
            attn = jax.nn.softmax(jnp.einsum('bh,bsh->bs', q, context), axis=-1)
            mixed = jnp.einsum('bs,bsh->bh', attn, context)
            a2 = jnp.tanh(jnp.concatenate([mixed, h1], axis=-1) @ Wo.T + bo)
            return ((h0, c0, h1, c1, a2), a2)
        z = jnp.zeros((b, h), inputs.dtype)
        carry0 = (z, z, z, z, z)
        _, outs = jax.lax.scan(step, carry0, jnp.swapaxes(inputs, 0, 1))
        return jnp.swapaxes(outs, 0, 1)

    def _L0_ffn_ref(x, router_W, router_b, W1, b1, W2, b2):
        import jax, jax.numpy as jnp
        import numpy as np
        D_MODEL = 128
        D_FF = 512
        N_EXPERTS = 8
        INIT_SCALE = 0.1

        def _trunc_normal(key, shape, std):
            return std * jax.random.truncated_normal(key, -2.0, 2.0, shape, dtype=jnp.float32)
        logits = jnp.einsum('bsd,de->bse', x.astype(jnp.float32), router_W) + router_b
        probs = jax.nn.softmax(logits, axis=-1)
        top1 = jnp.argmax(probs, axis=-1)
        mask = jax.nn.one_hot(top1, N_EXPERTS, dtype=x.dtype)
        gates = mask * probs.astype(x.dtype)
        h = jax.nn.relu(jnp.einsum('bsd,edf->besf', x, W1) + b1[:, None, :])
        y = jnp.einsum('besf,efd->besd', h, W2) + b2[:, None, :]
        out = jnp.einsum('bse,besd->bsd', gates, y)
        return out
    x = x + _L0_attn_ref(_layernorm(x, axis=-1), L0_attn_Wq, L0_attn_Wk, L0_attn_Wv)
    x = x + _L0_xattn_ref(_layernorm(x, axis=-1), ctx_1024, L0_xattn_Wi0, L0_xattn_Wh0, L0_xattn_bi0, L0_xattn_bh0, L0_xattn_Wi1, L0_xattn_Wh1, L0_xattn_bi1, L0_xattn_bh1, L0_xattn_Wq, L0_xattn_Wo, L0_xattn_bo)
    x = x + _L0_ffn_ref(_layernorm(x, axis=-1), L0_ffn_router_W, L0_ffn_router_b, L0_ffn_W1, L0_ffn_b1, L0_ffn_W2, L0_ffn_b2)
    return x

_drawn_inputs = setup_inputs


def setup_inputs(seed=0):
    import zlib

    import numpy as np

    out = dict(_drawn_inputs(seed))
    spreads = {'L0_xattn_bi0': (0.0, 0.8),
     'L0_xattn_bh0': (0.0, 0.8),
     'L0_xattn_bi1': (0.0, 0.717),
     'L0_xattn_bh1': (0.0, 0.632),
     'L0_xattn_bo': (0.0, 0.1),
     'L0_ffn_router_b': (0.0, 0.547),
     'L0_ffn_b1': (0.0, 0.8),
     'L0_ffn_b2': (0.0, 0.558)}
    factors = {'L0_xattn_Wi0': 8.0,
     'L0_xattn_Wh0': 8.0,
     'L0_xattn_Wi1': 8.0,
     'L0_xattn_Wh1': 8.0,
     'L0_xattn_Wq': 6.811,
     'L0_ffn_router_W': 5.1,
     'L0_ffn_W1': 8.0,
     'L0_ffn_W2': 8.0}
    for name, (base, spread) in spreads.items():
        noise = np.random.default_rng([zlib.crc32(name.encode()), seed]).standard_normal(out[name].shape)
        drawn = base * np.exp(spread * noise) if base else spread * noise
        out[name] = jnp.asarray(drawn.astype(out[name].dtype))
    for name, factor in factors.items():
        out[name] = (out[name] * factor).astype(out[name].dtype)
    return out
```

```python
from contextlib import ExitStack

import concourse.bass as bass
from concourse import mybir

F32 = mybir.dt.float32
F16 = mybir.dt.float16
BF16 = mybir.dt.bfloat16
I32 = mybir.dt.int32
ALU = mybir.AluOpType
ACT = mybir.ActivationFunctionType
AX = mybir.AxisListType

P = 128
B, T, D = 128, 64, 128
NPAIR = B // 2
NH, DK = 16, 8
HG = 4
EPS = 1e-5
GB = B // 2
GP = GB // 2
NE, FF = 8, 512
FC = FF // P
S = 4096.0
NTILE = T
WX0, WA0, WH0, WI1, WH1 = 0, 4, 8, 12, 16


def wait(eng, semaphore, value):
    if not (isinstance(value, int) and value <= 0):
        eng.wait_ge(semaphore, value)


def decoder_kernel(nc, x, ctxT, ctx, wqT, wkT, wvT, wi0T, wh0T, bi0, bh0, wi1T, wh1T, bi1, bh1,
                   xwq, woT, bo, rw, rb, w1, b1T, w2, b2, out):
    x1_dram = nc.dram_tensor("x1_scratch", [B, T, D], F32, kind="Internal").ap()

    with ExitStack() as persist:
        def sem(name):
            return persist.enter_context(nc.semaphore(name))

        def sbp(name, shape, dt=F32):
            return persist.enter_context(nc.sbuf_tensor(name, shape, dt))

        ident = sbp("ident", [P, P])
        ones = sbp("ones", [P, P])
        pm = sbp("pm", [P, 2])
        X = sbp("X", [P, NPAIR * D])
        Xp = X[:, :].rearrange("p (n d) -> p n d", d=D)
        XA = X[:, :].rearrange("p (t b) -> p t b", b=B)

        s_const = sem("s_const")

        recurrence_ctx = ExitStack()

        def sbr(name, shape, dt=F32):
            return recurrence_ctx.enter_context(nc.sbuf_tensor(name, shape, dt))

        KH = sbr("KH", [P, 2, B * T], F16)
        VH = sbr("VH", [P, 2, NPAIR, D], F16)
        XT = sbr("XT", [P, 2, T, B], F16)
        WL = sbr("WL", [P, 20, 2, P], F16)
        WO2 = sbr("WO2", [P, 2, P], F16)
        BL = sbr("BL", [P, 2, 4 * P], BF16)
        onesb = sbr("onesb", [P, GB], BF16)
        II = sbr("II", [P, 64])
        sc = sbr("sc", [P, 16])
        smask = sbr("smask", [P, 2 * GB])
        pmask = sbr("pmask", [64, 2, 64])
        bo_sb = sbr("bo_sb", [P, 1])
        S0, S1, SK, SV, I0, I1, IK, IV = range(8)

        with ExitStack() as c1:
            def sb(name, shape, dt=F32):
                return c1.enter_context(nc.sbuf_tensor(name, shape, dt))

            def ps(name, shape, dt=F32):
                return c1.enter_context(nc.psum_tensor(name, shape, dt))
            CT = XT[:, :, :, :].rearrange("p a t b -> p (a t b)").bitcast(F32)
            wl32 = sb("wl32", [P, 20 * P])
            xwq_sb = sb("xwq_sb", [P, P])
            wo_sb = sb("wo_sb", [P, 2, P])
            bb = sb("bb", [P, 4, 4 * P])
            rowm = sb("rowm", [P, 3])
            bw = sb("bw", [P, 4 * P])
            bhi = sb("bhi", [P, 4 * P], BF16)
            mx = sb("mx", [P, 5])
            mxr = sb("mxr", [5, 1])
            dg = sb("dg", [5, 5])
            gm = sb("gm", [P, 5])
            pw = sb("pw", [P, 5])
            tmp = sb("tmp", [P, 8])
            par = sb("par", [64, 2])
            ktmp = sb("ktmp", [P, 2, 512])
            psA = ps("psA", [P, 2, 512])
            psV = ps("psV", [P, 2, 512])
            psS = ps("psS", [P, 512])

            s_ctx = sem("s_ctx")
            s_x = sem("s_x")
            s_w = sem("s_w")
            s_b = sem("s_b")
            s_wo = sem("s_wo")
            s_bz = sem("s_bz")
            v_mx = sem("v_mx")
            p_sc = sem("p_sc")
            v_sc = sem("v_sc")
            v_scale = sem("v_scale")
            p_k = sem("p_k")
            p_v = sem("p_v")
            a_k = sem("a_k")
            a_v = sem("a_v")
            v_k = sem("v_k")
            v_v = sem("v_v")
            a_w = sem("a_w")
            v_w = sem("v_w")
            v_b = sem("v_b")
            v_pm = sem("v_pm")

            with nc.Block() as block:
                @block.sync
                def _(sync):
                    sync.dma_start(CT, ctxT).then_inc(s_ctx, 16)
                    sync.dma_start(xwq_sb[:, :], xwq).then_inc(s_wo, 16)
                    sync.dma_start(wo_sb[:, :, :], woT.rearrange("(a p) n -> p a n", a=2)).then_inc(s_wo, 16)
                    sync.dma_start(bo_sb[:, :], bo.rearrange("(p a) -> p a", a=1)).then_inc(s_wo, 16)
                    sync.dma_start(Xp, x.rearrange("(n two) t d -> (two t) n d", two=2)).then_inc(s_x, 16)
                    sync.wait_ge(s_x, 16)

                @block.scalar
                def _(act):
                    w4 = wl32[:, :].rearrange("p (k n) -> p k n", n=4 * P)
                    act.dma_start(w4[:, 0:2, :], wi0T.rearrange("(a p) n -> p a n", a=2)).then_inc(s_w, 16)
                    act.dma_start(w4[:, 2, :], wh0T).then_inc(s_w, 16)
                    act.dma_start(w4[:, 3, :], wi1T).then_inc(s_w, 16)
                    act.dma_start(w4[:, 4, :], wh1T).then_inc(s_w, 16)
                    act.wait_ge(s_bz, 1)
                    for k, src in enumerate((bi0, bh0, bi1, bh1)):
                        for r in (0, 32, 64):
                            act.dma_start(bb[r:r + 1, k, :], src.rearrange("(a n) -> a n", a=1)).then_inc(s_b, 16)
                    act.wait_ge(v_scale, 1)
                    for blk in range(20):
                        col = (S0 if blk < 12 else S1) + (8 if blk % 4 == 2 else 0)
                        nc.scalar.activation(WL[:, blk, 0, :], wl32[:, blk * P:(blk + 1) * P], ACT.Copy,
                                             scale=sc[:, col:col + 1]).then_inc(a_w, 1)
                    nc.scalar.activation(WO2[:, 0, :], wo_sb[:, 1, :], ACT.Copy,
                                         scale=sc[:, SV:SV + 1]).then_inc(a_w, 1)
                    for c in range(16):
                        act.wait_ge(p_k, c + 1)
                        nc.scalar.activation(KH[:, 0, c * 512:(c + 1) * 512], psA[:, c % 2, :], ACT.Copy,
                                             scale=sc[:, SK:SK + 1]).then_inc(a_k, 1)
                        act.wait_ge(p_v, c + 1)
                        nc.scalar.activation(VH[:, 0, 4 * c:4 * c + 4, :],
                                             psV[:, c % 2, :].rearrange("p (n d) -> p n d", d=D), ACT.Copy,
                                             scale=sc[:, SV:SV + 1]).then_inc(a_v, 1)

                @block.gpsimd
                def _(pool):
                    pool.memset(bb[:, :, :], 0.0).then_inc(s_bz, 1)
                    pool.memset(ident[:, :], 0.0).then_inc(s_const, 1)
                    pool.memset(ones[:, :], 1.0).then_inc(s_const, 1)
                    pool.memset(II[:, :], 0.0).then_inc(s_const, 1)
                    pool.memset(rowm[:, :], 0.0).then_inc(s_const, 1)
                    pool.memset(onesb[:, :], 1.0).then_inc(s_const, 1)
                    pool.wait_ge(s_const, 5)
                    pool.affine_select(out=ident[:, :], in_=ident[:, :], compare_op=ALU.not_equal, fill=1.0,
                                       base=0, pattern=[[-1, P]], channel_multiplier=1).then_inc(s_const, 1)
                    pool.affine_select(out=II[:, :], in_=II[:, :], compare_op=ALU.not_equal, fill=1.0,
                                       base=0, pattern=[[-1, 64]], channel_multiplier=1).then_inc(s_const, 1)
                    pool.affine_select(out=rowm[:, :], in_=rowm[:, :], compare_op=ALU.not_equal, fill=1.0,
                                       base=0, pattern=[[-32, 3]], channel_multiplier=1).then_inc(s_const, 1)
                    pool.wait_ge(s_const, 8)
                    pool.affine_select(out=II[:, :], in_=II[:, :], compare_op=ALU.not_equal, fill=1.0,
                                       base=-64, pattern=[[-1, 64]], channel_multiplier=1).then_inc(s_const, 1)

                @block.tensor
                def _(pe):
                    pe.wait_ge(s_const, 9)
                    pe.wait_ge(v_mx, 5)
                    nc.tensor.transpose(psS[0:5, 0:P], mx[:, :], ident[:, :]).then_inc(p_sc, 1)
                    pe.wait_ge(v_sc, 2)
                    nc.tensor.matmul(psS[:, 128:133], ones[0:5, :], dg[:, :], start=True, stop=True).then_inc(p_sc, 1)
                    pe.wait_ge(s_wo, 48)
                    for c in range(16):
                        if c >= 2:
                            pe.wait_ge(v_k, c - 1)
                        nc.tensor.matmul(psA[:, c % 2, :], xwq_sb[:, :], CT[:, c * 512:(c + 1) * 512],
                                         start=True, stop=True).then_inc(p_k, 1)
                        if c >= 2:
                            pe.wait_ge(v_v, c - 1)
                        for n in range(4):
                            mm = nc.tensor.matmul(psV[:, c % 2, n * P:(n + 1) * P],
                                                  CT[:, (4 * c + n) * P:(4 * c + n + 1) * P], wo_sb[:, 0, :],
                                                  start=True, stop=True)
                        mm.then_inc(p_v, 1)

                @block.vector
                def _(dve):
                    dve.wait_ge(s_w, 64)
                    nc.vector.tensor_reduce(mx[:, 0:1], wl32[:, 0:12 * P], AX.X, ALU.max,
                                            apply_absolute_value=True).then_inc(v_mx, 1)
                    nc.vector.tensor_reduce(mx[:, 1:2], wl32[:, 12 * P:], AX.X, ALU.max,
                                            apply_absolute_value=True).then_inc(v_mx, 1)
                    dve.wait_ge(s_wo, 48)
                    nc.vector.tensor_reduce(mx[:, 2:3], xwq_sb[:, :], AX.X, ALU.max,
                                            apply_absolute_value=True).then_inc(v_mx, 1)
                    nc.vector.tensor_reduce(mx[:, 3:4], wo_sb[:, :, :], AX.XY, ALU.max,
                                            apply_absolute_value=True).then_inc(v_mx, 1)
                    dve.wait_ge(s_ctx, 16)
                    nc.vector.tensor_reduce(mx[:, 4:5], CT, AX.X, ALU.max,
                                            apply_absolute_value=True).then_inc(v_mx, 1)
                    dve.wait_ge(p_sc, 1)
                    nc.vector.tensor_reduce(mxr[:, :], psS[0:5, 0:P], AX.X, ALU.max).then_inc(v_sc, 1)
                    dve.wait_ge(v_sc, 1)
                    nc.vector.tensor_scalar(dg[:, :], ident[0:5, 0:5], mxr[:, 0:1], None, ALU.mult).then_inc(v_sc, 1)
                    dve.wait_ge(p_sc, 2)
                    n = 2

                    def step(ins):
                        nonlocal n
                        n += 1
                        ins.then_inc(v_sc, 1)
                        dve.wait_ge(v_sc, n)
                    step(nc.vector.tensor_scalar(gm[:, :], psS[:, 128:133], 1e-12, 1e12, ALU.max, ALU.min))
                    step(nc.vector.tensor_scalar(pw[:, :].bitcast(I32), gm[:, :].bitcast(I32), 0x7F800000, None,
                                                 ALU.bitwise_and))
                    step(nc.vector.tensor_scalar(tmp[:, 0:2], pw[:, 0:2], 2.0 ** -13, None, ALU.mult))
                    step(nc.vector.scalar_tensor_tensor(tmp[:, 2:3], pw[:, 4:5], 2.0 ** -6, pw[:, 2:3],
                                                        ALU.mult, ALU.mult))
                    step(nc.vector.tensor_scalar(tmp[:, 4:5], pw[:, 4:5], 2.0 ** -8, 2.0 ** -6, ALU.max, ALU.mult))
                    step(nc.vector.tensor_tensor(tmp[:, 3:4], tmp[:, 4:5], pw[:, 3:4], ALU.mult))
                    step(nc.vector.reciprocal(sc[:, 0:4], tmp[:, 0:4]))
                    step(nc.vector.tensor_scalar(sc[:, 4:6], tmp[:, 0:2], 0.5 / S, None, ALU.mult))
                    step(nc.vector.tensor_scalar(sc[:, 6:8], tmp[:, 2:4], 1.0 / S, None, ALU.mult))
                    nc.vector.tensor_scalar(sc[:, 8:10], sc[:, 0:2], 2.0, None, ALU.mult).then_inc(v_scale, 1)
                    dve.wait_ge(s_const, 9)
                    nc.vector.tensor_reduce(pm[:, :], ident[:, :].rearrange("p (h k) -> p h k", h=2), AX.X,
                                            ALU.add).then_inc(v_pm, 1)
                    dve.wait_ge(v_pm, 1)
                    nc.vector.tensor_scalar(
                        smask[:, :].rearrange("p (n h k) -> p n h k", h=2, k=2),
                        pm[:, :].unsqueeze(1).unsqueeze(3).broadcast_to([P, GP, 2, 2]),
                        sc[:, IK:IK + 1], None, ALU.mult).then_inc(v_b, 1)
                    nc.vector.tensor_reduce(par[:, 0:1], ident[0:64, 0:64:2], AX.X, ALU.add).then_inc(v_b, 1)
                    nc.vector.tensor_reduce(par[:, 1:2], ident[0:64, 1:64:2], AX.X, ALU.add).then_inc(v_b, 1)
                    dve.wait_ge(v_b, 3)
                    nc.vector.tensor_scalar(pmask[:, :, :], par[:, :].unsqueeze(2).broadcast_to([64, 2, 64]),
                                            S, None, ALU.mult).then_inc(v_b, 1)
                    dve.wait_ge(s_b, 16 * 12)
                    dve.wait_ge(v_scale, 1)
                    n2 = 4

                    def step2(ins):
                        nonlocal n2
                        n2 += 1
                        ins.then_inc(v_b, 1)
                        dve.wait_ge(v_b, n2)
                    for layer in range(2):
                        step2(nc.vector.tensor_tensor(bw[:, :], bb[:, 2 * layer, :], bb[:, 2 * layer + 1, :], ALU.add))
                        step2(nc.vector.tensor_scalar(bw[:, :], bw[:, :], sc[:, layer:layer + 1], S, ALU.mult, ALU.mult))
                        step2(nc.vector.tensor_scalar(bw[:, 2 * P:3 * P], bw[:, 2 * P:3 * P], 2.0, None, ALU.mult))
                        for k in range(3):
                            step2(nc.vector.tensor_copy(bhi[:, :], bw[:, :]))
                            if k == 0:
                                step2(nc.vector.tensor_scalar(BL[:, layer, :], bhi[:, :], rowm[:, 0:1], None, ALU.mult))
                            else:
                                step2(nc.vector.scalar_tensor_tensor(BL[:, layer, :], bhi[:, :], rowm[:, k:k + 1],
                                                                     BL[:, layer, :], ALU.mult, ALU.add))
                            step2(nc.vector.tensor_tensor(bw[:, :], bw[:, :], bhi[:, :], ALU.subtract))
                    for blk in range(20):
                        col = (S0 if blk < 12 else S1) + (8 if blk % 4 == 2 else 0)
                        dve.wait_ge(a_w, blk + 1)
                        nc.vector.scalar_tensor_tensor(WL[:, blk, 1, :], wl32[:, blk * P:(blk + 1) * P],
                                                       sc[:, col:col + 1], WL[:, blk, 0, :],
                                                       ALU.mult, ALU.subtract).then_inc(v_w, 1)
                    dve.wait_ge(a_w, 21)
                    nc.vector.scalar_tensor_tensor(WO2[:, 1, :], wo_sb[:, 1, :], sc[:, SV:SV + 1], WO2[:, 0, :],
                                                   ALU.mult, ALU.subtract).then_inc(v_w, 1)
                    for c in range(16):
                        dve.wait_ge(a_k, c + 1)
                        nc.vector.scalar_tensor_tensor(KH[:, 1, c * 512:(c + 1) * 512], psA[:, c % 2, :],
                                                       sc[:, SK:SK + 1], KH[:, 0, c * 512:(c + 1) * 512],
                                                       ALU.mult, ALU.subtract).then_inc(v_k, 1)
                        dve.wait_ge(a_v, c + 1)
                        nc.vector.scalar_tensor_tensor(
                            VH[:, 1, 4 * c:4 * c + 4, :].rearrange("p n d -> p (n d)"), psV[:, c % 2, :],
                            sc[:, SV:SV + 1], VH[:, 0, 4 * c:4 * c + 4, :].rearrange("p n d -> p (n d)"),
                            ALU.mult, ALU.subtract).then_inc(v_v, 1)

        with ExitStack() as c2:
            def sb(name, shape, dt=F32):
                return c2.enter_context(nc.sbuf_tensor(name, shape, dt))

            def ps(name, shape, dt=F32):
                return c2.enter_context(nc.psum_tensor(name, shape, dt))
            wq_sb = sb("wq_sb", [P, P])
            wk_sb = sb("wk_sb", [P, DK])
            wv_sb = sb("wv_sb", [P, DK])
            wkr = sb("wkr", [P, NH, DK])
            m4 = sb("m4", [P, HG])
            ob = sb("ob", [P, 2, 2, DK])
            st6 = sb("st6", [P, NPAIR, 6])
            mv = sb("mv", [P, NPAIR, 2])
            sd = sb("sd", [P, NPAIR])
            rs = sb("rs", [P, NPAIR])
            xn = sb("xn", [P, 2, D])
            xnT = sb("xnT", [P, 2, 2, 2, 64])
            qT = sb("qT", [P, 2, P])
            KB = sb("KB", [P, 2, 2, HG, 64])
            VB = sb("VB", [P, 2, 2, 2, DK])
            pmx = sb("pmx", [P, 2, NH])
            pr = sb("pr", [P, NH, 64])
            prT = sb("prT", [P, 8, P])
            pv = sb("pv", [P, 512])
            rden = sb("rden", [P, NH])
            yv = sb("yv", [P, NH, DK])
            psSc = ps("psSc", [P, 4, 512])
            psQ = ps("psQ", [P, 512])
            psT = ps("psT", [P, 2, 512])
            psO = ps("psO", [P, 512])

            s_w2 = sem("s_w2")
            v_c = sem("v_c")
            v_st = sem("v_st")
            a_sd = sem("a_sd")
            v_rs = sem("v_rs")
            v_xn = sem("v_xn")
            p_xt = sem("p_xt")
            a_xt = sem("a_xt")
            p_q = sem("p_q")
            a_q = sem("a_q")
            v_kb = sem("v_kb")
            v_vb = sem("v_vb")
            p_s = sem("p_s")
            v_m = sem("v_m")
            v_sub = sem("v_sub")
            a_ex = sem("a_ex")
            p_pt = sem("p_pt")
            a_pt = sem("a_pt")
            p_o = sem("p_o")
            a_o = sem("a_o")
            p_ot = sem("p_ot")
            v_rd = sem("v_rd")
            v_y = sem("v_y")
            v_x1 = sem("v_x1")

            def even_odd(t):
                return t[:, :].rearrange("p (n d) -> p n d", d=D)

            with nc.Block() as block:
                @block.sync
                def _(sync):
                    sync.dma_start(wq_sb[:, :], wqT).then_inc(s_w2, 16)
                    sync.dma_start(wk_sb[:, :], wkT).then_inc(s_w2, 16)
                    sync.dma_start(wv_sb[:, :], wvT).then_inc(s_w2, 16)

                @block.tensor
                def _(pe):
                    pe.wait_ge(v_c, 4)

                    def front(i, u):
                        pe.wait_ge(v_xn, i + 1)
                        wait(pe, v_vb, i)
                        nc.tensor.transpose(psQ[:, 0:128], xn[:, u, :], ident[:, :]).then_inc(p_xt, 1)
                        pe.wait_ge(a_xt, i + 1)
                        nc.tensor.matmul(psQ[:, 128:256], wq_sb[:, :], xnT[:, u, :, 0, :], start=True, stop=True)
                        nc.tensor.matmul(psQ[:, 256:384], wkr[:, :, :].rearrange("p h d -> p (h d)"), xnT[:, u, :, 0, :],
                                         start=True, stop=True)
                        for b in range(2):
                            mm = nc.tensor.matmul(
                                psQ[:, 384 + 8 * b:392 + 8 * b],
                                xnT[:, u, b, :, :].rearrange("p a k -> p (a k)"),
                                wv_sb[:, :], start=True, stop=True)
                        mm.then_inc(p_q, 1)

                    def scores(i, u):
                        pe.wait_ge(a_q, i + 1)
                        pe.wait_ge(v_kb, i + 1)
                        wait(pe, v_sub, i)
                        for b in range(2):
                            for g in range(4):
                                mm = nc.tensor.matmul(
                                    psSc[64 * b:64 * b + 64, g, 0:256],
                                    qT[32 * g:32 * g + 32, u, 64 * b:64 * b + 64],
                                    KB[32 * g:32 * g + 32, u, b, :, :].rearrange("p h k -> p (h k)"),
                                    start=True, stop=True)
                        mm.then_inc(p_s, 1)

                    def back(i, u):
                        pe.wait_ge(a_ex, i + 1)
                        wait(pe, v_x1, 2 * i)
                        for hp in range(8):
                            mm = nc.tensor.transpose(psT[:, hp // 4, (hp % 4) * P:(hp % 4 + 1) * P],
                                                     pr[:, 2 * hp:2 * hp + 2, :].rearrange("p h k -> p (h k)"),
                                                     ident[:, :])
                            if hp % 4 == 3:
                                mm.then_inc(p_pt, 1)
                        pe.wait_ge(a_pt, 2 * i + 2)
                        for hp in range(8):
                            j, hh = hp % 4, hp // 4
                            nc.tensor.matmul(psO[32 * j:32 * j + 32, hh * P:(hh + 1) * P],
                                             VB[:, u, :, :, :].rearrange("p a b d -> p (a b d)"), prT[:, hp, :],
                                             start=True, stop=True)
                        for hp in range(8):
                            j, hh = hp % 4, hp // 4
                            mm = nc.tensor.matmul(psO[32 * j:32 * j + 32, 256 + hh * P:256 + (hh + 1) * P],
                                                  ob[:, :, :, :].rearrange("p a b d -> p (a b d)"), prT[:, hp, :],
                                                  start=True, stop=True)
                        mm.then_inc(p_o, 1)
                        pe.wait_ge(a_o, i + 1)
                        for k in range(4):
                            mm = nc.tensor.transpose(psT[:, 0, k * P:(k + 1) * P], pv[:, k * P:(k + 1) * P], ident[:, :])
                        mm.then_inc(p_ot, 1)

                    front(0, 0)
                    scores(0, 0)
                    def two(i):
                        front(i + 1, 1)
                        scores(i + 1, 1)
                        back(i, 0)
                        front(i + 2, 0)
                        scores(i + 2, 0)
                        back(i + 1, 1)

                    two(0)
                    with pe.Fori(2, NPAIR - 2, 2) as i:
                        two(i)
                    front(NPAIR - 1, 1)
                    scores(NPAIR - 1, 1)
                    back(NPAIR - 2, 0)
                    back(NPAIR - 1, 1)

                @block.scalar
                def _(act):
                    act.wait_ge(v_st, 2 * NPAIR + 1)
                    nc.scalar.activation(sd[:, :], sd[:, :], ACT.Sqrt).then_inc(a_sd, 1)

                    def front(i, u):
                        act.wait_ge(p_xt, i + 1)
                        nc.scalar.activation(xnT[:, u, :, :, :],
                                             psQ[:, 0:128].rearrange("p (b k) -> p b k", b=2).unsqueeze(2).broadcast_to([P, 2, 2, 64]),
                                             ACT.Copy).then_inc(a_xt, 1)
                        act.wait_ge(p_q, i + 1)
                        nc.scalar.activation(qT[:, u, :], psQ[:, 128:256], ACT.Copy,
                                             scale=DK ** -0.5).then_inc(a_q, 1)

                    def back(i, u):
                        act.wait_ge(v_sub, i + 1)
                        nc.scalar.activation(pr[:, :, :], pr[:, :, :], ACT.Exp).then_inc(a_ex, 1)
                        for k in range(2):
                            act.wait_ge(p_pt, 2 * i + k + 1)
                            nc.scalar.activation(prT[:, 4 * k:4 * k + 4, :].rearrange("p n t -> p (n t)"),
                                                 psT[:, k, :], ACT.Copy).then_inc(a_pt, 1)
                        act.wait_ge(p_o, i + 1)
                        nc.scalar.activation(pv[:, :], psO[:, :], ACT.Copy).then_inc(a_o, 1)

                    front(0, 0)
                    def two(i):
                        front(i + 1, 1)
                        back(i, 0)
                        front(i + 2, 0)
                        back(i + 1, 1)

                    two(0)
                    with act.Fori(2, NPAIR - 2, 2) as i:
                        two(i)
                    front(NPAIR - 1, 1)
                    back(NPAIR - 2, 0)
                    back(NPAIR - 1, 1)

                @block.vector
                def _(dve):
                    dve.wait_ge(s_w2, 48)
                    nc.vector.tensor_copy(wkr[:, :, :], wk_sb[:, :].unsqueeze(1).broadcast_to([P, NH, DK])).then_inc(v_c, 1)
                    nc.vector.tensor_reduce(m4[:, :], ident[:, :].rearrange("p (a h d) -> p h a d", a=4, h=HG),
                                            AX.XY, ALU.add).then_inc(v_c, 1)
                    for b in range(2):
                        nc.vector.tensor_copy(ob[:, b, :, :], pm[:, :].unsqueeze(2).broadcast_to([P, 2, DK])).then_inc(v_c, 1)
                    dve.wait_ge(v_c, 4)
                    for n in range(NPAIR):
                        nc.vector.bn_stats(st6[:, n, :], Xp[:, n, :]).then_inc(v_st, 1)
                    for n in range(NPAIR):
                        dve.wait_ge(v_st, n + 1)
                        nc.vector.bn_aggr(mv[:, n, :], st6[:, n, :]).then_inc(v_st, 1)
                    dve.wait_ge(v_st, 2 * NPAIR)
                    nc.vector.tensor_scalar(sd[:, :], mv[:, :, 1], EPS, None, ALU.add).then_inc(v_st, 1)
                    dve.wait_ge(a_sd, 1)
                    nc.vector.reciprocal(rs[:, :], sd[:, :]).then_inc(v_rs, 1)
                    dve.wait_ge(v_rs, 1)

                    def front(i, u, xi):
                        nc.vector.tensor_scalar(xn[:, u, :], xi["x"], xi["mean"], xi["rs"],
                                                ALU.subtract, ALU.mult).then_inc(v_xn, 1)
                        dve.wait_ge(a_q, i + 1)
                        nc.vector.tensor_tensor(
                            KB[:, u, :, :, :],
                            psQ[:, 256:384].rearrange("p (b k) -> p b k", b=2).unsqueeze(2).broadcast_to([P, 2, HG, 64]),
                            m4[:, :].unsqueeze(1).unsqueeze(3).broadcast_to([P, 2, HG, 64]),
                            ALU.mult).then_inc(v_kb, 1)
                        nc.vector.tensor_tensor(
                            VB[:, u, :, :, :],
                            psQ[:, 384:400].rearrange("p (b d) -> p b d", b=2).unsqueeze(2).broadcast_to([P, 2, 2, DK]),
                            pm[:, :].unsqueeze(1).unsqueeze(3).broadcast_to([P, 2, 2, DK]),
                            ALU.mult).then_inc(v_vb, 1)

                    def mid(i, u):
                        dve.wait_ge(p_s, i + 1)
                        sv = psSc[:, :, 0:256].rearrange("p g (h k) -> p g h k", h=HG)
                        nc.vector.tensor_reduce(pmx[:, u, :].rearrange("p (g h) -> p g h", g=4), sv, AX.X, ALU.max).then_inc(v_m, 1)
                        dve.wait_ge(v_m, i + 1)
                        wait(dve, p_pt, 2 * i)
                        nc.vector.tensor_tensor(
                            pr[:, :, :].rearrange("p (g h) k -> p g h k", g=4), sv,
                            pmx[:, u, :].rearrange("p (g h) -> p g h", g=4).unsqueeze(3).broadcast_to([P, 4, HG, 64]),
                            ALU.subtract).then_inc(v_sub, 1)

                    def back(i, u, xi):
                        dve.wait_ge(p_ot, i + 1)
                        tr = psT[:, 0, :].rearrange("p (k j b h d) -> p k j b h d", k=4, j=4, b=2, h=2)
                        for b in range(2):
                            q = slice(64 * b, 64 * b + 64)
                            nc.vector.reciprocal(rden[q, :].rearrange("p (k h) -> p k h", h=2),
                                                 psT[q, 0, 256:512].rearrange("p (k b h d) -> p k b h d", b=2, h=2, d=DK)[:, :, b, :, 0]).then_inc(v_rd, 1)
                        for b in range(2):
                            q = slice(64 * b, 64 * b + 64)
                            dve.wait_ge(v_rd, 2 * i + 2)
                            nc.vector.tensor_tensor(
                                yv[q, :, :].rearrange("p (k h) d -> p k h d", h=2),
                                psT[q, 0, 0:256].rearrange("p (k b h d) -> p k b h d", b=2, h=2, d=DK)[:, :, b, :, :],
                                rden[q, :].rearrange("p (k h) -> p k h", h=2).unsqueeze(3).broadcast_to([64, 8, 2, DK]),
                                ALU.mult).then_inc(v_y, 1)
                        for b in range(2):
                            q = slice(64 * b, 64 * b + 64)
                            dve.wait_ge(v_y, 2 * i + 1 + b)
                            nc.vector.tensor_tensor(xi["x"][q, :], xi["x"][q, :],
                                                    yv[q, :, :].rearrange("p h d -> p (h d)"), ALU.add).then_inc(v_x1, 1)

                    def at(i):
                        return {"x": X[:, bass.ds(i * D, D)],
                                "mean": mv[:, :, :].rearrange("p n k -> p (n k)")[:, bass.ds(i * 2, 1)],
                                "rs": rs[:, bass.ds(i, 1)]}

                    front(0, 0, at(0))
                    mid(0, 0)
                    def two(i):
                        front(i + 1, 1, at(i + 1))
                        mid(i + 1, 1)
                        back(i, 0, at(i))
                        front(i + 2, 0, at(i + 2))
                        mid(i + 2, 0)
                        back(i + 1, 1, at(i + 1))

                    two(0)
                    with dve.Fori(2, NPAIR - 2, 2) as i:
                        two(i)
                    front(NPAIR - 1, 1, at(NPAIR - 1))
                    mid(NPAIR - 1, 1)
                    back(NPAIR - 2, 0, at(NPAIR - 2))
                    back(NPAIR - 1, 1, at(NPAIR - 1))

        with ExitStack() as c3:
            def sb(name, shape, dt=F32):
                return c3.enter_context(nc.sbuf_tensor(name, shape, dt))
            st6 = sb("st6b", [P, NPAIR, 6])
            mv = sb("mvb", [P, NPAIR, 2])
            sd = sb("sdb", [P, NPAIR])
            rs = sb("rsb", [P, NPAIR])
            xn = sb("xnb", [P, 8, D])
            psX = c3.enter_context(nc.psum_tensor("psX", [P, 2, 512], F32))
            s_x1 = sem("s_x1")
            v_st = sem("v_st3")
            a_sd = sem("a_sd3")
            v_rs = sem("v_rs3")
            v_xn = sem("v_xn3")
            p_xt = sem("p_xt3")
            a_xt = sem("a_xt3")
            v_xt = sem("v_xt3")
            v_st3z = sem("v_st3z")
            NC4 = NPAIR // 4
            with nc.Block() as block:
                @block.sync
                def _(sync):
                    sync.dma_start(x1_dram.rearrange("(n two) t d -> (two t) n d", two=2), Xp).then_inc(s_x1, 16)
                    sync.wait_ge(s_x1, 16)

                @block.tensor
                def _(pe):
                    for c in range(NC4):
                        if c >= 2:
                            pe.wait_ge(v_xt, c - 1)
                        for n in range(4):
                            pe.wait_ge(v_xn, 4 * c + n + 1)
                            mm = nc.tensor.transpose(psX[:, c % 2, n * P:(n + 1) * P], xn[:, (4 * c + n) % 8, :], ident[:, :])
                        mm.then_inc(p_xt, 1)

                def parts(part, c):
                    return XT[:, part, :, 8 * c:8 * c + 8].rearrange("p t b -> p b t")

                @block.scalar
                def _(act):
                    act.wait_ge(v_st3z, 1)
                    nc.scalar.activation(sd[:, :], sd[:, :], ACT.Sqrt).then_inc(a_sd, 1)
                    for c in range(NC4):
                        act.wait_ge(p_xt, c + 1)
                        nc.scalar.activation(parts(0, c), psX[:, c % 2, :].rearrange("p (b t) -> p b t", t=T),
                                             ACT.Copy, scale=S).then_inc(a_xt, 1)

                @block.vector
                def _(dve):
                    for n in range(NPAIR):
                        nc.vector.bn_stats(st6[:, n, :], Xp[:, n, :]).then_inc(v_st, 1)
                    for n in range(NPAIR):
                        dve.wait_ge(v_st, n + 1)
                        nc.vector.bn_aggr(mv[:, n, :], st6[:, n, :]).then_inc(v_st, 1)
                    dve.wait_ge(v_st, 2 * NPAIR)
                    nc.vector.tensor_scalar(sd[:, :], mv[:, :, 1], EPS, None, ALU.add).then_inc(v_st3z, 1)
                    dve.wait_ge(a_sd, 1)
                    nc.vector.reciprocal(rs[:, :], sd[:, :]).then_inc(v_rs, 1)
                    dve.wait_ge(v_rs, 1)
                    for c in range(NC4 + 1):
                        if c < NC4:
                            if c >= 2:
                                dve.wait_ge(p_xt, c - 1)
                            for n in range(4 * c, 4 * c + 4):
                                nc.vector.tensor_scalar(xn[:, n % 8, :], Xp[:, n, :], mv[:, n, 0:1], rs[:, n:n + 1],
                                                        ALU.subtract, ALU.mult).then_inc(v_xn, 1)
                        if c >= 1:
                            k = c - 1
                            dve.wait_ge(a_xt, k + 1)
                            nc.vector.scalar_tensor_tensor(
                                parts(1, k), psX[:, k % 2, :].rearrange("p (b t) -> p b t", t=T), S, parts(0, k),
                                ALU.mult, ALU.subtract).then_inc(v_xt, 1)

        with ExitStack() as c4:
            def sb(name, shape, dt=F32):
                return c4.enter_context(nc.sbuf_tensor(name, shape, dt))

            class Group:
                pass
            G = []
            for g in range(2):
                q = Group()
                q.g = g
                t = "ab"[g]
                q.xs = sb(f"xs_{t}", [P, 2, GB], F16)
                q.gt = [sb(f"gt{l}_{t}", [P, 4, GB]) for l in range(2)]
                q.u = [sb(f"u{l}_{t}", [P, 2, GB]) for l in range(2)]
                q.c = [sb(f"c{l}_{t}", [P, GB]) for l in range(2)]
                q.tc = [sb(f"tc{l}_{t}", [P, GB]) for l in range(2)]
                q.os = [sb(f"os{l}_{t}", [P, GB]) for l in range(2)]
                q.h32 = [sb(f"h32{l}_{t}", [P, GB]) for l in range(2)]
                q.h = [sb(f"h{l}_{t}", [P, GB, 2], F16) for l in range(2)]
                q.a = sb(f"a_{t}", [P, GB, 2], F16)
                q.a32 = sb(f"a32_{t}", [P, GB])
                q.sm = sb(f"sm_{t}", [P, GB, 2])
                q.nm = sb(f"nm_{t}", [64, 1])
                q.p = sb(f"p_{t}", [64, 64])
                q.sum = sb(f"sum_{t}", [64, 1])
                q.r = sb(f"r_{t}", [64, 1])
                q.pe = sb(f"pe_{t}", [P, P])
                q.pm = sb(f"pmv_{t}", [P, GB, 2], F16)
                q.ar = sb(f"ar_{t}", [P, GB])
                ps = lambda n: c4.enter_context(nc.psum_tensor(f"{n}_{t}", [P, 512], F32))
                q.z = [ps("z0"), ps("z1")]
                q.S = ps("sc")
                q.M = ps("mx")
                q.s_xs = sem(f"xs_{t}")
                q.s_xu = sem(f"xu_{t}")
                q.s_sc = sem(f"sc_{t}")
                q.s_st = sem(f"st_{t}")
                q.s_pt = sem(f"pt_{t}")
                q.s_mx = sem(f"mx_{t}")
                q.s_ex = sem(f"ex_{t}")
                q.s_ta = sem(f"ta_{t}")
                q.s_sm = sem(f"sm_{t}")
                q.s_nm = sem(f"nm_{t}")
                q.s_r = sem(f"r_{t}")
                q.s_pe = sem(f"pe_{t}")
                q.s_pm = sem(f"pm_{t}")
                q.s_ar = sem(f"ar_{t}")
                q.s_ah = sem(f"ah_{t}")
                q.s_ao = sem(f"ao_{t}")
                q.s_z = [sem(f"z{l}_{t}") for l in range(2)]
                q.s_tg = [sem(f"tg{l}_{t}") for l in range(2)]
                q.s_tc = [sem(f"tc{l}_{t}") for l in range(2)]
                q.s_uv = [sem(f"uv{l}_{t}") for l in range(2)]
                q.s_c = [sem(f"c{l}_{t}") for l in range(2)]
                q.s_os = [sem(f"os{l}_{t}") for l in range(2)]
                q.s_h = [sem(f"h{l}_{t}") for l in range(2)]
                q.s_h32 = [sem(f"h32{l}_{t}") for l in range(2)]
                G.append(q)
            s_zero = sem("s_zero")

            def run_halves(half, eng):
                half(G[0], None, 0, None)
                half(G[1], G[0], 0, 0)
                half(G[0], G[1], 1, 0)
                with eng.Fori(1, T - 1) as t:
                    half(G[1], G[0], t, t)
                    half(G[0], G[1], t + 1, t)
                half(G[1], G[0], T - 1, T - 1)
                half(None, G[1], None, T - 1)

            with nc.Block() as block:
                @block.tensor
                def _(pe):
                    pe.wait_ge(s_zero, 16)

                    def product(out, blk, mov, first=False):
                        for k, (w, m) in enumerate(((0, 0), (1, 0), (0, 1))):
                            mm = nc.tensor.matmul(out, WL[:, blk, w, :], mov[m], start=False, stop=False,
                                                  skip_group_check=True)
                        return mm

                    def gates(q, layer, blk, mov):
                        for j in range(4):
                            mm = product(q.z[layer][:, j * GB:(j + 1) * GB], blk + j, mov)
                        return mm

                    def bias(q, layer):
                        for j in range(4):
                            nc.tensor.matmul(q.z[layer][:, j * GB:(j + 1) * GB], BL[:, layer, j * P:(j + 1) * P],
                                             onesb[:, :], start=(j == 0), stop=False, skip_group_check=True)

                    def half(L, A, lt, at):
                        if L:
                            bias(L, 0)
                            pe.wait_ge(L.s_xs, lt + 1)
                            gates(L, 0, WX0, [L.xs[:, k, :] for k in range(2)]).then_inc(L.s_xu, 1)
                            gates(L, 0, WH0, [L.h[0][:, :, k] for k in range(2)])
                            bias(L, 1)
                            gates(L, 1, WH1, [L.h[1][:, :, k] for k in range(2)])
                        if A:
                            pe.wait_ge(A.s_h[1], 2 * at + 2)
                            for n in range(GP):
                                pair = A.g * GP + n
                                for k in range(2):
                                    mm = nc.tensor.matmul(A.S[:, 4 * n:4 * n + 4], KH[:, k, pair * P:(pair + 1) * P],
                                                          A.h[1][:, 2 * n:2 * n + 2, :].rearrange("p b k -> p (b k)"),
                                                          start=(k == 0), stop=(k == 1))
                            mm.then_inc(A.s_sc, 1)
                        if L:
                            wait(pe, L.s_ah, 2 * lt)
                            gates(L, 0, WA0, [L.a[:, :, k] for k in range(2)]).then_inc(L.s_z[0], 1)
                        if A:
                            for k, (w, m) in enumerate(((0, 0), (1, 0), (0, 1))):
                                nc.tensor.matmul(A.M[:, 0:2 * GB:2], WO2[:, w, :], A.h[1][:, :, m],
                                                 start=(k == 0), stop=False, skip_group_check=True)
                            pe.wait_ge(A.s_sm, at + 1)
                            for k in range(2):
                                mm = nc.tensor.matmul(A.S[0:64, 128:192], A.sm[:, :, k], II[:, :],
                                                      start=(k == 0), stop=(k == 1))
                            mm.then_inc(A.s_st, 1)
                            pe.wait_ge(A.s_pe, at + 1)
                            nc.tensor.transpose(A.S[:, 256:384], A.pe[:, :], ident[:, :]).then_inc(A.s_pt, 1)
                        if L:
                            pe.wait_ge(L.s_h[0], 2 * lt + 2)
                            gates(L, 1, WI1, [L.h[0][:, :, k] for k in range(2)]).then_inc(L.s_z[1], 1)
                        if A:
                            pe.wait_ge(A.s_pm, 2 * at + 2)
                            for n in range(GP):
                                pair = A.g * GP + n
                                for k in range(2):
                                    mm = nc.tensor.matmul(A.M[:, 4 * n:4 * n + 4], VH[:, k, pair, :],
                                                          A.pm[:, 2 * n:2 * n + 2, :].rearrange("p b k -> p (b k)"),
                                                          start=False, stop=False, skip_group_check=True)
                            mm.then_inc(A.s_mx, 1)

                    run_halves(half, pe)

                @block.scalar
                def _(act):
                    def half(L, A, lt, at):
                        def gate_tanh(l):
                            act.wait_ge(L.s_z[l], lt + 1)
                            nc.scalar.activation(L.gt[l][:, :, :].rearrange("p g b -> p (g b)"), L.z[l][:, 0:4 * GB],
                                                 ACT.Tanh, scale=sc[:, I0 + l:I0 + l + 1]).then_inc(L.s_tg[l], 1)

                        def out_gate(l):
                            act.wait_ge(L.s_tg[l], lt + 1)
                            nc.scalar.activation(L.os[l][:, :], L.gt[l][:, 3, :], ACT.Copy, scale=S / 2,
                                                 bias=S / 2).then_inc(L.s_os[l], 1)

                        def cell_tanh(l):
                            act.wait_ge(L.s_c[l], lt + 1)
                            nc.scalar.activation(L.tc[l][:, :], L.c[l][:, :], ACT.Tanh, scale=0.5).then_inc(L.s_tc[l], 1)
                        if L:
                            gate_tanh(0)
                            out_gate(0)
                        if A:
                            act.wait_ge(A.s_nm, at + 1)
                            nc.scalar.activation(A.p[:, :], A.S[0:64, 128:192], ACT.Exp, bias=A.nm[:, 0:1],
                                                 accum_out=A.sum[:, 0:1]).then_inc(A.s_ex, 1)
                        if L:
                            cell_tanh(0)
                            gate_tanh(1)
                            out_gate(1)
                            cell_tanh(1)
                        if A:
                            act.wait_ge(A.s_ar, at + 1)
                            wait(act, A.s_ao, at)
                            nc.scalar.activation(A.a32[:, :], A.ar[:, :], ACT.Tanh, bias=bo_sb[:, 0:1],
                                                 scale=sc[:, IV:IV + 1]).then_inc(A.s_ta, 1)
                    run_halves(half, act)

                @block.gpsimd
                def _(pool):
                    for q in G:
                        for tile in (q.h[0], q.h[1], q.a):
                            pool.memset(tile[:, :, :], 0.0).then_inc(s_zero, 1)
                        for tile in (q.c[0], q.c[1]):
                            pool.memset(tile[:, :], 0.0).then_inc(s_zero, 1)
                        for k in range(2):
                            pool.tensor_copy(q.xs[:, k, :], XT[:, k, 0, q.g * GB:(q.g + 1) * GB]).then_inc(s_zero, 1)
                        pool.memset(q.pe[:, :], 0.0).then_inc(s_zero, 1)
                    pool.wait_ge(s_zero, 16)
                    for q in G:
                        pool.sem_inc(q.s_xs, 1)

                    def half(L, A, lt, at):
                        if L:
                            if not (isinstance(lt, int) and lt == T - 1):
                                pool.wait_ge(L.s_xu, lt + 1)
                                pool.tensor_copy(L.xs[:, :, :], XTn(L, lt + 1)).then_inc(L.s_xs, 1)
                        if A:
                            pool.wait_ge(A.s_ta, at + 1)
                            pool.tensor_copy(X[:, bass.ds(at * B + A.g * GB, GB)], A.a32[:, :]).then_inc(A.s_ao, 1)

                    def XTn(L, t):
                        return XTf[:, :, bass.ds(t * B + L.g * GB, GB)]
                    XTf = XT[:, :, :, :].rearrange("p k t b -> p k (t b)")

                    half(G[0], None, 0, None)
                    half(G[1], G[0], 0, 0)
                    half(G[0], G[1], 1, 0)
                    with pool.Fori(1, T - 2) as t:
                        half(G[1], G[0], t, t)
                        half(G[0], G[1], t + 1, t)
                    half(G[1], G[0], T - 2, T - 2)
                    half(G[0], G[1], T - 1, T - 2)
                    half(G[1], G[0], T - 1, T - 1)
                    half(None, G[1], None, T - 1)

                @block.vector
                def _(dve):
                    dve.wait_ge(s_zero, 16)

                    def half(L, A, lt, at):
                        def cell(l):
                            dve.wait_ge(L.s_tg[l], lt + 1)
                            nc.vector.scalar_tensor_tensor(L.u[l][:, 0, :], L.gt[l][:, 1, :], 1.0, L.c[l][:, :],
                                                           ALU.add, ALU.mult).then_inc(L.s_uv[l], 1)
                            nc.vector.scalar_tensor_tensor(L.u[l][:, 1, :], L.gt[l][:, 0, :], 1.0, L.gt[l][:, 2, :],
                                                           ALU.add, ALU.mult).then_inc(L.s_uv[l], 1)
                            dve.wait_ge(L.s_uv[l], 2 * lt + 2)
                            nc.vector.scalar_tensor_tensor(L.c[l][:, :], L.u[l][:, 0, :], 0.5, L.u[l][:, 1, :],
                                                           ALU.mult, ALU.add).then_inc(L.s_c[l], 1)

                        def hidden(l):
                            dve.wait_ge(L.s_tc[l], lt + 1)
                            dve.wait_ge(L.s_os[l], lt + 1)
                            nc.vector.tensor_tensor(L.h[l][:, :, 0], L.os[l][:, :], L.tc[l][:, :],
                                                    ALU.mult).then_inc(L.s_h[l], 1)
                            nc.vector.tensor_tensor(L.h32[l][:, :], L.os[l][:, :], L.tc[l][:, :],
                                                    ALU.mult).then_inc(L.s_h32[l], 1)
                            dve.wait_ge(L.s_h32[l], lt + 1)
                            dve.wait_ge(L.s_h[l], 2 * lt + 1)
                            nc.vector.tensor_tensor(L.h[l][:, :, 1], L.h32[l][:, :], L.h[l][:, :, 0],
                                                    ALU.subtract).then_inc(L.s_h[l], 1)
                        if A:
                            dve.wait_ge(A.s_sc, at + 1)
                            nc.vector.tensor_tensor(A.sm[:, :, :].rearrange("p b k -> p (b k)"), A.S[:, 0:2 * GB],
                                                    smask[:, :], ALU.mult).then_inc(A.s_sm, 1)
                            dve.wait_ge(A.s_st, at + 1)
                            nc.vector.tensor_reduce(A.nm[:, :], A.S[0:64, 128:192], AX.X, ALU.max,
                                                    negate=True).then_inc(A.s_nm, 1)
                        if L:
                            cell(0)
                        if A:
                            dve.wait_ge(A.s_ex, at + 1)
                            nc.vector.reciprocal(A.r[:, :], A.sum[:, :]).then_inc(A.s_r, 1)
                            dve.wait_ge(A.s_r, at + 1)
                            nc.vector.scalar_tensor_tensor(
                                A.pe[0:64, :].rearrange("p (h s) -> p h s", h=2),
                                A.p[:, :].unsqueeze(1).broadcast_to([64, 2, 64]), A.r[:, 0:1], pmask[:, :, :],
                                ALU.mult, ALU.mult).then_inc(A.s_pe, 1)
                        if L:
                            hidden(0)
                        if A:
                            dve.wait_ge(A.s_pt, at + 1)
                            nc.vector.tensor_copy(A.pm[:, :, 0], A.S[:, 256:320]).then_inc(A.s_pm, 1)
                            dve.wait_ge(A.s_pm, 2 * at + 1)
                            nc.vector.tensor_tensor(A.pm[:, :, 1], A.S[:, 256:320], A.pm[:, :, 0],
                                                    ALU.subtract).then_inc(A.s_pm, 1)
                        if L:
                            cell(1)
                        if A:
                            dve.wait_ge(A.s_mx, at + 1)
                            nc.vector.tensor_reduce(A.ar[:, :], A.M[:, 0:2 * GB].rearrange("p (b k) -> p b k", k=2),
                                                    AX.X, ALU.add).then_inc(A.s_ar, 1)
                        if L:
                            hidden(1)
                        if A:
                            dve.wait_ge(A.s_ta, at + 1)
                            nc.vector.tensor_scalar(A.a[:, :, 0], A.a32[:, :], S, None, ALU.mult).then_inc(A.s_ah, 1)
                            dve.wait_ge(A.s_ah, 2 * at + 1)
                            nc.vector.scalar_tensor_tensor(A.a[:, :, 1], A.a32[:, :], S, A.a[:, :, 0],
                                                           ALU.mult, ALU.subtract).then_inc(A.s_ah, 1)
                    run_halves(half, dve)
        recurrence_ctx.close()

        with ExitStack() as c5:
            def sb(name, shape, dt=F32):
                return c5.enter_context(nc.sbuf_tensor(name, shape, dt))

            def ps(name, shape, dt=F32):
                return c5.enter_context(nc.psum_tensor(name, shape, dt))
            X2 = sb("X2", [P, T, D])
            w1_sb = sb("w1_sb", [P, NE, FF])
            w2_sb = sb("w2_sb", [P, NE, FC, D])
            b1_sb = sb("b1_sb", [P, NE, FC])
            b2_sb = sb("b2_sb", [NE, D])
            rw_sb = sb("rw_sb", [P, NE])
            rbb = sb("rbb", [P, NE])
            wgt = sb("wgt", [P, NE])
            st6 = sb("st6c", [P, T, 6])
            mv = sb("mvc", [P, T, 2])
            sd = sb("sdc", [P, T])
            rs = sb("rsc", [P, T])
            xn = sb("xnc", [P, 8, D])
            lg = sb("lg", [P, T, NE])
            m1 = sb("m1", [P, T])
            eg = sb("eg", [P, T, NE])
            cd = sb("cd", [P, T, NE])
            gate = sb("gate", [P, T, NE])
            gc = sb("gc", [P, 4 * NE])
            gT = sb("gT", [NE, 2, 512])
            hid = sb("hid", [P, 4, 512])
            acc = sb("acc", [P, 2, 4, D])
            psT = ps("psT5", [P, 2, 512])
            psH = ps("psH", [P, 3, 512])
            psY = ps("psY", [P, 2, 512])
            psG = ps("psG", [P, 512])
            names = ("s_ld s_wf s_rb v5 p5a v5x v5st a5sd v5rs v5n p5t a5t p5l v5l v5g a5g p5g a5gt "
                     "p5h v5h p5y v5y s_out v5cst g5c").split()
            q = {n: sem(n) for n in names}
            NCH = T // 4
            with nc.Block() as block:
                @block.sync
                def _(sync):
                    sync.dma_start(X2[:, :, :], x1_dram).then_inc(q["s_ld"], 16)
                    sync.dma_start(w1_sb[:, :, :], w1.rearrange("e p f -> p e f")).then_inc(q["s_wf"], 16)
                    sync.dma_start(w2_sb[:, :, :, :], w2.rearrange("e (c p) n -> p e c n", p=P)).then_inc(q["s_wf"], 16)
                    sync.dma_start(b1_sb[:, :, :], b1T).then_inc(q["s_wf"], 16)
                    sync.dma_start(b2_sb[:, :], b2).then_inc(q["s_wf"], 16)
                    sync.dma_start(rw_sb[:, :], rw).then_inc(q["s_wf"], 16)
                    sync.dma_start(rbb[:, :], rb.rearrange("(a n) -> a n", a=1).broadcast_to([P, NE])).then_inc(q["s_wf"], 16)
                    with sync.Fori(0, NCH) as c:
                        sync.wait_ge(q["v5y"], (NE + 1) * c + NE + 1)
                        sync.dma_start(out.rearrange("b t d -> b (t d)")[:, bass.ds(c * 512, 512)],
                                       X2[:, :, :].rearrange("p t d -> p (t d)")[:, bass.ds(c * 512, 512)]).then_inc(q["s_out"], 16)
                    sync.wait_ge(q["s_out"], 16 * NCH)

                @block.gpsimd
                def _(pool):
                    pool.wait_ge(q["v5g"], 8)
                    def chunk(c):
                        wait(pool, q["p5g"], c)
                        pool.tensor_copy(gc[:, :], gate[:, :, :].rearrange("p t e -> p (t e)")
                                         [:, bass.ds(c * 4 * NE, 4 * NE)]).then_inc(q["g5c"], 1)

                    chunk(0)
                    with pool.Fori(1, NCH) as c:
                        chunk(c)

                def logits(pe, c):
                    pe.wait_ge(q["a5t"], c + 1)
                    for n in range(4):
                        t = 4 * c + n
                        mm = nc.tensor.matmul(psG[:, t * NE:(t + 1) * NE], XA[:, t, :], rw_sb[:, :],
                                              start=True, stop=True)
                    mm.then_inc(q["p5l"], 1)

                @block.tensor
                def _(pe):
                    for c in range(NCH):
                        if c >= 2:
                            pe.wait_ge(q["v5x"], c - 1)
                        for n in range(4):
                            mm = nc.tensor.transpose(psT[:, c % 2, n * P:(n + 1) * P], XA[:, 4 * c + n, :], ident[:, :])
                        mm.then_inc(q["p5a"], 1)
                    pe.wait_ge(q["s_wf"], 96)
                    for c in range(NCH):
                        pe.wait_ge(q["v5x"], NCH)
                        if c >= 2:
                            pe.wait_ge(q["a5t"], c - 1)
                        for n in range(4):
                            pe.wait_ge(q["v5n"], 4 * c + n + 1)
                            mm = nc.tensor.transpose(psT[:, c % 2, n * P:(n + 1) * P], xn[:, (4 * c + n) % 8, :], ident[:, :])
                        mm.then_inc(q["p5t"], 1)
                        if c >= 1:
                            logits(pe, c - 1)
                    logits(pe, NCH - 1)
                    pe.wait_ge(q["v5g"], 8)
                    def chunk(c):
                        wait(pe, q["a5gt"], c)
                        pe.wait_ge(q["g5c"], c + 1)
                        for n in range(4):
                            mm = nc.tensor.transpose(psG[0:NE, n * P:(n + 1) * P], gc[:, n * NE:(n + 1) * NE], ident[:, :])
                        mm.then_inc(q["p5g"], 1)
                        pe.wait_ge(q["a5gt"], c + 1)
                        wait(pe, q["v5y"], (NE + 1) * c)
                        for n in range(4):
                            mm = nc.tensor.matmul(psY[:, 0, n * P:(n + 1) * P], gT[:, 0, n * P:(n + 1) * P], b2_sb[:, :],
                                                  start=True, stop=True)
                        mm.then_inc(q["p5y"], 1)
                        for e in range(NE):
                            for f in range(FC):
                                k = e * FC + f
                                wait(pe, q["v5h"], NE * FC * c + max(0, k - 2))
                                nc.tensor.matmul(psH[:, (k % 3), :], w1_sb[:, e, f * P:(f + 1) * P],
                                                 X[:, bass.ds(c * 512, 512)], start=True, stop=True).then_inc(q["p5h"], 1)
                            pe.wait_ge(q["v5h"], NE * FC * c + e * FC + FC)
                            wait(pe, q["v5y"], (NE + 1) * c + e)
                            for n in range(4):
                                for f in range(FC):
                                    mm = nc.tensor.matmul(psY[:, (e + 1) % 2, n * P:(n + 1) * P],
                                                          hid[:, f, n * P:(n + 1) * P], w2_sb[:, e, f, :],
                                                          start=(f == 0), stop=(f == FC - 1))
                            mm.then_inc(q["p5y"], 1)

                    chunk(0)
                    with pe.Fori(1, NCH) as c:
                        chunk(c)

                @block.scalar
                def _(act):
                    act.wait_ge(q["v5st"], 2 * T + 1)
                    nc.scalar.activation(sd[:, :], sd[:, :], ACT.Sqrt).then_inc(q["a5sd"], 1)
                    for c in range(NCH):
                        act.wait_ge(q["p5t"], c + 1)
                        nc.scalar.activation(X[:, c * 512:(c + 1) * 512], psT[:, c % 2, :], ACT.Copy).then_inc(q["a5t"], 1)
                    act.wait_ge(q["v5g"], 2)
                    nc.scalar.activation(eg[:, :, :], eg[:, :, :], ACT.Exp).then_inc(q["a5g"], 1)
                    def chunk(c):
                        act.wait_ge(q["p5g"], c + 1)
                        nc.scalar.activation(gT[:, 0, :], psG[0:NE, :], ACT.Copy).then_inc(q["a5gt"], 1)
                        for k in range(NE * FC):
                            act.wait_ge(q["p5h"], NE * FC * c + k + 1)
                            if k % FC == 0:
                                wait(act, q["p5y"], (NE + 1) * c + k // FC + (1 if k else 0))
                            nc.scalar.activation(hid[:, k % FC, :], psH[:, k % 3, :], ACT.Relu,
                                                 bias=b1_sb[:, k // FC, k % FC:k % FC + 1]).then_inc(q["v5h"], 1)

                    chunk(0)
                    with act.Fori(1, NCH) as c:
                        chunk(c)

                @block.vector
                def _(dve):
                    for e in range(NE):
                        dve.memset(wgt[:, e:e + 1], float(NE - e)).then_inc(q["v5cst"], 1)
                    dve.wait_ge(q["s_ld"], 16)
                    for c in range(NCH):
                        dve.wait_ge(q["p5a"], c + 1)
                        nc.vector.tensor_tensor(X2[:, 4 * c:4 * c + 4, :].rearrange("p t d -> p (t d)"), psT[:, c % 2, :],
                                                X2[:, 4 * c:4 * c + 4, :].rearrange("p t d -> p (t d)"), ALU.add).then_inc(q["v5x"], 1)
                    dve.wait_ge(q["v5x"], NCH)
                    for n in range(T):
                        nc.vector.bn_stats(st6[:, n, :], X2[:, n, :]).then_inc(q["v5st"], 1)
                    for n in range(T):
                        dve.wait_ge(q["v5st"], n + 1)
                        nc.vector.bn_aggr(mv[:, n, :], st6[:, n, :]).then_inc(q["v5st"], 1)
                    dve.wait_ge(q["v5st"], 2 * T)
                    nc.vector.tensor_scalar(sd[:, :], mv[:, :, 1], EPS, None, ALU.add).then_inc(q["v5st"], 1)
                    dve.wait_ge(q["a5sd"], 1)
                    nc.vector.reciprocal(rs[:, :], sd[:, :]).then_inc(q["v5rs"], 1)
                    dve.wait_ge(q["v5rs"], 1)
                    for c in range(NCH):
                        if c >= 2:
                            dve.wait_ge(q["p5t"], c - 1)
                        for n in range(4 * c, 4 * c + 4):
                            nc.vector.tensor_scalar(xn[:, n % 8, :], X2[:, n, :], mv[:, n, 0:1], rs[:, n:n + 1],
                                                    ALU.subtract, ALU.mult).then_inc(q["v5n"], 1)
                    dve.wait_ge(q["p5l"], NCH)
                    dve.wait_ge(q["s_wf"], 96)
                    dve.wait_ge(q["v5cst"], NE)
                    full = [P, T, NE]
                    k = 0

                    def step(ins, wait=True):
                        nonlocal k
                        k += 1
                        ins.then_inc(q["v5g"], 1)
                        dve.wait_ge(q["v5g"], k)
                    ins = nc.vector.tensor_tensor(lg[:, :, :], psG[:, :].rearrange("p (t e) -> p t e", e=NE),
                                                  rbb[:, :].unsqueeze(1).broadcast_to(full), ALU.add)
                    ins.then_inc(q["v5l"], 1)
                    dve.wait_ge(q["v5l"], 1)
                    step(nc.vector.tensor_reduce(m1[:, :], lg[:, :, :], AX.X, ALU.max))
                    step(nc.vector.tensor_tensor(eg[:, :, :], lg[:, :, :], m1[:, :].unsqueeze(2).broadcast_to(full), ALU.subtract))
                    step(nc.vector.tensor_tensor(cd[:, :, :], lg[:, :, :], m1[:, :].unsqueeze(2).broadcast_to(full), ALU.is_equal))
                    step(nc.vector.tensor_tensor(cd[:, :, :], cd[:, :, :], wgt[:, :].unsqueeze(1).broadcast_to(full), ALU.mult))
                    step(nc.vector.tensor_reduce(m1[:, :], cd[:, :, :], AX.X, ALU.max))
                    step(nc.vector.tensor_tensor(cd[:, :, :], cd[:, :, :], m1[:, :].unsqueeze(2).broadcast_to(full), ALU.is_equal))
                    dve.wait_ge(q["a5g"], 1)
                    step(nc.vector.tensor_reduce(m1[:, :], eg[:, :, :], AX.X, ALU.add))
                    nc.vector.reciprocal(m1[:, :], m1[:, :]).then_inc(q["v5l"], 1)
                    dve.wait_ge(q["v5l"], 2)
                    step(nc.vector.tensor_tensor(gate[:, :, :], cd[:, :, :], m1[:, :].unsqueeze(2).broadcast_to(full), ALU.mult))
                    X2f = X2[:, :, :].rearrange("p t d -> p (t d)")
                    def chunk(c):
                        dve.wait_ge(q["p5y"], (NE + 1) * c + 1)
                        xc = X2f[:, bass.ds(c * 512, 512)]
                        nc.vector.tensor_tensor(xc, psY[:, 0, :], xc, ALU.add).then_inc(q["v5y"], 1)
                        for e in range(NE):
                            dve.wait_ge(q["p5y"], (NE + 1) * c + e + 2)
                            dve.wait_ge(q["v5y"], (NE + 1) * c + e + 1)
                            for n in range(4):
                                xt = X2f[:, bass.ds(c * 512 + n * P, P)]
                                gcol = gate[:, :, :].rearrange("p t e -> p (t e)")[:, bass.ds(c * 4 * NE + n * NE + e, 1)]
                                ins = nc.vector.scalar_tensor_tensor(xt, psY[:, (e + 1) % 2, n * P:(n + 1) * P], gcol, xt,
                                                                     ALU.mult, ALU.add)
                            ins.then_inc(q["v5y"], 1)

                    chunk(0)
                    with dve.Fori(1, NCH) as c:
                        chunk(c)


_ORDER = ["x", "ctxT", "ctx", "wqT", "wkT", "wvT", "wi0T", "wh0T", "bi0", "bh0", "wi1T", "wh1T", "bi1", "bh1",
          "xwq", "woT", "bo", "rw", "rb", "w1", "b1T", "w2", "b2"]


def kernel(**inputs):
    import numpy as np
    import concourse.bacc as bacc
    from concourse.bass_utils import run_bass_kernel_spmd

    g = {k: np.asarray(v) for k, v in inputs.items()}
    c = np.ascontiguousarray
    ctx = g["ctx_1024"]
    arrays = {
        "x": g["x"], "ctxT": c(ctx.transpose(2, 0, 1).reshape(D, B * T)),
        "wqT": c(g["L0_attn_Wq"].T), "wkT": c(g["L0_attn_Wk"].T), "wvT": c(g["L0_attn_Wv"].T),
        "wi0T": c(g["L0_xattn_Wi0"].T), "wh0T": c(g["L0_xattn_Wh0"].T),
        "bi0": g["L0_xattn_bi0"], "bh0": g["L0_xattn_bh0"],
        "wi1T": c(g["L0_xattn_Wi1"].T), "wh1T": c(g["L0_xattn_Wh1"].T),
        "bi1": g["L0_xattn_bi1"], "bh1": g["L0_xattn_bh1"],
        "xwq": g["L0_xattn_Wq"], "woT": c(g["L0_xattn_Wo"].T), "bo": g["L0_xattn_bo"],
        "rw": g["L0_ffn_router_W"], "rb": g["L0_ffn_router_b"],
        "w1": g["L0_ffn_W1"], "b1T": c(g["L0_ffn_b1"].reshape(NE, FC, P).transpose(2, 0, 1)),
        "w2": g["L0_ffn_W2"], "b2": g["L0_ffn_b2"],
    }
    nc = bacc.Bacc("TRN2", target_bir_lowering=False, num_devices=1)
    aps = {}
    feed = {}
    for name, a in arrays.items():
        a = c(a)
        feed[f"in_{name}"] = a
        aps[name] = nc.dram_tensor(f"in_{name}", a.shape, mybir.dt.from_np(a.dtype), kind="ExternalInput").ap()
    o = nc.dram_tensor("out_0", [B, T, D], F32, kind="ExternalOutput").ap()
    decoder_kernel(nc, ctx=None, out=o, **aps)
    r = run_bass_kernel_spmd(nc, [feed], core_ids=[0])
    return r.results[0]["out_0"]
```

```python
from contextlib import ExitStack

import concourse.bass as bass
from concourse import mybir

F32 = mybir.dt.float32
F16 = mybir.dt.float16
BF16 = mybir.dt.bfloat16
I32 = mybir.dt.int32
U32 = mybir.dt.uint32
ALU = mybir.AluOpType
ACT = mybir.ActivationFunctionType
AX = mybir.AxisListType

P = 128
B, T, D = 128, 64, 128
NPAIR = B // 2
NH, DK = 16, 8
HG = 4
EPS = 1e-5
GB = B // 2
GP = GB // 2
NE, FF = 8, 512
FC = FF // P
WIDE = 512 // GP
PAD = (WIDE - 4) // 2
NSPLIT = 24
S = 4096.0
NT = B * T // P + NE
WX0, WA0, WH0, WI1, WH1 = 0, 4, 8, 12, 16


def wait(eng, semaphore, value):
    if not (isinstance(value, int) and value <= 0):
        eng.wait_ge(semaphore, value)


def decoder_kernel(nc, x, ctxT, wqT, wkT, wvT, wi0T, wh0T, bi0, bh0, wi1T, wh1T, bi1, bh1,
                   xwq, woT, bo, rw, rb, w1, b1, w2, b2, out):
    x1_dram = nc.dram_tensor("x1_scratch", [B, T, D], F32, kind="Internal").ap()
    xs_dram = nc.dram_tensor("sorted_x", [NT * P, D], F32, kind="Internal").ap()
    ys_dram = nc.dram_tensor("sorted_y", [NT * P, D], F32, kind="Internal").ap()

    with ExitStack() as persist:
        block_sems = []

        def sem(name):
            block_sems.append(nc.alloc_semaphore(name=name))
            return block_sems[-1]

        def clear_semaphores():
            nc.clear_and_free_semaphores(block_sems)
            nc.all_engine_barrier()
            block_sems.clear()

        def sbp(name, shape, dt=F32):
            return persist.enter_context(nc.sbuf_tensor(name, shape, dt))

        ident = sbp("ident", [P, P])
        ones = sbp("ones", [P, P])
        pm = sbp("pm", [P, 2])
        X = sbp("X", [P, NPAIR * D])
        Xp = X[:, :].rearrange("p (n d) -> p n d", d=D)
        XA = X[:, :].rearrange("p (t b) -> p t b", b=B)

        s_const = sem("s_const")

        recurrence_ctx = ExitStack()

        def sbr(name, shape, dt=F32):
            return recurrence_ctx.enter_context(nc.sbuf_tensor(name, shape, dt))

        KH = sbr("KH", [P, 2, B * T], F16)
        VH = sbr("VH", [P, 2, NPAIR, D], F16)
        XT = sbr("XT", [P, 2, T, B], F16)
        WL = sbr("WL", [P, 20, 2, P], F16)
        WO2 = sbr("WO2", [P, 2, P], F16)
        BL = sbr("BL", [P, 2, 4 * P], BF16)
        onesb = sbr("onesb", [P, GB], BF16)
        II = sbr("II", [P, 64])
        sc = sbr("sc", [P, 16])
        smask = sbr("smask", [P, 2 * GB])
        pmask = sbr("pmask", [64, 2, 64])
        bo_sb = sbr("bo_sb", [P, 1])
        pw = sbr("pw", [P, 8])
        wq_sb = sbr("wq_sb", [P, P])
        wk_sb = sbr("wk_sb", [P, DK])
        wv_sb = sbr("wv_sb", [P, DK])
        S0, S1, SK, SV, I0, I1, IK, IV = range(8)

        with ExitStack() as c1:
            def sb(name, shape, dt=F32):
                return c1.enter_context(nc.sbuf_tensor(name, shape, dt))

            def ps(name, shape, dt=F32):
                return c1.enter_context(nc.psum_tensor(name, shape, dt))
            CT = XT[:, :, :, :].rearrange("p a t b -> p (a t b)").bitcast(F32)
            wl32 = sb("wl32", [P, 20 * P])
            xwq_sb = sb("xwq_sb", [P, P])
            wo_sb = sb("wo_sb", [P, 2, P])
            bb = sb("bb", [P, 4, 4 * P])
            rowm = sb("rowm", [P, 3])
            bw = sb("bw", [P, 4 * P])
            bhi = sb("bhi", [P, 4 * P], BF16)
            mx = sb("mx", [P, 8])
            mxr = sb("mxr", [8, 1])
            dg = sb("dg", [8, 8])
            gm = sb("gm", [P, 8])
            tmp = sb("tmp", [P, 8])
            par = sb("par", [64, 2])
            ktmp = sb("ktmp", [P, 2, 512])
            psA = ps("psA", [P, 2, 512])
            psV = ps("psV", [P, 2, 512])
            psS = ps("psS", [P, 512])

            s_ctx = sem("s_ctx")
            s_x = sem("s_x")
            s_w = sem("s_w")
            s_b = sem("s_b")
            s_wo = sem("s_wo")
            s_bz = sem("s_bz")
            v_mx = sem("v_mx")
            p_sc = sem("p_sc")
            v_sc = sem("v_sc")
            v_scale = sem("v_scale")
            p_k = sem("p_k")
            p_v = sem("p_v")
            a_k = sem("a_k")
            a_v = sem("a_v")
            v_k = sem("v_k")
            v_v = sem("v_v")
            a_w = sem("a_w")
            v_w = sem("v_w")
            v_b = sem("v_b")
            v_pm = sem("v_pm")

            with nc.Block() as block:
                @block.sync
                def _(sync):
                    sync.dma_start(CT, ctxT).then_inc(s_ctx, 16)
                    sync.dma_start(xwq_sb[:, :], xwq).then_inc(s_wo, 16)
                    sync.dma_start(wo_sb[:, :, :], woT.rearrange("(a p) n -> p a n", a=2)).then_inc(s_wo, 16)
                    sync.dma_start(wq_sb[:, :], wqT).then_inc(s_wo, 16)
                    sync.dma_start(wk_sb[:, :], wkT).then_inc(s_wo, 16)
                    sync.dma_start(wv_sb[:, :], wvT).then_inc(s_wo, 16)
                    sync.dma_start(bo_sb[:, :], bo.rearrange("(p a) -> p a", a=1)).then_inc(s_wo, 16)
                    sync.dma_start(Xp, x.rearrange("(n two) t d -> (two t) n d", two=2)).then_inc(s_x, 16)
                    sync.wait_ge(s_x, 16)

                @block.scalar
                def _(act):
                    w4 = wl32[:, :].rearrange("p (k n) -> p k n", n=4 * P)
                    act.dma_start(w4[:, 0:2, :], wi0T.rearrange("(a p) n -> p a n", a=2)).then_inc(s_w, 16)
                    act.dma_start(w4[:, 2, :], wh0T).then_inc(s_w, 16)
                    act.dma_start(w4[:, 3, :], wi1T).then_inc(s_w, 16)
                    act.dma_start(w4[:, 4, :], wh1T).then_inc(s_w, 16)
                    act.wait_ge(s_bz, 1)
                    for k, src in enumerate((bi0, bh0, bi1, bh1)):
                        for r in (0, 32, 64):
                            act.dma_start(bb[r:r + 1, k, :], src.rearrange("(a n) -> a n", a=1)).then_inc(s_b, 16)
                    act.wait_ge(v_scale, 1)
                    for blk in range(20):
                        col = (S0 if blk < 12 else S1) + (8 if blk % 4 == 2 else 0)
                        nc.scalar.activation(WL[:, blk, 0, :], wl32[:, blk * P:(blk + 1) * P], ACT.Copy,
                                             scale=sc[:, col:col + 1]).then_inc(a_w, 1)
                    nc.scalar.activation(WO2[:, 0, :], wo_sb[:, 1, :], ACT.Copy,
                                         scale=sc[:, SV:SV + 1]).then_inc(a_w, 1)
                    for c in range(16):
                        act.wait_ge(p_k, c + 1)
                        nc.scalar.activation(KH[:, 0, c * 512:(c + 1) * 512], psA[:, c % 2, :], ACT.Copy,
                                             scale=sc[:, SK:SK + 1]).then_inc(a_k, 1)
                        act.wait_ge(p_v, c + 1)
                        nc.scalar.activation(VH[:, 0, 4 * c:4 * c + 4, :],
                                             psV[:, c % 2, :].rearrange("p (n d) -> p n d", d=D), ACT.Copy,
                                             scale=sc[:, SV:SV + 1]).then_inc(a_v, 1)

                @block.gpsimd
                def _(pool):
                    pool.memset(bb[:, :, :], 0.0).then_inc(s_bz, 1)
                    pool.memset(ident[:, :], 0.0).then_inc(s_const, 1)
                    pool.memset(ones[:, :], 1.0).then_inc(s_const, 1)
                    pool.memset(II[:, :], 0.0).then_inc(s_const, 1)
                    pool.memset(rowm[:, :], 0.0).then_inc(s_const, 1)
                    pool.memset(onesb[:, :], 1.0).then_inc(s_const, 1)
                    pool.wait_ge(s_const, 5)
                    pool.affine_select(out=ident[:, :], in_=ident[:, :], compare_op=ALU.not_equal, fill=1.0,
                                       base=0, pattern=[[-1, P]], channel_multiplier=1).then_inc(s_const, 1)
                    pool.affine_select(out=II[:, :], in_=II[:, :], compare_op=ALU.not_equal, fill=1.0,
                                       base=0, pattern=[[-1, 64]], channel_multiplier=1).then_inc(s_const, 1)
                    pool.affine_select(out=rowm[:, :], in_=rowm[:, :], compare_op=ALU.not_equal, fill=1.0,
                                       base=0, pattern=[[-32, 3]], channel_multiplier=1).then_inc(s_const, 1)
                    pool.wait_ge(s_const, 8)
                    pool.affine_select(out=II[:, :], in_=II[:, :], compare_op=ALU.not_equal, fill=1.0,
                                       base=-64, pattern=[[-1, 64]], channel_multiplier=1).then_inc(s_const, 1)

                @block.tensor
                def _(pe):
                    pe.wait_ge(s_const, 9)
                    pe.wait_ge(v_mx, 8)
                    nc.tensor.transpose(psS[0:8, 0:P], mx[:, :], ident[:, :]).then_inc(p_sc, 1)
                    pe.wait_ge(v_sc, 2)
                    nc.tensor.matmul(psS[:, 128:136], ones[0:8, :], dg[:, :], start=True, stop=True).then_inc(p_sc, 1)
                    pe.wait_ge(s_wo, 96)
                    for c in range(16):
                        if c >= 2:
                            pe.wait_ge(v_k, c - 1)
                        nc.tensor.matmul(psA[:, c % 2, :], xwq_sb[:, :], CT[:, c * 512:(c + 1) * 512],
                                         start=True, stop=True).then_inc(p_k, 1)
                        if c >= 2:
                            pe.wait_ge(v_v, c - 1)
                        for n in range(4):
                            mm = nc.tensor.matmul(psV[:, c % 2, n * P:(n + 1) * P],
                                                  CT[:, (4 * c + n) * P:(4 * c + n + 1) * P], wo_sb[:, 0, :],
                                                  start=True, stop=True)
                        mm.then_inc(p_v, 1)

                @block.vector
                def _(dve):
                    dve.wait_ge(s_w, 64)
                    nc.vector.tensor_reduce(mx[:, 0:1], wl32[:, 0:12 * P], AX.X, ALU.max,
                                            apply_absolute_value=True).then_inc(v_mx, 1)
                    nc.vector.tensor_reduce(mx[:, 1:2], wl32[:, 12 * P:], AX.X, ALU.max,
                                            apply_absolute_value=True).then_inc(v_mx, 1)
                    dve.wait_ge(s_wo, 96)
                    nc.vector.tensor_reduce(mx[:, 2:3], xwq_sb[:, :], AX.X, ALU.max,
                                            apply_absolute_value=True).then_inc(v_mx, 1)
                    nc.vector.tensor_reduce(mx[:, 3:4], wo_sb[:, :, :], AX.XY, ALU.max,
                                            apply_absolute_value=True).then_inc(v_mx, 1)
                    for k, w in enumerate((wq_sb, wk_sb, wv_sb)):
                        nc.vector.tensor_reduce(mx[:, 5 + k:6 + k], w[:, :], AX.X, ALU.max,
                                                apply_absolute_value=True).then_inc(v_mx, 1)
                    dve.wait_ge(s_ctx, 16)
                    nc.vector.tensor_reduce(mx[:, 4:5], CT, AX.X, ALU.max,
                                            apply_absolute_value=True).then_inc(v_mx, 1)
                    dve.wait_ge(p_sc, 1)
                    nc.vector.tensor_reduce(mxr[:, :], psS[0:8, 0:P], AX.X, ALU.max).then_inc(v_sc, 1)
                    dve.wait_ge(v_sc, 1)
                    nc.vector.tensor_scalar(dg[:, :], ident[0:8, 0:8], mxr[:, 0:1], None, ALU.mult).then_inc(v_sc, 1)
                    dve.wait_ge(p_sc, 2)
                    n = 2

                    def step(ins):
                        nonlocal n
                        n += 1
                        ins.then_inc(v_sc, 1)
                        dve.wait_ge(v_sc, n)
                    step(nc.vector.tensor_scalar(gm[:, :], psS[:, 128:136], 1e-12, 1e12, ALU.max, ALU.min))
                    step(nc.vector.tensor_scalar(pw[:, :].bitcast(I32), gm[:, :].bitcast(I32), 0x7F800000, None,
                                                 ALU.bitwise_and))
                    step(nc.vector.tensor_scalar(tmp[:, 0:2], pw[:, 0:2], 2.0 ** -13, None, ALU.mult))
                    step(nc.vector.scalar_tensor_tensor(tmp[:, 2:3], pw[:, 4:5], 2.0 ** -6, pw[:, 2:3],
                                                        ALU.mult, ALU.mult))
                    step(nc.vector.tensor_scalar(tmp[:, 4:5], pw[:, 4:5], 2.0 ** -8, 2.0 ** -6, ALU.max, ALU.mult))
                    step(nc.vector.tensor_tensor(tmp[:, 3:4], tmp[:, 4:5], pw[:, 3:4], ALU.mult))
                    step(nc.vector.reciprocal(sc[:, 0:4], tmp[:, 0:4]))
                    step(nc.vector.tensor_scalar(sc[:, 4:6], tmp[:, 0:2], 0.5 / S, None, ALU.mult))
                    step(nc.vector.tensor_scalar(sc[:, 6:8], tmp[:, 2:4], 1.0 / S, None, ALU.mult))
                    nc.vector.tensor_scalar(sc[:, 8:10], sc[:, 0:2], 2.0, None, ALU.mult).then_inc(v_scale, 1)
                    dve.wait_ge(s_const, 9)
                    nc.vector.tensor_reduce(pm[:, :], ident[:, :].rearrange("p (h k) -> p h k", h=2), AX.X,
                                            ALU.add).then_inc(v_pm, 1)
                    dve.wait_ge(v_pm, 1)
                    nc.vector.tensor_scalar(
                        smask[:, :].rearrange("p (n h k) -> p n h k", h=2, k=2),
                        pm[:, :].unsqueeze(1).unsqueeze(3).broadcast_to([P, GP, 2, 2]),
                        sc[:, IK:IK + 1], None, ALU.mult).then_inc(v_b, 1)
                    nc.vector.tensor_reduce(par[:, 0:1], ident[0:64, 0:64:2], AX.X, ALU.add).then_inc(v_b, 1)
                    nc.vector.tensor_reduce(par[:, 1:2], ident[0:64, 1:64:2], AX.X, ALU.add).then_inc(v_b, 1)
                    dve.wait_ge(v_b, 3)
                    nc.vector.tensor_scalar(pmask[:, :, :], par[:, :].unsqueeze(2).broadcast_to([64, 2, 64]),
                                            S, None, ALU.mult).then_inc(v_b, 1)
                    dve.wait_ge(s_b, 16 * 12)
                    dve.wait_ge(v_scale, 1)
                    n2 = 4

                    def step2(ins):
                        nonlocal n2
                        n2 += 1
                        ins.then_inc(v_b, 1)
                        dve.wait_ge(v_b, n2)
                    for layer in range(2):
                        step2(nc.vector.tensor_tensor(bw[:, :], bb[:, 2 * layer, :], bb[:, 2 * layer + 1, :], ALU.add))
                        step2(nc.vector.tensor_scalar(bw[:, :], bw[:, :], sc[:, layer:layer + 1], S, ALU.mult, ALU.mult))
                        step2(nc.vector.tensor_scalar(bw[:, 2 * P:3 * P], bw[:, 2 * P:3 * P], 2.0, None, ALU.mult))
                        for k in range(3):
                            step2(nc.vector.tensor_copy(bhi[:, :], bw[:, :]))
                            if k == 0:
                                step2(nc.vector.tensor_scalar(BL[:, layer, :], bhi[:, :], rowm[:, 0:1], None, ALU.mult))
                            else:
                                step2(nc.vector.scalar_tensor_tensor(BL[:, layer, :], bhi[:, :], rowm[:, k:k + 1],
                                                                     BL[:, layer, :], ALU.mult, ALU.add))
                            step2(nc.vector.tensor_tensor(bw[:, :], bw[:, :], bhi[:, :], ALU.subtract))
                    for blk in range(20):
                        col = (S0 if blk < 12 else S1) + (8 if blk % 4 == 2 else 0)
                        dve.wait_ge(a_w, blk + 1)
                        nc.vector.scalar_tensor_tensor(WL[:, blk, 1, :], wl32[:, blk * P:(blk + 1) * P],
                                                       sc[:, col:col + 1], WL[:, blk, 0, :],
                                                       ALU.mult, ALU.subtract).then_inc(v_w, 1)
                    dve.wait_ge(a_w, 21)
                    nc.vector.scalar_tensor_tensor(WO2[:, 1, :], wo_sb[:, 1, :], sc[:, SV:SV + 1], WO2[:, 0, :],
                                                   ALU.mult, ALU.subtract).then_inc(v_w, 1)
                    for c in range(16):
                        dve.wait_ge(a_k, c + 1)
                        nc.vector.scalar_tensor_tensor(KH[:, 1, c * 512:(c + 1) * 512], psA[:, c % 2, :],
                                                       sc[:, SK:SK + 1], KH[:, 0, c * 512:(c + 1) * 512],
                                                       ALU.mult, ALU.subtract).then_inc(v_k, 1)
                        dve.wait_ge(a_v, c + 1)
                        nc.vector.scalar_tensor_tensor(
                            VH[:, 1, 4 * c:4 * c + 4, :].rearrange("p n d -> p (n d)"), psV[:, c % 2, :],
                            sc[:, SV:SV + 1], VH[:, 0, 4 * c:4 * c + 4, :].rearrange("p n d -> p (n d)"),
                            ALU.mult, ALU.subtract).then_inc(v_v, 1)

        clear_semaphores()

        with ExitStack() as c2:
            def sb(name, shape, dt=F32):
                return c2.enter_context(nc.sbuf_tensor(name, shape, dt))

            def ps(name, shape, dt=F32):
                return c2.enter_context(nc.psum_tensor(name, shape, dt))
            QA = 4
            DOWN = 2.0 ** -18
            wrep = sb("wrep", [P, QA + 1, HG, 4, DK])
            wst = sb("wst", [P, 2, QA + 1, P], F16)
            wvs = sb("wvs", [P, 2, DK], F16)
            m4 = sb("m4", [P, 4])
            lo = sb("lo", [P, 2])
            s2 = sb("s2", [P, 8])
            pmv = sb("pmv", [P, 2])
            ob = sb("ob", [P, 2, 2, DK])
            st6 = sb("st6", [P, NPAIR, 6])
            mv = sb("mv", [P, NPAIR, 2])
            sd = sb("sd", [P, NPAIR])
            rs = sb("rs", [P, NPAIR])
            xn = sb("xn", [P, 2, D])
            xh = sb("xh", [P, 2, 2, P], F16)
            hq = sb("hq", [P, 512], F16)
            hk = sb("hk", [P, P], F16)
            QS = sb("QS", [P, 2, 512], F16)
            KS = sb("KS", [P, 2, P], F16)
            VB = sb("VB", [P, 2, 2, 2, DK])
            pmx = sb("pmx", [P, 2, NH])
            pr = sb("pr", [P, 2, NH, 64])
            prT = sb("prT", [P, 8, P])
            pv = sb("pv", [P, 512])
            rden = sb("rden", [P, NH])
            yv = sb("yv", [P, NH, DK])
            psSc = ps("psSc", [P, 4, 512])
            psQ = ps("psQ", [P, 512])
            psK = ps("psK", [P, 512])
            psT = ps("psT", [P, 2, 512])

            v_c = sem("v_c")
            v_s2 = sem("v_s2")
            a_w2 = sem("a_w2")
            v_w2 = sem("v_w2")
            v_st = sem("v_st")
            a_sd = sem("a_sd")
            v_rs = sem("v_rs")
            v_xn = sem("v_xn")
            p_xt = sem("p_xt")
            a_xh = sem("a_xh")
            v_xl = sem("v_xl")
            p_q = sem("p_q")
            a_hq = sem("a_hq")
            v_qs = sem("v_qs")
            v_vb = sem("v_vb")
            p_s = sem("p_s")
            v_m = sem("v_m")
            v_sub = sem("v_sub")
            a_ex = sem("a_ex")
            p_pt = sem("p_pt")
            a_pt = sem("a_pt")
            p_o = sem("p_o")
            a_o = sem("a_o")
            p_ot = sem("p_ot")
            v_rd = sem("v_rd")
            v_y = sem("v_y")
            v_x1 = sem("v_x1")

            def has(n):
                return not isinstance(n, int) or 0 <= n < NPAIR

            def run_steps(eng, step):
                for i in range(-3, 2):
                    step(i, i % 2)
                with eng.Fori(2, NPAIR - 5, 2) as i:
                    step(i, 0)
                    step(i + 1, 1)
                for i in range(NPAIR - 4, NPAIR + 1):
                    step(i, i % 2)

            with nc.Block() as block:
                @block.tensor
                def _(pe):
                    pe.wait_ge(v_c, 5)
                    pe.wait_ge(v_w2, QA + 2)

                    def split3(out, w, x, first=0):
                        for k, (a, b) in enumerate(((0, 0), (1, 0), (0, 1))):
                            mm = nc.tensor.matmul(out, w(a), x(b), start=(k == 0), stop=(k == 2))
                        return mm

                    def scores(n, u, a0):
                        for a in (a0, a0 + 1):
                            for b in range(2):
                                for g in range(4):
                                    mm = nc.tensor.matmul(
                                        psSc[64 * b:64 * b + 64, g, 64 * a:64 * a + 64],
                                        QS[32 * g:32 * g + 32, u, a * P + 64 * b:a * P + 64 * b + 64],
                                        KS[32 * g:32 * g + 32, u, 64 * b:64 * b + 64],
                                        start=True, stop=True)
                        return mm

                    def step(i, u):
                        if has(i + 2):
                            n = i + 2
                            pe.wait_ge(v_xn, n + 1)
                            wait(pe, v_qs, n)
                            wait(pe, v_vb, n - 1)
                            nc.tensor.transpose(psK[:, 0:P], xn[:, u, :], ident[:, :]).then_inc(p_xt, 1)
                        if has(i + 1):
                            n = i + 1
                            pe.wait_ge(v_qs, n + 1)
                            wait(pe, v_sub, n)
                            scores(n, 1 - u, 0)
                        if has(i - 1):
                            n = i - 1
                            pe.wait_ge(a_o, n + 1)
                            for k in range(4):
                                mm = nc.tensor.transpose(psT[:, 1, k * P:(k + 1) * P], pv[:, k * P:(k + 1) * P], ident[:, :])
                            mm.then_inc(p_ot, 1)
                        if has(i + 1):
                            scores(n, 1 - u, 2).then_inc(p_s, 1)
                        if has(i):
                            pe.wait_ge(a_ex, i + 1)
                            for hp in range(8):
                                if hp == 4:
                                    wait(pe, v_y, 2 * i)
                                mm = nc.tensor.transpose(psT[:, hp // 4, (hp % 4) * P:(hp % 4 + 1) * P],
                                                         pr[:, u, 2 * hp:2 * hp + 2, :].rearrange("p h k -> p (h k)"),
                                                         ident[:, :])
                                if hp % 4 == 3:
                                    mm.then_inc(p_pt, 1)
                        if has(i + 2):
                            n = i + 2
                            pe.wait_ge(a_xh, n + 1)
                            pe.wait_ge(v_xl, n + 1)
                            for a in range(QA):
                                split3(psQ[:, a * P:(a + 1) * P], lambda k: wst[:, k, a, :], lambda k: xh[:, u, k, :])
                            mm = split3(psK[:, P:2 * P], lambda k: wst[:, k, QA, :], lambda k: xh[:, u, k, :])
                        if has(i + 1):
                            for b in range(2):
                                for h in range(2):
                                    mm = split3(psK[64 * h:64 * h + 64, 2 * P + DK * b:2 * P + DK * (b + 1)],
                                                lambda k: xh[:, 1 - u, k, 64 * b:64 * b + 64], lambda k: wvs[:, k, :])
                        if has(i + 2) or has(i + 1):
                            mm.then_inc(p_q, 1)
                        if has(i):
                            pe.wait_ge(v_vb, i + 1)
                            for half in range(2):
                                pe.wait_ge(a_pt, 2 * i + half + 1)
                                for w, c0 in ((VB[:, u, :, :, :], 0), (ob[:, :, :, :], 256)):
                                    for j in range(4):
                                        mm = nc.tensor.matmul(psT[32 * j:32 * j + 32, 0, c0 + half * P:c0 + (half + 1) * P],
                                                              w.rearrange("p a b d -> p (a b d)"), prT[:, 4 * half + j, :],
                                                              start=True, stop=True)
                            mm.then_inc(p_o, 1)
                    run_steps(pe, step)

                @block.scalar
                def _(act):
                    act.wait_ge(v_st, 2 * NPAIR + 1)
                    nc.scalar.activation(sd[:, :], sd[:, :], ACT.Sqrt).then_inc(a_sd, 1)
                    act.wait_ge(v_s2, 6)
                    act.wait_ge(v_c, 5)
                    for a in range(QA + 1):
                        nc.scalar.activation(wst[:, 0, a, :], wrep[:, a, :, :, :].rearrange("p g r d -> p (g r d)"), ACT.Copy,
                                             scale=s2[:, a // QA:a // QA + 1]).then_inc(a_w2, 1)
                    nc.scalar.activation(wvs[:, 0, :], wv_sb[:, :], ACT.Copy, scale=s2[:, 2:3]).then_inc(a_w2, 1)

                    def step(i, u):
                        if has(i - 1):
                            n = i - 1
                            act.wait_ge(p_o, n + 1)
                            wait(act, p_ot, n)
                            nc.scalar.activation(pv[:, :], psT[:, 0, :], ACT.Copy).then_inc(a_o, 1)
                        if has(i + 2):
                            n = i + 2
                            act.wait_ge(p_xt, n + 1)
                            nc.scalar.activation(xh[:, u, 0, :], psK[:, 0:P], ACT.Copy, scale=S).then_inc(a_xh, 1)
                        if has(i):
                            wait(act, p_o, i)
                            for k in range(2):
                                act.wait_ge(p_pt, 2 * i + k + 1)
                                nc.scalar.activation(prT[:, 4 * k:4 * k + 4, :].rearrange("p n t -> p (n t)"),
                                                     psT[:, k, :], ACT.Copy).then_inc(a_pt, 1)
                        if has(i + 2):
                            n = i + 2
                            act.wait_ge(p_q, n + 1)
                            wait(act, v_qs, n)
                            nc.scalar.activation(hq[:, :], psQ[:, :], ACT.Copy, scale=lo[:, 0:1]).then_inc(a_hq, 1)
                            nc.scalar.activation(hk[:, :], psK[:, P:2 * P], ACT.Copy, scale=lo[:, 1:2]).then_inc(a_hq, 1)
                        if has(i + 1):
                            act.wait_ge(v_sub, i + 2)
                            pn = pr[:, 1 - u, :, :].rearrange("p h k -> p (h k)")
                            nc.scalar.activation(pn, pn, ACT.Exp, scale=s2[:, 3:4]).then_inc(a_ex, 1)
                    run_steps(act, step)

                @block.vector
                def _(dve):
                    nc.vector.tensor_copy(
                        wrep[:, 0:QA, :, :, :].rearrange("p a g r d -> p (a g) r d"),
                        wq_sb[:, :].rearrange("p (h d) -> p h d", d=DK).unsqueeze(2).broadcast_to([P, NH, 4, DK])).then_inc(v_c, 1)
                    nc.vector.tensor_copy(
                        wrep[:, QA, :, :, :].rearrange("p g r d -> p (g r) d"),
                        wk_sb[:, :].unsqueeze(1).broadcast_to([P, 16, DK])).then_inc(v_c, 1)
                    nc.vector.tensor_reduce(m4[:, :], ident[:, :].rearrange("p (g r d) -> p r g d", g=4, r=4),
                                            AX.XY, ALU.add).then_inc(v_c, 1)
                    for b in range(2):
                        nc.vector.tensor_copy(ob[:, b, :, :], pm[:, :].unsqueeze(2).broadcast_to([P, 2, DK])).then_inc(v_c, 1)
                    dve.wait_ge(v_c, 5)
                    nc.vector.tensor_scalar(s2[:, 5:8], pw[:, 5:8], 2.0 ** -13, None, ALU.mult).then_inc(v_s2, 1)
                    dve.wait_ge(v_s2, 1)
                    nc.vector.reciprocal(s2[:, 0:3], s2[:, 5:8]).then_inc(v_s2, 1)
                    nc.vector.scalar_tensor_tensor(s2[:, 3:4], pw[:, 5:6], 2.0 ** -14 * DK ** -0.5, pw[:, 6:7],
                                                   ALU.mult, ALU.mult).then_inc(v_s2, 1)
                    nc.vector.tensor_scalar(s2[:, 4:5], pw[:, 7:8], 2.0 ** -13 / S, None, ALU.mult).then_inc(v_s2, 1)
                    dve.wait_ge(v_s2, 4)
                    nc.vector.tensor_scalar(pmv[:, :], pm[:, :], s2[:, 4:5], None, ALU.mult).then_inc(v_s2, 1)
                    nc.vector.tensor_tensor(lo[:, 0:1], m4[:, 2:3], m4[:, 3:4], ALU.add).then_inc(v_c, 1)
                    nc.vector.tensor_tensor(lo[:, 1:2], m4[:, 1:2], m4[:, 3:4], ALU.add).then_inc(v_c, 1)
                    dve.wait_ge(v_c, 7)
                    nc.vector.tensor_scalar(lo[:, :], lo[:, :], DOWN, None, ALU.mult).then_inc(v_s2, 1)
                    for n in range(NPAIR):
                        nc.vector.bn_stats(st6[:, n, :], Xp[:, n, :]).then_inc(v_st, 1)
                    for n in range(NPAIR):
                        dve.wait_ge(v_st, n + 1)
                        nc.vector.bn_aggr(mv[:, n, :], st6[:, n, :]).then_inc(v_st, 1)
                    dve.wait_ge(v_st, 2 * NPAIR)
                    nc.vector.tensor_scalar(sd[:, :], mv[:, :, 1], EPS, None, ALU.add).then_inc(v_st, 1)
                    for a in range(QA + 1):
                        dve.wait_ge(a_w2, a + 1)
                        nc.vector.scalar_tensor_tensor(wst[:, 1, a, :], wrep[:, a, :, :, :].rearrange("p g r d -> p (g r d)"),
                                                       s2[:, a // QA:a // QA + 1], wst[:, 0, a, :],
                                                       ALU.mult, ALU.subtract).then_inc(v_w2, 1)
                    dve.wait_ge(a_w2, QA + 2)
                    nc.vector.scalar_tensor_tensor(wvs[:, 1, :], wv_sb[:, :], s2[:, 2:3], wvs[:, 0, :],
                                                   ALU.mult, ALU.subtract).then_inc(v_w2, 1)
                    dve.wait_ge(a_sd, 1)
                    nc.vector.reciprocal(rs[:, :], sd[:, :]).then_inc(v_rs, 1)
                    dve.wait_ge(v_rs, 1)
                    dve.wait_ge(v_s2, 6)
                    mvf = mv[:, :, :].rearrange("p n k -> p (n k)")

                    def step(i, u):
                        if has(i + 2):
                            n = i + 2
                            dve.wait_ge(a_xh, n + 1)
                            nc.vector.scalar_tensor_tensor(xh[:, u, 1, :], psK[:, 0:P], S, xh[:, u, 0, :],
                                                           ALU.mult, ALU.subtract).then_inc(v_xl, 1)
                        if has(i + 3):
                            n = i + 3
                            wait(dve, p_xt, n - 1)
                            nc.vector.tensor_scalar(xn[:, 1 - u, :], X[:, bass.ds(n * D, D)], mvf[:, bass.ds(n * 2, 1)],
                                                    rs[:, bass.ds(n, 1)], ALU.subtract, ALU.mult).then_inc(v_xn, 1)
                        if has(i - 1):
                            n = i - 1
                            dve.wait_ge(p_ot, n + 1)
                            for b in range(2):
                                q = slice(64 * b, 64 * b + 64)
                                nc.vector.reciprocal(
                                    rden[q, :].rearrange("p (k h) -> p k h", h=2),
                                    psT[q, 1, 256:512].rearrange("p (k b h d) -> p k b h d", b=2, h=2, d=DK)[:, :, b, :, 0]
                                ).then_inc(v_rd, 1)
                            dve.wait_ge(v_rd, 2 * n + 2)
                            for b in range(2):
                                q = slice(64 * b, 64 * b + 64)
                                nc.vector.tensor_tensor(
                                    yv[q, :, :].rearrange("p (k h) d -> p k h d", h=2),
                                    psT[q, 1, 0:256].rearrange("p (k b h d) -> p k b h d", b=2, h=2, d=DK)[:, :, b, :, :],
                                    rden[q, :].rearrange("p (k h) -> p k h", h=2).unsqueeze(3).broadcast_to([64, 8, 2, DK]),
                                    ALU.mult).then_inc(v_y, 1)
                            dve.wait_ge(v_y, 2 * n + 2)
                            xrow = X[:, bass.ds(n * D, D)].rearrange("p (a g d) -> p a g d", a=QA, g=4)
                            nc.vector.tensor_tensor(xrow, xrow, yv[:, :, :].rearrange("p (g a) d -> p a g d", g=4),
                                                    ALU.add).then_inc(v_x1, 1)
                        if has(i + 1):
                            n = i + 1
                            dve.wait_ge(p_s, n + 1)
                            sv = psSc[:, :, 0:256].rearrange("p g (a k) -> p g a k", a=QA)
                            mxv = pmx[:, 1 - u, :].rearrange("p (g a) -> p g a", g=4)
                            nc.vector.tensor_reduce(mxv, sv, AX.X, ALU.max).then_inc(v_m, 1)
                            dve.wait_ge(v_m, n + 1)
                            wait(dve, p_pt, 2 * (n - 1))
                            nc.vector.tensor_tensor(pr[:, 1 - u, :, :].rearrange("p (g a) k -> p g a k", g=4), sv,
                                                    mxv.unsqueeze(3).broadcast_to([P, 4, QA, 64]),
                                                    ALU.subtract).then_inc(v_sub, 1)
                        if has(i + 2):
                            n = i + 2
                            dve.wait_ge(a_hq, 2 * n + 2)
                            nc.vector.scalar_tensor_tensor(KS[:, u, :], psK[:, P:2 * P], DOWN, hk[:, :],
                                                           ALU.mult, ALU.subtract)
                            nc.vector.scalar_tensor_tensor(QS[:, u, :], psQ[:, :], DOWN, hq[:, :],
                                                           ALU.mult, ALU.subtract).then_inc(v_qs, 1)
                        if has(i + 1):
                            n = i + 1
                            dve.wait_ge(p_q, n + 2)
                            wait(dve, p_o, n - 1)
                            nc.vector.tensor_tensor(
                                VB[:, 1 - u, :, :, :],
                                psK[:, 256:272].rearrange("p (b d) -> p b d", b=2).unsqueeze(2).broadcast_to([P, 2, 2, DK]),
                                pmv[:, :].unsqueeze(1).unsqueeze(3).broadcast_to([P, 2, 2, DK]),
                                ALU.mult).then_inc(v_vb, 1)
                    run_steps(dve, step)

        clear_semaphores()

        with ExitStack() as c3:
            def sb(name, shape, dt=F32):
                return c3.enter_context(nc.sbuf_tensor(name, shape, dt))
            st6 = sb("st6b", [P, NPAIR, 6])
            mv = sb("mvb", [P, NPAIR, 2])
            sd = sb("sdb", [P, NPAIR])
            rs = sb("rsb", [P, NPAIR])
            xn = sb("xnb", [P, 8, D])
            psX = c3.enter_context(nc.psum_tensor("psX", [P, 2, 512], F32))
            s_x1 = sem("s_x1")
            v_st = sem("v_st3")
            a_sd = sem("a_sd3")
            v_rs = sem("v_rs3")
            v_xn = sem("v_xn3")
            p_xt = sem("p_xt3")
            a_xt = sem("a_xt3")
            v_xt = sem("v_xt3")
            v_st3z = sem("v_st3z")
            NC4 = NPAIR // 4
            with nc.Block() as block:
                @block.sync
                def _(sync):
                    sync.dma_start(x1_dram.rearrange("(n two) t d -> (two t) n d", two=2), Xp).then_inc(s_x1, 16)
                    sync.wait_ge(s_x1, 16)

                @block.tensor
                def _(pe):
                    for c in range(NC4):
                        if c >= 2:
                            pe.wait_ge(v_xt, c - 1)
                        for n in range(4):
                            pe.wait_ge(v_xn, 4 * c + n + 1)
                            mm = nc.tensor.transpose(psX[:, c % 2, n * P:(n + 1) * P], xn[:, (4 * c + n) % 8, :], ident[:, :])
                        mm.then_inc(p_xt, 1)

                def parts(part, c):
                    return XT[:, part, :, 8 * c:8 * c + 8].rearrange("p t b -> p b t")

                @block.scalar
                def _(act):
                    act.wait_ge(v_st3z, 1)
                    nc.scalar.activation(sd[:, :], sd[:, :], ACT.Sqrt).then_inc(a_sd, 1)
                    for c in range(NC4):
                        act.wait_ge(p_xt, c + 1)
                        nc.scalar.activation(parts(0, c), psX[:, c % 2, :].rearrange("p (b t) -> p b t", t=T),
                                             ACT.Copy, scale=S).then_inc(a_xt, 1)

                @block.vector
                def _(dve):
                    for n in range(NPAIR):
                        nc.vector.bn_stats(st6[:, n, :], Xp[:, n, :]).then_inc(v_st, 1)
                    for n in range(NPAIR):
                        dve.wait_ge(v_st, n + 1)
                        nc.vector.bn_aggr(mv[:, n, :], st6[:, n, :]).then_inc(v_st, 1)
                    dve.wait_ge(v_st, 2 * NPAIR)
                    nc.vector.tensor_scalar(sd[:, :], mv[:, :, 1], EPS, None, ALU.add).then_inc(v_st3z, 1)
                    dve.wait_ge(a_sd, 1)
                    nc.vector.reciprocal(rs[:, :], sd[:, :]).then_inc(v_rs, 1)
                    dve.wait_ge(v_rs, 1)
                    for c in range(NC4 + 1):
                        if c < NC4:
                            if c >= 2:
                                dve.wait_ge(p_xt, c - 1)
                            for n in range(4 * c, 4 * c + 4):
                                nc.vector.tensor_scalar(xn[:, n % 8, :], Xp[:, n, :], mv[:, n, 0:1], rs[:, n:n + 1],
                                                        ALU.subtract, ALU.mult).then_inc(v_xn, 1)
                        if c >= 1:
                            k = c - 1
                            dve.wait_ge(a_xt, k + 1)
                            nc.vector.scalar_tensor_tensor(
                                parts(1, k), psX[:, k % 2, :].rearrange("p (b t) -> p b t", t=T), S, parts(0, k),
                                ALU.mult, ALU.subtract).then_inc(v_xt, 1)

        clear_semaphores()

        with ExitStack() as c4:
            def sb(name, shape, dt=F32):
                return c4.enter_context(nc.sbuf_tensor(name, shape, dt))

            class Group:
                pass
            G = []
            for g in range(2):
                q = Group()
                q.g = g
                t = "ab"[g]
                q.xs = sb(f"xs_{t}", [P, 2, GB], F16)
                q.gt = [sb(f"gt{l}_{t}", [P, 4, GB]) for l in range(2)]
                q.u = [sb(f"u{l}_{t}", [P, 2, GB]) for l in range(2)]
                q.c = [sb(f"c{l}_{t}", [P, GB]) for l in range(2)]
                q.tc = [sb(f"tc{l}_{t}", [P, GB]) for l in range(2)]
                q.os = [sb(f"os{l}_{t}", [P, GB]) for l in range(2)]
                q.h32 = [sb(f"h32{l}_{t}", [P, GB]) for l in range(2)]
                q.h = [sb(f"h{l}_{t}", [P, GB + PAD, 2], F16) for l in range(2)]
                q.a = sb(f"a_{t}", [P, GB, 2], F16)
                q.a32 = sb(f"a32_{t}", [P, GB])
                q.sm = sb(f"sm_{t}", [P, GB, 2])
                q.nm = sb(f"nm_{t}", [64, 1])
                q.p = sb(f"p_{t}", [64, 64])
                q.sum = sb(f"sum_{t}", [64, 1])
                q.r = sb(f"r_{t}", [64, 1])
                q.pe = sb(f"pe_{t}", [P, P])
                q.pm = sb(f"pmv_{t}", [P, GB + PAD, 2], F16)
                q.ar = sb(f"ar_{t}", [P, GB])
                ps = lambda n: c4.enter_context(nc.psum_tensor(f"{n}_{t}", [P, 512], F32))
                q.z = [ps("z0"), ps("z1")]
                q.S = ps("sc")
                q.M = ps("mx")
                q.Sv = q.S[:, :].rearrange("p (n w) -> p n w", w=WIDE)[:, :, 0:4]
                q.Mv = q.M[:, :].rearrange("p (n w) -> p n w", w=WIDE)[:, :, 0:4].rearrange(
                    "p n (b k) -> p n b k", k=2)
                q.s_xs = sem(f"xs_{t}")
                q.s_xu = sem(f"xu_{t}")
                q.s_sc = sem(f"sc_{t}")
                q.s_st = sem(f"st_{t}")
                q.s_pt = sem(f"pt_{t}")
                q.s_mx = sem(f"mx_{t}")
                q.s_ex = sem(f"ex_{t}")
                q.s_ta = sem(f"ta_{t}")
                q.s_sm = sem(f"sm_{t}")
                q.s_nm = sem(f"nm_{t}")
                q.s_r = sem(f"r_{t}")
                q.s_pe = sem(f"pe_{t}")
                q.s_pm = sem(f"pm_{t}")
                q.s_ar = sem(f"ar_{t}")
                q.s_ah = sem(f"ah_{t}")
                q.s_ao = sem(f"ao_{t}")
                q.s_z = [sem(f"z{l}_{t}") for l in range(2)]
                q.s_tg = [sem(f"tg{l}_{t}") for l in range(2)]
                q.s_tc = [sem(f"tc{l}_{t}") for l in range(2)]
                q.s_uv = [sem(f"uv{l}_{t}") for l in range(2)]
                q.s_c = [sem(f"c{l}_{t}") for l in range(2)]
                q.s_os = [sem(f"os{l}_{t}") for l in range(2)]
                q.s_h = [sem(f"h{l}_{t}") for l in range(2)]
                q.s_h32 = [sem(f"h32{l}_{t}") for l in range(2)]
                G.append(q)
            s_zero = sem("s_zero")
            zt = sb("zt", [P, 8 * D])
            v_zt = sem("v_zt")
            d_z = sem("d_z")

            def run_halves(half, eng):
                half(G[0], None, 0, None)
                half(G[1], G[0], 0, 0)
                half(G[0], G[1], 1, 0)
                with eng.Fori(1, T - 1) as t:
                    half(G[1], G[0], t, t)
                    half(G[0], G[1], t + 1, t)
                half(G[1], G[0], T - 1, T - 1)
                half(None, G[1], None, T - 1)

            with nc.Block() as block:
                @block.sync
                def _(sync):
                    sync.wait_ge(v_zt, 1)
                    for k in range(NT // 8):
                        sync.dma_start(xs_dram[k * 8 * P:(k + 1) * 8 * P, :].rearrange("(p j) d -> p (j d)", j=8),
                                       zt[:, :]).then_inc(d_z, 16)
                    sync.wait_ge(d_z, 16 * (NT // 8))

                @block.tensor
                def _(pe):
                    pe.wait_ge(s_zero, 18)

                    def gates(q, layer, blk, mov, parts=((0, 0), (1, 0), (0, 1))):
                        for j in range(4):
                            for w, m in parts:
                                mm = nc.tensor.matmul(q.z[layer][:, j * GB:(j + 1) * GB], WL[:, blk + j, w, :],
                                                      mov[m], start=False, stop=False, skip_group_check=True)
                        return mm

                    def gates_as_ready(q, layer, blk, mov, ready, t):
                        wait(pe, ready, 2 * t - 1)
                        gates(q, layer, blk, mov, ((0, 0), (1, 0)))
                        wait(pe, ready, 2 * t)
                        return gates(q, layer, blk, mov, ((0, 1),))

                    def bias(q, layer):
                        for j in range(4):
                            nc.tensor.matmul(q.z[layer][:, j * GB:(j + 1) * GB], BL[:, layer, j * P:(j + 1) * P],
                                             onesb[:, :], start=(j == 0), stop=False, skip_group_check=True)

                    def early0h(q):
                        bias(q, 0)
                        gates(q, 0, WH0, [q.h[0][:, 0:GB, k] for k in range(2)])

                    def early0x(q, t):
                        pe.wait_ge(q.s_xs, t + 1)
                        gates(q, 0, WX0, [q.xs[:, k, :] for k in range(2)]).then_inc(q.s_xu, 1)

                    def early1(q):
                        bias(q, 1)
                        gates(q, 1, WH1, [q.h[1][:, 0:GB, k] for k in range(2)])

                    def half(L, A, lt, at):
                        last = isinstance(at, int) and at == T - 1
                        def scores(n0, n1):
                            for n in range(n0, n1):
                                pair = A.g * GP + n
                                for k in range(2):
                                    mm = nc.tensor.matmul(A.S[:, WIDE * n:WIDE * (n + 1)],
                                                          KH[:, k, pair * P:(pair + 1) * P],
                                                          A.h[1][:, 2 * n:2 * n + WIDE // 2, :].rearrange("p b k -> p (b k)"),
                                                          start=(k == 0), stop=(k == 1))
                            return mm
                        if A:
                            pe.wait_ge(A.s_h[1], 2 * at + 2)
                            scores(0, NSPLIT)
                        if L:
                            gates_as_ready(L, 0, WA0, [L.a[:, :, k] for k in range(2)], L.s_ah, lt).then_inc(L.s_z[0], 1)
                        if A:
                            scores(NSPLIT, GP).then_inc(A.s_sc, 1)
                            if not last:
                                early0h(A)
                            pe.wait_ge(A.s_sm, at + 1)
                            for k in range(2):
                                mm = nc.tensor.matmul(A.S[0:64, 0:64], A.sm[:, :, k], II[:, :],
                                                      start=(k == 0), stop=(k == 1))
                            mm.then_inc(A.s_st, 1)
                            if not last:
                                early1(A)
                        if L:
                            gates_as_ready(L, 1, WI1, [L.h[0][:, 0:GB, k] for k in range(2)], L.s_h[0],
                                           lt + 1).then_inc(L.s_z[1], 1)
                        if A:
                            pe.wait_ge(A.s_pe, at + 1)
                            nc.tensor.transpose(A.S[:, 128:256], A.pe[:, :], ident[:, :]).then_inc(A.s_pt, 1)
                            if not last:
                                early0x(A, at + 1)
                        if A:
                            for k, (w, m) in enumerate(((0, 0), (1, 0), (0, 1))):
                                nc.tensor.matmul(A.Mv[:, :, :, 0], WO2[:, w, :],
                                                 A.h[1][:, 0:GB, m].rearrange("p (n b) -> p n b", b=2),
                                                 start=(k == 0), stop=False, skip_group_check=True)
                            pe.wait_ge(A.s_pm, 2 * at + 2)
                            for n in range(GP):
                                pair = A.g * GP + n
                                for k in range(2):
                                    mm = nc.tensor.matmul(A.M[:, WIDE * n:WIDE * (n + 1)], VH[:, k, pair, :],
                                                          A.pm[:, 2 * n:2 * n + WIDE // 2, :].rearrange("p b k -> p (b k)"),
                                                          start=False, stop=False, skip_group_check=True)
                            mm.then_inc(A.s_mx, 1)

                    for q in G:
                        early0h(q)
                        early0x(q, 0)
                        early1(q)
                    run_halves(half, pe)

                @block.scalar
                def _(act):
                    def half(L, A, lt, at):
                        def gate_tanh(l):
                            act.wait_ge(L.s_z[l], lt + 1)
                            nc.scalar.activation(L.gt[l][:, :, :].rearrange("p g b -> p (g b)"), L.z[l][:, 0:4 * GB],
                                                 ACT.Tanh, scale=sc[:, I0 + l:I0 + l + 1]).then_inc(L.s_tg[l], 1)

                        def out_gate(l):
                            act.wait_ge(L.s_tg[l], lt + 1)
                            nc.scalar.activation(L.os[l][:, :], L.gt[l][:, 3, :], ACT.Copy, scale=S / 2,
                                                 bias=S / 2).then_inc(L.s_os[l], 1)

                        def cell_tanh(l):
                            act.wait_ge(L.s_c[l], lt + 1)
                            nc.scalar.activation(L.tc[l][:, :], L.c[l][:, :], ACT.Tanh, scale=0.5).then_inc(L.s_tc[l], 1)
                        if L:
                            gate_tanh(0)
                            out_gate(0)
                            cell_tanh(0)
                        if A:
                            act.wait_ge(A.s_nm, at + 1)
                            nc.scalar.activation(A.p[:, :], A.S[0:64, 0:64], ACT.Exp, bias=A.nm[:, 0:1],
                                                 accum_out=A.sum[:, 0:1]).then_inc(A.s_ex, 1)
                        if L:
                            gate_tanh(1)
                            out_gate(1)
                            cell_tanh(1)
                        if A:
                            act.wait_ge(A.s_ar, at + 1)
                            wait(act, A.s_ao, at)
                            nc.scalar.activation(A.a32[:, :], A.ar[:, :], ACT.Tanh, bias=bo_sb[:, 0:1],
                                                 scale=sc[:, IV:IV + 1]).then_inc(A.s_ta, 1)
                    run_halves(half, act)

                @block.gpsimd
                def _(pool):
                    pool.memset(zt[:, :], 0.0).then_inc(v_zt, 1)
                    for q in G:
                        for tile in (q.h[0], q.h[1], q.a, q.pm):
                            pool.memset(tile[:, :, :], 0.0).then_inc(s_zero, 1)
                        for tile in (q.c[0], q.c[1]):
                            pool.memset(tile[:, :], 0.0).then_inc(s_zero, 1)
                        for k in range(2):
                            pool.tensor_copy(q.xs[:, k, :], XT[:, k, 0, q.g * GB:(q.g + 1) * GB]).then_inc(s_zero, 1)
                        pool.memset(q.pe[:, :], 0.0).then_inc(s_zero, 1)
                    pool.wait_ge(s_zero, 18)
                    for q in G:
                        pool.sem_inc(q.s_xs, 1)

                    def half(L, A, lt, at):
                        if L:
                            if not (isinstance(lt, int) and lt == T - 1):
                                pool.wait_ge(L.s_xu, lt + 1)
                                pool.tensor_copy(L.xs[:, :, :], XTn(L, lt + 1)).then_inc(L.s_xs, 1)
                        if A:
                            pool.wait_ge(A.s_ta, at + 1)
                            pool.tensor_copy(X[:, bass.ds(at * B + A.g * GB, GB)], A.a32[:, :]).then_inc(A.s_ao, 1)

                    def XTn(L, t):
                        return XTf[:, :, bass.ds(t * B + L.g * GB, GB)]
                    XTf = XT[:, :, :, :].rearrange("p k t b -> p k (t b)")

                    half(G[0], None, 0, None)
                    half(G[1], G[0], 0, 0)
                    half(G[0], G[1], 1, 0)
                    with pool.Fori(1, T - 2) as t:
                        half(G[1], G[0], t, t)
                        half(G[0], G[1], t + 1, t)
                    half(G[1], G[0], T - 2, T - 2)
                    half(G[0], G[1], T - 1, T - 2)
                    half(G[1], G[0], T - 1, T - 1)
                    half(None, G[1], None, T - 1)

                @block.vector
                def _(dve):
                    dve.wait_ge(s_zero, 18)

                    def half(L, A, lt, at):
                        def cell(l):
                            dve.wait_ge(L.s_tg[l], lt + 1)
                            nc.vector.scalar_tensor_tensor(L.u[l][:, 0, :], L.gt[l][:, 1, :], 1.0, L.c[l][:, :],
                                                           ALU.add, ALU.mult).then_inc(L.s_uv[l], 1)
                            nc.vector.scalar_tensor_tensor(L.u[l][:, 1, :], L.gt[l][:, 0, :], 1.0, L.gt[l][:, 2, :],
                                                           ALU.add, ALU.mult).then_inc(L.s_uv[l], 1)
                            dve.wait_ge(L.s_uv[l], 2 * lt + 2)
                            nc.vector.scalar_tensor_tensor(L.c[l][:, :], L.u[l][:, 0, :], 0.5, L.u[l][:, 1, :],
                                                           ALU.mult, ALU.add).then_inc(L.s_c[l], 1)

                        def hidden(l):
                            dve.wait_ge(L.s_tc[l], lt + 1)
                            dve.wait_ge(L.s_os[l], lt + 1)
                            nc.vector.tensor_tensor(L.h[l][:, 0:GB, 0], L.os[l][:, :], L.tc[l][:, :],
                                                    ALU.mult).then_inc(L.s_h[l], 1)
                            nc.vector.tensor_tensor(L.h32[l][:, :], L.os[l][:, :], L.tc[l][:, :],
                                                    ALU.mult).then_inc(L.s_h32[l], 1)

                        def hidden_low(l):
                            dve.wait_ge(L.s_h32[l], lt + 1)
                            dve.wait_ge(L.s_h[l], 2 * lt + 1)
                            nc.vector.tensor_tensor(L.h[l][:, 0:GB, 1], L.h32[l][:, :], L.h[l][:, 0:GB, 0],
                                                    ALU.subtract).then_inc(L.s_h[l], 1)
                        if A:
                            dve.wait_ge(A.s_sc, at + 1)
                            nc.vector.tensor_tensor(A.sm[:, :, :].rearrange("p (n b) k -> p n (b k)", b=2), A.Sv,
                                                    smask[:, :].rearrange("p (n w) -> p n w", w=4), ALU.mult).then_inc(A.s_sm, 1)
                        if L:
                            cell(0)
                        if A:
                            dve.wait_ge(A.s_st, at + 1)
                            nc.vector.tensor_reduce(A.nm[:, :], A.S[0:64, 0:64], AX.X, ALU.max,
                                                    negate=True).then_inc(A.s_nm, 1)
                        if L:
                            hidden(0)
                        if A:
                            dve.wait_ge(A.s_ex, at + 1)
                            nc.vector.reciprocal(A.r[:, :], A.sum[:, :]).then_inc(A.s_r, 1)
                        if L:
                            hidden_low(0)
                        if A:
                            dve.wait_ge(A.s_r, at + 1)
                            nc.vector.scalar_tensor_tensor(
                                A.pe[0:64, :].rearrange("p (h s) -> p h s", h=2),
                                A.p[:, :].unsqueeze(1).broadcast_to([64, 2, 64]), A.r[:, 0:1], pmask[:, :, :],
                                ALU.mult, ALU.mult).then_inc(A.s_pe, 1)
                            dve.wait_ge(A.s_pt, at + 1)
                            nc.vector.tensor_copy(A.pm[:, 0:GB, 0], A.S[:, 128:192]).then_inc(A.s_pm, 1)
                            dve.wait_ge(A.s_pm, 2 * at + 1)
                            nc.vector.tensor_tensor(A.pm[:, 0:GB, 1], A.S[:, 128:192], A.pm[:, 0:GB, 0],
                                                    ALU.subtract).then_inc(A.s_pm, 1)
                        if L:
                            cell(1)
                        if L:
                            hidden(1)
                            hidden_low(1)
                        if A:
                            dve.wait_ge(A.s_mx, at + 1)
                            nc.vector.tensor_reduce(A.ar[:, :].rearrange("p (n b) -> p n b", b=2), A.Mv,
                                                    AX.X, ALU.add).then_inc(A.s_ar, 1)
                        if A:
                            dve.wait_ge(A.s_ta, at + 1)
                            nc.vector.tensor_scalar(A.a[:, :, 0], A.a32[:, :], S, None, ALU.mult).then_inc(A.s_ah, 1)
                            dve.wait_ge(A.s_ah, 2 * at + 1)
                            nc.vector.scalar_tensor_tensor(A.a[:, :, 1], A.a32[:, :], S, A.a[:, :, 0],
                                                           ALU.mult, ALU.subtract).then_inc(A.s_ah, 1)
                    run_halves(half, dve)
        recurrence_ctx.close()

        clear_semaphores()

        with ExitStack() as c5:
            def sb(name, shape, dt=F32):
                return c5.enter_context(nc.sbuf_tensor(name, shape, dt))

            def ps(name, shape, dt=F32):
                return c5.enter_context(nc.psum_tensor(name, shape, dt))
            X2 = sb("X2", [P, T, D])
            XN = X[:, :].rearrange("p (t d) -> p t d", d=D)
            w1_sb = sb("w1_sb", [P, NE * FF])
            w2_sb = sb("w2_sb", [P, NE * FC * D])
            b1_sb = sb("b1_sb", [P, NE * FF])
            b2_sb = sb("b2_sb", [P, NE * D])
            rw_sb = sb("rw_sb", [P, NE])
            rbb = sb("rbb", [P, NE])
            wgt = sb("wgt", [P, NE])
            upper = sb("upper", [P, P])
            st6 = sb("st6c", [P, T, 6])
            mv = sb("mvc", [P, T, 2])
            sd = sb("sdc", [P, T])
            rs = sb("rsc", [P, T])
            xT = sb("xTc", [P, 2, 512])
            lg = sb("lg", [P, T, NE])
            m1 = sb("m1", [P, T])
            eg = sb("eg", [P, T, NE])
            one = sb("one", [P, T, NE])
            gate = sb("gate", [P, T])
            tot = sb("tot", [P, T, NE])
            cum = sb("cum", [P, NE, T])
            onesT = sb("onesT", [P, T])
            cnt = sb("cnt", [P, NE])
            cnti = sb("cnti", [P, NE], I32)
            pad = sb("pad", [P, NE])
            end = sb("end", [P, NE])
            slotf = sb("slotf", [P, T])
            slot = sb("slot", [P, T], U32)
            tilestart = sb("tilestart", [P, NT])
            past = sb("past", [P, NT, NE])
            tex = sb("tex", [P, NT])
            etab = sb("etab", [P, 2, NT], I32)
            xg = sb("xg", [P, 2, D])
            xgT = sb("xgT", [P, 2, P])
            hb = sb("hb", [P, 2, FF])
            hT = sb("hT", [P, 2, FC, P])
            ys = sb("ys", [P, 2, D])
            psX = ps("psX5", [P, 2, 512])
            psH = ps("psH", [P, 2, 512])
            psHT = ps("psHT", [P, 2, 512])
            psY = ps("psY", [P, 2, 512])
            psL, psU, psN = psH[:, 0, :], psH[:, 1, :], psHT[:, 0, :]
            s_x2 = sem("s_x2")
            s_wf = sem("s_wf")
            p_a = sem("p_a5")
            v_x2 = sem("v_x2")
            v_st = sem("v_st5")
            a_sd = sem("a_sd5")
            v_rs = sem("v_rs5")
            v_xn = sem("v_xn5")
            p_t = sem("p_t5")
            a_t = sem("a_t5")
            p_l = sem("p_l5")
            v_r = sem("v_r5")
            v_one = sem("v_one")
            v_sub = sem("v_sub5")
            a_eg = sem("a_eg")
            p_n = sem("p_n5")
            v_slot = sem("v_slot")
            g_c = sem("g_c")
            v_c = sem("v_c5")
            d_sc = sem("d_sc")
            d_xg = [sem(f"d_xg{u}") for u in range(2)]
            p_xt = sem("p_xt5")
            a_xt = sem("a_xt5")
            p_h = sem("p_h")
            v_hb = sem("v_hb")
            p_ht = sem("p_ht")
            a_ht = sem("a_ht")
            p_y = sem("p_y")
            v_ys = sem("v_ys")
            d_ys = [sem(f"d_ys{u}") for u in range(2)]
            d_yg = [sem(f"d_yg{c}") for c in range(T // 4)]
            v_out = sem("v_out")
            d_out = sem("d_out")
            NCH = T // 4
            x_rows = xs_dram.rearrange("(j p) d -> p j d", p=P)
            y_rows = ys_dram.rearrange("(j p) d -> p j d", p=P)

            with nc.Block() as block:
                @block.sync
                def _(sync):
                    sync.dma_start(X2[:, :, :], x1_dram).then_inc(s_x2, 16)
                    sync.dma_start(rw_sb[:, :], rw).then_inc(s_wf, 16)
                    sync.dma_start(rbb[:, :], rb.rearrange("(a n) -> a n", a=1).broadcast_to([P, NE])).then_inc(s_wf, 16)
                    sync.dma_start(w1_sb[:, :].rearrange("p (e f) -> p e f", e=NE), w1.rearrange("e p f -> p e f")).then_inc(s_wf, 16)
                    sync.dma_start(w2_sb[:, :].rearrange("p (e c n) -> p e c n", e=NE, c=FC),
                                   w2.rearrange("e (c p) n -> p e c n", p=P)).then_inc(s_wf, 16)
                    sync.dma_start(b1_sb[:, :], b1.rearrange("(a e) f -> a (e f)", a=1).broadcast_to([P, NE * FF])).then_inc(s_wf, 16)
                    sync.dma_start(b2_sb[:, :], b2.rearrange("(a e) f -> a (e f)", a=1).broadcast_to([P, NE * D])).then_inc(s_wf, 16)

                    def load(j, u):
                        wait(sync, p_xt, j - 1)
                        sync.dma_start(xg[:, u, :], x_rows[:, bass.ds(j, 1), :].rearrange("p j d -> p (j d)")).then_inc(d_xg[u], 16)

                    def store(j, u):
                        sync.wait_ge(v_ys, j + 1)
                        sync.dma_start(y_rows[:, bass.ds(j, 1), :].rearrange("p j d -> p (j d)"), ys[:, u, :]).then_inc(d_ys[u], 16)
                    sync.wait_ge(d_sc, 16 * T)
                    load(0, 0)
                    load(1, 1)

                    def two(j):
                        load(j + 2, 0)
                        store(j, 0)
                        load(j + 3, 1)
                        store(j + 1, 1)
                    two(0)
                    with sync.Fori(2, NT - 3, 2) as j:
                        two(j)
                    store(NT - 2, 0)
                    store(NT - 1, 1)
                    for c in range(NCH):
                        sync.wait_ge(v_out, 4 * c + 4)
                        sync.dma_start(out[:, 4 * c:4 * c + 4, :], X2[:, 4 * c:4 * c + 4, :]).then_inc(d_out, 16)
                    sync.wait_ge(d_out, 16 * NCH)

                @block.gpsimd
                def _(pool):
                    pool.memset(upper[:, :], 1.0).then_inc(g_c, 1)
                    pool.wait_ge(g_c, 1)
                    pool.affine_select(out=upper[:, :], in_=upper[:, :], compare_op=ALU.is_gt, fill=0.0,
                                       base=0, pattern=[[1, P]], channel_multiplier=-1).then_inc(g_c, 1)
                    for t in range(T):
                        pool.wait_ge(v_slot, 1)
                        pool.indirect_dma_start(xs_dram, bass.IndirectOffsetOnAxis(slot[:, t:t + 1], 0),
                                                XN[:, t, :], None).then_inc(d_sc, 16)
                    pool.wait_ge(d_sc, 16 * T)
                    for u in range(2):
                        pool.wait_ge(d_ys[u], 8 * NT)
                    for t in range(T):
                        pool.indirect_dma_start(XN[:, t, :], None, ys_dram,
                                                bass.IndirectOffsetOnAxis(slot[:, t:t + 1], 0)).then_inc(d_yg[t // 4], 16)

                @block.tensor
                def _(pe):
                    for c in range(NCH):
                        if c >= 2:
                            pe.wait_ge(v_x2, c - 1)
                        for n in range(4):
                            mm = nc.tensor.transpose(psX[:, c % 2, n * P:(n + 1) * P], XA[:, 4 * c + n, :], ident[:, :])
                        mm.then_inc(p_a, 1)
                    pe.wait_ge(s_wf, 96)

                    def logits(c):
                        pe.wait_ge(a_t, c + 1)
                        for n in range(4):
                            t = 4 * c + n
                            mm = nc.tensor.matmul(psL[:, t * NE:(t + 1) * NE], xT[:, c % 2, n * P:(n + 1) * P], rw_sb[:, :],
                                                  start=True, stop=True)
                        mm.then_inc(p_l, 1)
                    pe.wait_ge(v_x2, NCH)
                    for c in range(NCH):
                        if c >= 2:
                            pe.wait_ge(a_t, c - 1)
                        for n in range(4):
                            pe.wait_ge(v_xn, 4 * c + n + 1)
                            mm = nc.tensor.transpose(psX[:, c % 2, n * P:(n + 1) * P], XN[:, 4 * c + n, :], ident[:, :])
                        mm.then_inc(p_t, 1)
                        if c >= 1:
                            logits(c - 1)
                    logits(NCH - 1)
                    pe.wait_ge(g_c, 2)
                    pe.wait_ge(v_one, 1)
                    of = one[:, :, :].rearrange("p t e -> p (t e)")
                    nc.tensor.matmul(psN, ones[:, :], of, start=True, stop=True).then_inc(p_n, 1)
                    nc.tensor.matmul(psU, upper[:, :], of, start=True, stop=True).then_inc(p_n, 1)

                    def turn(j, u):
                        pe.wait_ge(d_xg[u], 8 * (j - u) + 16)
                        wait(pe, a_xt, j - 1)
                        nc.tensor.transpose(psX[:, u, 0:P], xg[:, u, :], ident[:, :]).then_inc(p_xt, 1)

                    def hidden(j, u):
                        col = pe.value_load(etab[0:1, 0, bass.ds(j, 1)], min_val=0, max_val=(NE - 1) * FF)
                        pe.wait_ge(a_xt, j + 1)
                        wait(pe, v_hb, j - 1)
                        nc.tensor.matmul(psH[:, u, :], xgT[:, u, :], w1_sb[:, bass.ds(col, FF)],
                                         start=True, stop=True).then_inc(p_h, 1)

                    def turn_hidden(j, u):
                        pe.wait_ge(v_hb, j + 1)
                        wait(pe, a_ht, j - 1)
                        for c in range(FC):
                            mm = nc.tensor.transpose(psHT[:, u, c * P:(c + 1) * P], hb[:, u, c * P:(c + 1) * P], ident[:, :])
                        mm.then_inc(p_ht, 1)

                    def output(j, u):
                        col = pe.value_load(etab[0:1, 0, bass.ds(j, 1)], min_val=0, max_val=(NE - 1) * FF)
                        pe.wait_ge(a_ht, j + 1)
                        wait(pe, v_ys, j - 1)
                        for c in range(FC):
                            mm = nc.tensor.matmul(psY[:, u, 0:P], hT[:, u, c, :], w2_sb[:, bass.ds(col + c * P, P)],
                                                  start=(c == 0), stop=(c == FC - 1))
                        mm.then_inc(p_y, 1)
                    pe.wait_ge(v_slot, 2)
                    turn(0, 0)
                    hidden(0, 0)

                    def step(j, u):
                        turn(j + 1, 1 - u)
                        turn_hidden(j, u)
                        hidden(j + 1, 1 - u)
                        output(j, u)
                    step(0, 0)
                    step(1, 1)
                    with pe.Fori(2, NT - 3, 2) as j:
                        step(j, 0)
                        step(j + 1, 1)
                    step(NT - 2, 0)
                    turn_hidden(NT - 1, 1)
                    output(NT - 1, 1)

                @block.scalar
                def _(act):
                    act.wait_ge(v_st, 2 * T + 1)
                    nc.scalar.activation(sd[:, :], sd[:, :], ACT.Sqrt).then_inc(a_sd, 1)
                    for c in range(NCH):
                        act.wait_ge(p_t, c + 1)
                        if c >= 2:
                            act.wait_ge(p_l, c - 1)
                        nc.scalar.activation(xT[:, c % 2, :], psX[:, c % 2, :], ACT.Copy).then_inc(a_t, 1)
                    act.wait_ge(v_sub, 2)
                    nc.scalar.activation(eg[:, :, :], eg[:, :, :], ACT.Exp).then_inc(a_eg, 1)

                    def turned(j, u):
                        act.wait_ge(p_xt, j + 1)
                        wait(act, p_h, j - 1)
                        nc.scalar.activation(xgT[:, u, :], psX[:, u, 0:P], ACT.Copy).then_inc(a_xt, 1)

                    def relu(j, u):
                        act.wait_ge(p_ht, j + 1)
                        wait(act, p_y, j - 1)
                        nc.scalar.activation(hT[:, u, :, :].rearrange("p c n -> p (c n)"), psHT[:, u, :],
                                             ACT.Relu).then_inc(a_ht, 1)
                    turned(0, 0)

                    def step(j, u):
                        turned(j + 1, 1 - u)
                        relu(j, u)
                    step(0, 0)
                    step(1, 1)
                    with act.Fori(2, NT - 3, 2) as j:
                        step(j, 0)
                        step(j + 1, 1)
                    step(NT - 2, 0)
                    relu(NT - 1, 1)

                @block.vector
                def _(dve):
                    for e in range(NE):
                        dve.memset(wgt[:, e:e + 1], float(NE - e)).then_inc(v_c, 1)
                    dve.memset(onesT[:, :], 1.0).then_inc(v_c, 1)
                    dve.memset(tilestart[:, :], float(P)).then_inc(v_c, 1)
                    dve.memset(pad[:, :], 1.0).then_inc(v_c, 1)
                    dve.wait_ge(s_x2, 16)
                    for c in range(NCH):
                        dve.wait_ge(p_a, c + 1)
                        xc = X2[:, 4 * c:4 * c + 4, :].rearrange("p t d -> p (t d)")
                        nc.vector.tensor_tensor(xc, psX[:, c % 2, :], xc, ALU.add).then_inc(v_x2, 1)
                    dve.wait_ge(v_x2, NCH)
                    for n in range(T):
                        nc.vector.bn_stats(st6[:, n, :], X2[:, n, :]).then_inc(v_st, 1)
                    for n in range(T):
                        dve.wait_ge(v_st, n + 1)
                        nc.vector.bn_aggr(mv[:, n, :], st6[:, n, :]).then_inc(v_st, 1)
                    dve.wait_ge(v_st, 2 * T)
                    nc.vector.tensor_scalar(sd[:, :], mv[:, :, 1], EPS, None, ALU.add).then_inc(v_st, 1)
                    dve.wait_ge(a_sd, 1)
                    nc.vector.reciprocal(rs[:, :], sd[:, :]).then_inc(v_rs, 1)
                    dve.wait_ge(v_rs, 1)
                    for n in range(T):
                        nc.vector.tensor_scalar(XN[:, n, :], X2[:, n, :], mv[:, n, 0:1], rs[:, n:n + 1],
                                                ALU.subtract, ALU.mult).then_inc(v_xn, 1)
                    full = [P, T, NE]
                    k = 0

                    def step(ins):
                        nonlocal k
                        k += 1
                        ins.then_inc(v_r, 1)
                        dve.wait_ge(v_r, k)
                    dve.wait_ge(p_l, NCH)
                    dve.wait_ge(s_wf, 96)
                    dve.wait_ge(v_c, NE + 3)
                    step(nc.vector.tensor_tensor(lg[:, :, :], psL.rearrange("p (t e) -> p t e", e=NE),
                                                 rbb[:, :].unsqueeze(1).broadcast_to(full), ALU.add))
                    step(nc.vector.tensor_reduce(m1[:, :], lg[:, :, :], AX.X, ALU.max))
                    nc.vector.tensor_tensor(eg[:, :, :], lg[:, :, :], m1[:, :].unsqueeze(2).broadcast_to(full),
                                            ALU.subtract).then_inc(v_sub, 2)
                    step(nc.vector.tensor_tensor(one[:, :, :], lg[:, :, :], m1[:, :].unsqueeze(2).broadcast_to(full), ALU.is_equal))
                    step(nc.vector.tensor_tensor(one[:, :, :], one[:, :, :], wgt[:, :].unsqueeze(1).broadcast_to(full), ALU.mult))
                    step(nc.vector.tensor_reduce(m1[:, :], one[:, :, :], AX.X, ALU.max))
                    nc.vector.tensor_tensor(one[:, :, :], one[:, :, :], m1[:, :].unsqueeze(2).broadcast_to(full),
                                            ALU.is_equal).then_inc(v_one, 1)
                    dve.wait_ge(p_n, 1)
                    step(nc.vector.tensor_copy(tot[:, :, :], psN.rearrange("p (t e) -> p t e", e=NE)))
                    for e in range(NE - 1):
                        nc.vector.tensor_tensor_scan(cum[:, e, :], onesT[:, :], tot[:, :, e], 0.0, ALU.mult, ALU.add).then_inc(v_c, 1)
                    step(nc.vector.tensor_tensor_scan(cum[:, NE - 1, :], onesT[:, :], tot[:, :, NE - 1], 0.0, ALU.mult, ALU.add))
                    dve.wait_ge(v_c, 2 * NE + 2)
                    step(nc.vector.tensor_scalar(cnt[:, :], cum[:, :, T - 1], float(P - 1), None, ALU.add))
                    step(nc.vector.tensor_copy(cnti[:, :], cnt[:, :]))
                    step(nc.vector.tensor_scalar(cnti[:, :], cnti[:, :], -P, None, ALU.bitwise_and))
                    step(nc.vector.tensor_copy(cnt[:, :], cnti[:, :]))
                    step(nc.vector.tensor_tensor_scan(end[:, :], pad[:, :], cnt[:, :], 0.0, ALU.mult, ALU.add))
                    step(nc.vector.tensor_tensor(pad[:, :], end[:, :], cnt[:, :], ALU.subtract))
                    cumv = cum[:, :, :].rearrange("p e t -> p t e")
                    step(nc.vector.tensor_tensor(tot[:, :, :], cumv, tot[:, :, :], ALU.subtract))
                    dve.wait_ge(p_n, 2)
                    step(nc.vector.tensor_tensor(tot[:, :, :], psU.rearrange("p (t e) -> p t e", e=NE), tot[:, :, :], ALU.add))
                    step(nc.vector.tensor_tensor(tot[:, :, :], tot[:, :, :], pad[:, :].unsqueeze(1).broadcast_to(full), ALU.add))
                    step(nc.vector.tensor_tensor(tot[:, :, :], tot[:, :, :], one[:, :, :], ALU.mult))
                    step(nc.vector.tensor_reduce(slotf[:, :], tot[:, :, :], AX.X, ALU.add))
                    nc.vector.tensor_copy(slot[:, :], slotf[:, :]).then_inc(v_slot, 1)
                    step(nc.vector.tensor_tensor_scan(tex[:, :], ones[:, 0:NT], tilestart[:, :], -float(P), ALU.mult, ALU.add))
                    step(nc.vector.tensor_tensor(past[:, :, :], tex[:, :].unsqueeze(2).broadcast_to([P, NT, NE]),
                                                 end[:, :].unsqueeze(1).broadcast_to([P, NT, NE]), ALU.is_ge))
                    step(nc.vector.tensor_reduce(tex[:, :], past[:, :, :], AX.X, ALU.add))
                    step(nc.vector.tensor_scalar(tex[:, :], tex[:, :], float(NE - 1), None, ALU.min))
                    step(nc.vector.tensor_scalar(etab[:, 0, :], tex[:, :], float(FF), None, ALU.mult))
                    nc.vector.tensor_scalar(etab[:, 1, :], tex[:, :], float(D), None, ALU.mult).then_inc(v_slot, 1)
                    dve.wait_ge(a_eg, 1)
                    step(nc.vector.tensor_reduce(m1[:, :], eg[:, :, :], AX.X, ALU.add))
                    nc.vector.reciprocal(gate[:, :], m1[:, :]).then_inc(v_sub, 1)
                    dve.wait_ge(v_slot, 2)

                    def add_b1(j, u):
                        col = dve.value_load(etab[0:1, 0, bass.ds(j, 1)], min_val=0, max_val=(NE - 1) * FF)
                        dve.wait_ge(p_h, j + 1)
                        wait(dve, p_ht, j - 1)
                        nc.vector.tensor_tensor(hb[:, u, :], psH[:, u, :], b1_sb[:, bass.ds(col, FF)], ALU.add).then_inc(v_hb, 1)

                    def add_b2(j, u):
                        col = dve.value_load(etab[0:1, 1, bass.ds(j, 1)], min_val=0, max_val=(NE - 1) * D)
                        dve.wait_ge(p_y, j + 1)
                        wait(dve, d_ys[u], 8 * (j - u))
                        nc.vector.tensor_tensor(ys[:, u, :], psY[:, u, 0:P], b2_sb[:, bass.ds(col, D)], ALU.add).then_inc(v_ys, 1)
                    add_b1(0, 0)

                    def step2(j, u):
                        add_b1(j + 1, 1 - u)
                        add_b2(j, u)
                    step2(0, 0)
                    step2(1, 1)
                    with dve.Fori(2, NT - 3, 2) as j:
                        step2(j, 0)
                        step2(j + 1, 1)
                    step2(NT - 2, 0)
                    add_b2(NT - 1, 1)
                    for t in range(T):
                        dve.wait_ge(d_yg[t // 4], 4 * 16)
                        if t == 0:
                            dve.wait_ge(v_sub, 3)
                        nc.vector.scalar_tensor_tensor(X2[:, t, :], XN[:, t, :], gate[:, t:t + 1], X2[:, t, :],
                                                       ALU.mult, ALU.add).then_inc(v_out, 1)


def kernel(**inputs):
    import numpy as np
    import concourse.bacc as bacc
    from concourse.bass_utils import run_bass_kernel_spmd

    g = {k: np.asarray(v) for k, v in inputs.items()}
    c = np.ascontiguousarray
    ctx = g["ctx_1024"]
    arrays = {
        "x": g["x"], "ctxT": c(ctx.transpose(2, 0, 1).reshape(D, B * T)),
        "wqT": c(g["L0_attn_Wq"].T), "wkT": c(g["L0_attn_Wk"].T), "wvT": c(g["L0_attn_Wv"].T),
        "wi0T": c(g["L0_xattn_Wi0"].T), "wh0T": c(g["L0_xattn_Wh0"].T),
        "bi0": g["L0_xattn_bi0"], "bh0": g["L0_xattn_bh0"],
        "wi1T": c(g["L0_xattn_Wi1"].T), "wh1T": c(g["L0_xattn_Wh1"].T),
        "bi1": g["L0_xattn_bi1"], "bh1": g["L0_xattn_bh1"],
        "xwq": g["L0_xattn_Wq"], "woT": c(g["L0_xattn_Wo"].T), "bo": g["L0_xattn_bo"],
        "rw": g["L0_ffn_router_W"], "rb": g["L0_ffn_router_b"],
        "w1": g["L0_ffn_W1"], "b1": g["L0_ffn_b1"],
        "w2": g["L0_ffn_W2"], "b2": g["L0_ffn_b2"],
    }
    nc = bacc.Bacc("TRN2", target_bir_lowering=False, num_devices=1)
    aps = {}
    feed = {}
    for name, a in arrays.items():
        a = c(a)
        feed[f"in_{name}"] = a
        aps[name] = nc.dram_tensor(f"in_{name}", a.shape, mybir.dt.from_np(a.dtype), kind="ExternalInput").ap()
    o = nc.dram_tensor("out_0", [B, T, D], F32, kind="ExternalOutput").ap()
    decoder_kernel(nc, out=o, **aps)
    r = run_bass_kernel_spmd(nc, [feed], core_ids=[0])
    return r.results[0]["out_0"]
```

```python
from contextlib import ExitStack

import concourse.bass as bass
from concourse import mybir

F32 = mybir.dt.float32
F16 = mybir.dt.float16
BF16 = mybir.dt.bfloat16
I32 = mybir.dt.int32
U32 = mybir.dt.uint32
ALU = mybir.AluOpType
ACT = mybir.ActivationFunctionType
AX = mybir.AxisListType

P = 128
B, T, D = 128, 64, 128
NPAIR = B // 2
NH, DK = 16, 8
HG = 4
EPS = 1e-5
GB = B // 2
GP = GB // 2
NE, FF = 8, 512
FC = FF // P
WIDE = 512 // GP
PAD = (WIDE - 4) // 2
NSPLIT = 24
S = 4096.0
NT = B * T // P + NE
AT_X2, AT_GATE, AT_ROW, ROW = D, 2 * D, 2 * D + 1, 2 * D + 2
NOWHERE = 2 * B * T
WX0, WA0, WH0, WI1, WH1 = 0, 4, 8, 12, 16


def wait(eng, semaphore, value):
    if not (isinstance(value, int) and value <= 0):
        eng.wait_ge(semaphore, value)


def decoder_kernel(nc, x, ctxT, wqT, wkT, wvT, wi0T, wh0T, bi0, bh0, wi1T, wh1T, bi1, bh1,
                   xwq, woT, bo, rw, rb, w1, b1, w2, b2, out):
    x1_dram = nc.dram_tensor("x1_scratch", [B, T, D], F32, kind="Internal").ap()
    xs_dram = nc.dram_tensor("sorted_x", [NT * P, ROW], F32, kind="Internal").ap()

    with ExitStack() as persist:
        block_sems = []

        def sem(name):
            block_sems.append(nc.alloc_semaphore(name=name))
            return block_sems[-1]

        def clear_semaphores():
            nc.clear_and_free_semaphores(block_sems)
            nc.all_engine_barrier()
            block_sems.clear()

        def sbp(name, shape, dt=F32):
            return persist.enter_context(nc.sbuf_tensor(name, shape, dt))

        ident = sbp("ident", [P, P])
        ones = sbp("ones", [P, P])
        pm = sbp("pm", [P, 2])
        X = sbp("X", [P, NPAIR * D])
        Xp = X[:, :].rearrange("p (n d) -> p n d", d=D)
        XA = X[:, :].rearrange("p (t b) -> p t b", b=B)

        s_const = sem("s_const")

        x1_st = sbp("x1_st", [P, NPAIR, 6])
        x1_stf = x1_st[:, :, :].rearrange("p n k -> p (n k)")

        recurrence_ctx = ExitStack()

        def sbr(name, shape, dt=F32):
            return recurrence_ctx.enter_context(nc.sbuf_tensor(name, shape, dt))

        KH = sbr("KH", [P, 2, B * T], F16)
        VH = sbr("VH", [P, 2, NPAIR, D], F16)
        XT = sbr("XT", [P, 2, T, B], F16)
        WL = sbr("WL", [P, 20, 2, P], F16)
        WO2 = sbr("WO2", [P, 2, P], F16)
        BL = sbr("BL", [P, 2, 4 * P], BF16)
        onesb = sbr("onesb", [P, GB], BF16)
        II = sbr("II", [P, 64])
        sc = sbr("sc", [P, 16])
        smask = sbr("smask", [P, 2 * GB])
        pmask = sbr("pmask", [64, 2, 64])
        bo_sb = sbr("bo_sb", [P, 1])
        pw = sbr("pw", [P, 8])
        wq_sb = sbr("wq_sb", [P, P])
        wk_sb = sbr("wk_sb", [P, DK])
        wv_sb = sbr("wv_sb", [P, DK])
        S0, S1, SK, SV, I0, I1, IK, IV = range(8)

        with ExitStack() as c1:
            def sb(name, shape, dt=F32):
                return c1.enter_context(nc.sbuf_tensor(name, shape, dt))

            def ps(name, shape, dt=F32):
                return c1.enter_context(nc.psum_tensor(name, shape, dt))
            CT = XT[:, :, :, :].rearrange("p a t b -> p (a t b)").bitcast(F32)
            wl32 = sb("wl32", [P, 20 * P])
            xwq_sb = sb("xwq_sb", [P, P])
            wo_sb = sb("wo_sb", [P, 2, P])
            bb = sb("bb", [P, 4, 4 * P])
            rowm = sb("rowm", [P, 3])
            bw = sb("bw", [P, 4 * P])
            bhi = sb("bhi", [P, 4 * P], BF16)
            mx = sb("mx", [P, 8])
            mxr = sb("mxr", [8, 1])
            dg = sb("dg", [8, 8])
            gm = sb("gm", [P, 8])
            tmp = sb("tmp", [P, 8])
            par = sb("par", [64, 2])
            ktmp = sb("ktmp", [P, 2, 512])
            psA = ps("psA", [P, 2, 512])
            psV = ps("psV", [P, 2, 512])
            psS = ps("psS", [P, 512])

            s_ctx = sem("s_ctx")
            s_x = sem("s_x")
            s_w = sem("s_w")
            s_b = sem("s_b")
            s_wo = sem("s_wo")
            s_bz = sem("s_bz")
            v_mx = sem("v_mx")
            p_sc = sem("p_sc")
            v_sc = sem("v_sc")
            v_scale = sem("v_scale")
            p_k = sem("p_k")
            p_v = sem("p_v")
            a_k = sem("a_k")
            a_v = sem("a_v")
            v_k = sem("v_k")
            v_v = sem("v_v")
            a_w = sem("a_w")
            v_w = sem("v_w")
            v_b = sem("v_b")
            v_pm = sem("v_pm")

            with nc.Block() as block:
                @block.sync
                def _(sync):
                    sync.dma_start(CT, ctxT).then_inc(s_ctx, 16)
                    sync.dma_start(xwq_sb[:, :], xwq).then_inc(s_wo, 16)
                    sync.dma_start(wo_sb[:, :, :], woT.rearrange("(a p) n -> p a n", a=2)).then_inc(s_wo, 16)
                    sync.dma_start(wq_sb[:, :], wqT).then_inc(s_wo, 16)
                    sync.dma_start(wk_sb[:, :], wkT).then_inc(s_wo, 16)
                    sync.dma_start(wv_sb[:, :], wvT).then_inc(s_wo, 16)
                    sync.dma_start(bo_sb[:, :], bo.rearrange("(p a) -> p a", a=1)).then_inc(s_wo, 16)
                    sync.dma_start(Xp, x.rearrange("(n two) t d -> (two t) n d", two=2)).then_inc(s_x, 16)
                    sync.wait_ge(s_x, 16)

                @block.scalar
                def _(act):
                    w4 = wl32[:, :].rearrange("p (k n) -> p k n", n=4 * P)
                    act.dma_start(w4[:, 0:2, :], wi0T.rearrange("(a p) n -> p a n", a=2)).then_inc(s_w, 16)
                    act.dma_start(w4[:, 2, :], wh0T).then_inc(s_w, 16)
                    act.dma_start(w4[:, 3, :], wi1T).then_inc(s_w, 16)
                    act.dma_start(w4[:, 4, :], wh1T).then_inc(s_w, 16)
                    act.wait_ge(s_bz, 1)
                    for k, src in enumerate((bi0, bh0, bi1, bh1)):
                        for r in (0, 32, 64):
                            act.dma_start(bb[r:r + 1, k, :], src.rearrange("(a n) -> a n", a=1)).then_inc(s_b, 16)
                    act.wait_ge(v_scale, 1)
                    for blk in range(20):
                        col = (S0 if blk < 12 else S1) + (8 if blk % 4 == 2 else 0)
                        nc.scalar.activation(WL[:, blk, 0, :], wl32[:, blk * P:(blk + 1) * P], ACT.Copy,
                                             scale=sc[:, col:col + 1]).then_inc(a_w, 1)
                    nc.scalar.activation(WO2[:, 0, :], wo_sb[:, 1, :], ACT.Copy,
                                         scale=sc[:, SV:SV + 1]).then_inc(a_w, 1)
                    for c in range(16):
                        act.wait_ge(p_k, c + 1)
                        nc.scalar.activation(KH[:, 0, c * 512:(c + 1) * 512], psA[:, c % 2, :], ACT.Copy,
                                             scale=sc[:, SK:SK + 1]).then_inc(a_k, 1)
                        act.wait_ge(p_v, c + 1)
                        nc.scalar.activation(VH[:, 0, 4 * c:4 * c + 4, :],
                                             psV[:, c % 2, :].rearrange("p (n d) -> p n d", d=D), ACT.Copy,
                                             scale=sc[:, SV:SV + 1]).then_inc(a_v, 1)

                @block.gpsimd
                def _(pool):
                    pool.memset(bb[:, :, :], 0.0).then_inc(s_bz, 1)
                    pool.memset(ident[:, :], 0.0).then_inc(s_const, 1)
                    pool.memset(ones[:, :], 1.0).then_inc(s_const, 1)
                    pool.memset(II[:, :], 0.0).then_inc(s_const, 1)
                    pool.memset(rowm[:, :], 0.0).then_inc(s_const, 1)
                    pool.memset(onesb[:, :], 1.0).then_inc(s_const, 1)
                    pool.wait_ge(s_const, 5)
                    pool.affine_select(out=ident[:, :], in_=ident[:, :], compare_op=ALU.not_equal, fill=1.0,
                                       base=0, pattern=[[-1, P]], channel_multiplier=1).then_inc(s_const, 1)
                    pool.affine_select(out=II[:, :], in_=II[:, :], compare_op=ALU.not_equal, fill=1.0,
                                       base=0, pattern=[[-1, 64]], channel_multiplier=1).then_inc(s_const, 1)
                    pool.affine_select(out=rowm[:, :], in_=rowm[:, :], compare_op=ALU.not_equal, fill=1.0,
                                       base=0, pattern=[[-32, 3]], channel_multiplier=1).then_inc(s_const, 1)
                    pool.wait_ge(s_const, 8)
                    pool.affine_select(out=II[:, :], in_=II[:, :], compare_op=ALU.not_equal, fill=1.0,
                                       base=-64, pattern=[[-1, 64]], channel_multiplier=1).then_inc(s_const, 1)

                @block.tensor
                def _(pe):
                    pe.wait_ge(s_const, 9)
                    pe.wait_ge(v_mx, 8)
                    nc.tensor.transpose(psS[0:8, 0:P], mx[:, :], ident[:, :]).then_inc(p_sc, 1)
                    pe.wait_ge(v_sc, 2)
                    nc.tensor.matmul(psS[:, 128:136], ones[0:8, :], dg[:, :], start=True, stop=True).then_inc(p_sc, 1)
                    pe.wait_ge(s_wo, 96)
                    for c in range(16):
                        if c >= 2:
                            pe.wait_ge(v_k, c - 1)
                        nc.tensor.matmul(psA[:, c % 2, :], xwq_sb[:, :], CT[:, c * 512:(c + 1) * 512],
                                         start=True, stop=True).then_inc(p_k, 1)
                        if c >= 2:
                            pe.wait_ge(v_v, c - 1)
                        for n in range(4):
                            mm = nc.tensor.matmul(psV[:, c % 2, n * P:(n + 1) * P],
                                                  CT[:, (4 * c + n) * P:(4 * c + n + 1) * P], wo_sb[:, 0, :],
                                                  start=True, stop=True)
                        mm.then_inc(p_v, 1)

                @block.vector
                def _(dve):
                    dve.wait_ge(s_w, 64)
                    nc.vector.tensor_reduce(mx[:, 0:1], wl32[:, 0:12 * P], AX.X, ALU.max,
                                            apply_absolute_value=True).then_inc(v_mx, 1)
                    nc.vector.tensor_reduce(mx[:, 1:2], wl32[:, 12 * P:], AX.X, ALU.max,
                                            apply_absolute_value=True).then_inc(v_mx, 1)
                    dve.wait_ge(s_wo, 96)
                    nc.vector.tensor_reduce(mx[:, 2:3], xwq_sb[:, :], AX.X, ALU.max,
                                            apply_absolute_value=True).then_inc(v_mx, 1)
                    nc.vector.tensor_reduce(mx[:, 3:4], wo_sb[:, :, :], AX.XY, ALU.max,
                                            apply_absolute_value=True).then_inc(v_mx, 1)
                    for k, w in enumerate((wq_sb, wk_sb, wv_sb)):
                        nc.vector.tensor_reduce(mx[:, 5 + k:6 + k], w[:, :], AX.X, ALU.max,
                                                apply_absolute_value=True).then_inc(v_mx, 1)
                    dve.wait_ge(s_ctx, 16)
                    nc.vector.tensor_reduce(mx[:, 4:5], CT, AX.X, ALU.max,
                                            apply_absolute_value=True).then_inc(v_mx, 1)
                    dve.wait_ge(p_sc, 1)
                    nc.vector.tensor_reduce(mxr[:, :], psS[0:8, 0:P], AX.X, ALU.max).then_inc(v_sc, 1)
                    dve.wait_ge(v_sc, 1)
                    nc.vector.tensor_scalar(dg[:, :], ident[0:8, 0:8], mxr[:, 0:1], None, ALU.mult).then_inc(v_sc, 1)
                    dve.wait_ge(p_sc, 2)
                    n = 2

                    def step(ins):
                        nonlocal n
                        n += 1
                        ins.then_inc(v_sc, 1)
                        dve.wait_ge(v_sc, n)
                    step(nc.vector.tensor_scalar(gm[:, :], psS[:, 128:136], 1e-12, 1e12, ALU.max, ALU.min))
                    step(nc.vector.tensor_scalar(pw[:, :].bitcast(I32), gm[:, :].bitcast(I32), 0x7F800000, None,
                                                 ALU.bitwise_and))
                    step(nc.vector.tensor_scalar(tmp[:, 0:2], pw[:, 0:2], 2.0 ** -13, None, ALU.mult))
                    step(nc.vector.scalar_tensor_tensor(tmp[:, 2:3], pw[:, 4:5], 2.0 ** -6, pw[:, 2:3],
                                                        ALU.mult, ALU.mult))
                    step(nc.vector.tensor_scalar(tmp[:, 4:5], pw[:, 4:5], 2.0 ** -8, 2.0 ** -6, ALU.max, ALU.mult))
                    step(nc.vector.tensor_tensor(tmp[:, 3:4], tmp[:, 4:5], pw[:, 3:4], ALU.mult))
                    step(nc.vector.reciprocal(sc[:, 0:4], tmp[:, 0:4]))
                    step(nc.vector.tensor_scalar(sc[:, 4:6], tmp[:, 0:2], 0.5 / S, None, ALU.mult))
                    step(nc.vector.tensor_scalar(sc[:, 6:8], tmp[:, 2:4], 1.0 / S, None, ALU.mult))
                    nc.vector.tensor_scalar(sc[:, 8:10], sc[:, 0:2], 2.0, None, ALU.mult).then_inc(v_scale, 1)
                    dve.wait_ge(s_const, 9)
                    nc.vector.tensor_reduce(pm[:, :], ident[:, :].rearrange("p (h k) -> p h k", h=2), AX.X,
                                            ALU.add).then_inc(v_pm, 1)
                    dve.wait_ge(v_pm, 1)
                    nc.vector.tensor_scalar(
                        smask[:, :].rearrange("p (n h k) -> p n h k", h=2, k=2),
                        pm[:, :].unsqueeze(1).unsqueeze(3).broadcast_to([P, GP, 2, 2]),
                        sc[:, IK:IK + 1], None, ALU.mult).then_inc(v_b, 1)
                    nc.vector.tensor_reduce(par[:, 0:1], ident[0:64, 0:64:2], AX.X, ALU.add).then_inc(v_b, 1)
                    nc.vector.tensor_reduce(par[:, 1:2], ident[0:64, 1:64:2], AX.X, ALU.add).then_inc(v_b, 1)
                    dve.wait_ge(v_b, 3)
                    nc.vector.tensor_scalar(pmask[:, :, :], par[:, :].unsqueeze(2).broadcast_to([64, 2, 64]),
                                            S, None, ALU.mult).then_inc(v_b, 1)
                    dve.wait_ge(s_b, 16 * 12)
                    dve.wait_ge(v_scale, 1)
                    n2 = 4

                    def step2(ins):
                        nonlocal n2
                        n2 += 1
                        ins.then_inc(v_b, 1)
                        dve.wait_ge(v_b, n2)
                    for layer in range(2):
                        step2(nc.vector.tensor_tensor(bw[:, :], bb[:, 2 * layer, :], bb[:, 2 * layer + 1, :], ALU.add))
                        step2(nc.vector.tensor_scalar(bw[:, :], bw[:, :], sc[:, layer:layer + 1], S, ALU.mult, ALU.mult))
                        step2(nc.vector.tensor_scalar(bw[:, 2 * P:3 * P], bw[:, 2 * P:3 * P], 2.0, None, ALU.mult))
                        for k in range(3):
                            step2(nc.vector.tensor_copy(bhi[:, :], bw[:, :]))
                            if k == 0:
                                step2(nc.vector.tensor_scalar(BL[:, layer, :], bhi[:, :], rowm[:, 0:1], None, ALU.mult))
                            else:
                                step2(nc.vector.scalar_tensor_tensor(BL[:, layer, :], bhi[:, :], rowm[:, k:k + 1],
                                                                     BL[:, layer, :], ALU.mult, ALU.add))
                            step2(nc.vector.tensor_tensor(bw[:, :], bw[:, :], bhi[:, :], ALU.subtract))
                    for blk in range(20):
                        col = (S0 if blk < 12 else S1) + (8 if blk % 4 == 2 else 0)
                        dve.wait_ge(a_w, blk + 1)
                        nc.vector.scalar_tensor_tensor(WL[:, blk, 1, :], wl32[:, blk * P:(blk + 1) * P],
                                                       sc[:, col:col + 1], WL[:, blk, 0, :],
                                                       ALU.mult, ALU.subtract).then_inc(v_w, 1)
                    dve.wait_ge(a_w, 21)
                    nc.vector.scalar_tensor_tensor(WO2[:, 1, :], wo_sb[:, 1, :], sc[:, SV:SV + 1], WO2[:, 0, :],
                                                   ALU.mult, ALU.subtract).then_inc(v_w, 1)
                    for c in range(16):
                        dve.wait_ge(a_k, c + 1)
                        nc.vector.scalar_tensor_tensor(KH[:, 1, c * 512:(c + 1) * 512], psA[:, c % 2, :],
                                                       sc[:, SK:SK + 1], KH[:, 0, c * 512:(c + 1) * 512],
                                                       ALU.mult, ALU.subtract).then_inc(v_k, 1)
                        dve.wait_ge(a_v, c + 1)
                        nc.vector.scalar_tensor_tensor(
                            VH[:, 1, 4 * c:4 * c + 4, :].rearrange("p n d -> p (n d)"), psV[:, c % 2, :],
                            sc[:, SV:SV + 1], VH[:, 0, 4 * c:4 * c + 4, :].rearrange("p n d -> p (n d)"),
                            ALU.mult, ALU.subtract).then_inc(v_v, 1)

        clear_semaphores()

        with ExitStack() as c2:
            def sb(name, shape, dt=F32):
                return c2.enter_context(nc.sbuf_tensor(name, shape, dt))

            def ps(name, shape, dt=F32):
                return c2.enter_context(nc.psum_tensor(name, shape, dt))
            QA = 4
            DOWN = 2.0 ** -18
            wrep = sb("wrep", [P, QA + 1, HG, 4, DK])
            wst = sb("wst", [P, 2, QA + 1, P], F16)
            wvs = sb("wvs", [P, 2, DK], F16)
            m4 = sb("m4", [P, 4])
            lo = sb("lo", [P, 2])
            s2 = sb("s2", [P, 8])
            pmv = sb("pmv", [P, 2])
            ob = sb("ob", [P, 2, 2, DK])
            st6 = sb("st6", [P, NPAIR, 6])
            mv = sb("mv", [P, NPAIR, 2])
            sd = sb("sd", [P, NPAIR])
            rs = sb("rs", [P, NPAIR])
            xn = sb("xn", [P, 2, D])
            xh = sb("xh", [P, 2, 2, P], F16)
            hq = sb("hq", [P, 512], F16)
            hk = sb("hk", [P, P], F16)
            QS = sb("QS", [P, 2, 512], F16)
            KS = sb("KS", [P, 2, P], F16)
            VB = sb("VB", [P, 2, 2, 2, DK])
            pmx = sb("pmx", [P, 2, NH])
            pr = sb("pr", [P, 2, NH, 64])
            prT = sb("prT", [P, 8, P])
            pv = sb("pv", [P, 512])
            rden = sb("rden", [P, NH])
            yv = sb("yv", [P, NH, DK])
            psSc = ps("psSc", [P, 4, 512])
            psQ = ps("psQ", [P, 512])
            psK = ps("psK", [P, 512])
            psT = ps("psT", [P, 2, 512])

            v_c = sem("v_c")
            v_s2 = sem("v_s2")
            a_w2 = sem("a_w2")
            v_w2 = sem("v_w2")
            v_st = sem("v_st")
            a_sd = sem("a_sd")
            v_rs = sem("v_rs")
            v_xn = sem("v_xn")
            p_xt = sem("p_xt")
            a_xh = sem("a_xh")
            v_xl = sem("v_xl")
            p_q = sem("p_q")
            p_v = sem("p_vb")
            a_hq = sem("a_hq")
            v_qs = sem("v_qs")
            v_vb = sem("v_vb")
            p_s = sem("p_s")
            v_m = sem("v_m")
            v_sub = sem("v_sub")
            a_ex = sem("a_ex")
            p_pt = sem("p_pt")
            a_pt = sem("a_pt")
            p_o = sem("p_o")
            a_o = sem("a_o")
            p_ot = sem("p_ot")
            v_rd = sem("v_rd")
            v_y = sem("v_y")
            v_x1 = sem("v_x1")
            v_x1st = sem("v_x1st")

            def has(n):
                return not isinstance(n, int) or 0 <= n < NPAIR

            def run_steps(eng, step):
                for i in range(-3, 2):
                    step(i, i % 2)
                with eng.Fori(2, NPAIR - 5, 2) as i:
                    step(i, 0)
                    step(i + 1, 1)
                for i in range(NPAIR - 4, NPAIR + 1):
                    step(i, i % 2)

            with nc.Block() as block:
                @block.tensor
                def _(pe):
                    pe.wait_ge(v_c, 5)
                    pe.wait_ge(v_w2, QA + 2)

                    def split3(out, w, x, first=0):
                        for k, (a, b) in enumerate(((0, 0), (1, 0), (0, 1))):
                            mm = nc.tensor.matmul(out, w(a), x(b), start=(k == 0), stop=(k == 2))
                        return mm

                    def scores(n, u):
                        for a in range(QA):
                            for b in range(2):
                                for g in range(4):
                                    mm = nc.tensor.matmul(
                                        psSc[64 * b:64 * b + 64, g, 64 * a:64 * a + 64],
                                        QS[32 * g:32 * g + 32, u, a * P + 64 * b:a * P + 64 * b + 64],
                                        KS[32 * g:32 * g + 32, u, 64 * b:64 * b + 64],
                                        start=True, stop=True)
                        return mm

                    def step(i, u):
                        if has(i + 2):
                            n = i + 2
                            pe.wait_ge(v_xn, n + 1)
                            wait(pe, v_qs, n)
                            wait(pe, v_vb, n - 1)
                            nc.tensor.transpose(psK[:, 0:P], xn[:, u, :], ident[:, :]).then_inc(p_xt, 1)
                        if has(i + 1):
                            n = i + 1
                            pe.wait_ge(v_qs, n + 1)
                            wait(pe, v_sub, n)
                            scores(n, 1 - u).then_inc(p_s, 1)
                        if has(i - 1):
                            n = i - 1
                            pe.wait_ge(a_o, n + 1)
                            wait(pe, v_y, 2 * n)
                            if has(i) and not has(i + 1):
                                pe.wait_ge(v_sub, i + 1)
                            for k in range(4):
                                c0 = 256 + k % 2 * P
                                mm = nc.tensor.transpose(psSc[:, k // 2, c0:c0 + P], pv[:, k * P:(k + 1) * P], ident[:, :])
                            mm.then_inc(p_ot, 1)
                        if has(i):
                            pe.wait_ge(a_ex, i + 1)
                            for hp in range(8):
                                mm = nc.tensor.transpose(psT[:, hp // 4, (hp % 4) * P:(hp % 4 + 1) * P],
                                                         pr[:, u, 2 * hp:2 * hp + 2, :].rearrange("p h k -> p (h k)"),
                                                         ident[:, :])
                                if hp % 4 == 3:
                                    mm.then_inc(p_pt, 1)
                        if has(i + 2):
                            n = i + 2
                            pe.wait_ge(a_xh, n + 1)
                            pe.wait_ge(v_xl, n + 1)
                            for a in range(QA):
                                split3(psQ[:, a * P:(a + 1) * P], lambda k: wst[:, k, a, :], lambda k: xh[:, u, k, :])
                            split3(psK[:, P:2 * P], lambda k: wst[:, k, QA, :], lambda k: xh[:, u, k, :]).then_inc(p_q, 1)
                        if has(i + 1):
                            wait(pe, v_vb, i + 1)
                            for b in range(2):
                                for h in range(2):
                                    mm = split3(psK[64 * h:64 * h + 64, 2 * P + DK * b:2 * P + DK * (b + 1)],
                                                lambda k: xh[:, 1 - u, k, 64 * b:64 * b + 64], lambda k: wvs[:, k, :])
                            mm.then_inc(p_v, 1)
                        elif has(i + 2):
                            pe.sem_inc(p_v, 1)
                        if has(i):
                            pe.wait_ge(v_vb, i + 1)
                            for half in range(2):
                                pe.wait_ge(a_pt, 2 * i + half + 1)
                                for w, c0 in ((VB[:, u, :, :, :], 0), (ob[:, :, :, :], 256)):
                                    for j in range(4):
                                        mm = nc.tensor.matmul(psT[32 * j:32 * j + 32, 0, c0 + half * P:c0 + (half + 1) * P],
                                                              w.rearrange("p a b d -> p (a b d)"), prT[:, 4 * half + j, :],
                                                              start=True, stop=True)
                            mm.then_inc(p_o, 1)
                    run_steps(pe, step)

                @block.scalar
                def _(act):
                    act.wait_ge(v_st, 2 * NPAIR + 1)
                    nc.scalar.activation(sd[:, :], sd[:, :], ACT.Sqrt).then_inc(a_sd, 1)
                    act.wait_ge(v_s2, 6)
                    act.wait_ge(v_c, 5)
                    for a in range(QA + 1):
                        nc.scalar.activation(wst[:, 0, a, :], wrep[:, a, :, :, :].rearrange("p g r d -> p (g r d)"), ACT.Copy,
                                             scale=s2[:, a // QA:a // QA + 1]).then_inc(a_w2, 1)
                    nc.scalar.activation(wvs[:, 0, :], wv_sb[:, :], ACT.Copy, scale=s2[:, 2:3]).then_inc(a_w2, 1)

                    def step(i, u):
                        if has(i - 1):
                            n = i - 1
                            act.wait_ge(p_o, n + 1)
                            wait(act, p_ot, n)
                            nc.scalar.activation(pv[:, :], psT[:, 0, :], ACT.Copy).then_inc(a_o, 1)
                        if has(i + 2):
                            n = i + 2
                            act.wait_ge(p_xt, n + 1)
                            nc.scalar.activation(xh[:, u, 0, :], psK[:, 0:P], ACT.Copy, scale=S).then_inc(a_xh, 1)
                        if has(i):
                            wait(act, p_o, i)
                            for k in range(2):
                                act.wait_ge(p_pt, 2 * i + k + 1)
                                nc.scalar.activation(prT[:, 4 * k:4 * k + 4, :].rearrange("p n t -> p (n t)"),
                                                     psT[:, k, :], ACT.Copy).then_inc(a_pt, 1)
                        if has(i + 2):
                            n = i + 2
                            act.wait_ge(p_q, n + 1)
                            wait(act, v_qs, n)
                            nc.scalar.activation(hq[:, :], psQ[:, :], ACT.Copy, scale=lo[:, 0:1]).then_inc(a_hq, 1)
                            act.wait_ge(p_v, i + 3)
                            nc.scalar.activation(hk[:, :], psK[:, P:2 * P], ACT.Copy, scale=lo[:, 1:2]).then_inc(a_hq, 1)
                        if has(i + 1):
                            act.wait_ge(v_sub, i + 2)
                            pn = pr[:, 1 - u, :, :].rearrange("p h k -> p (h k)")
                            nc.scalar.activation(pn, pn, ACT.Exp, scale=s2[:, 3:4]).then_inc(a_ex, 1)
                    run_steps(act, step)

                @block.vector
                def _(dve):
                    nc.vector.tensor_copy(
                        wrep[:, 0:QA, :, :, :].rearrange("p a g r d -> p (a g) r d"),
                        wq_sb[:, :].rearrange("p (h d) -> p h d", d=DK).unsqueeze(2).broadcast_to([P, NH, 4, DK])).then_inc(v_c, 1)
                    nc.vector.tensor_copy(
                        wrep[:, QA, :, :, :].rearrange("p g r d -> p (g r) d"),
                        wk_sb[:, :].unsqueeze(1).broadcast_to([P, 16, DK])).then_inc(v_c, 1)
                    nc.vector.tensor_reduce(m4[:, :], ident[:, :].rearrange("p (g r d) -> p r g d", g=4, r=4),
                                            AX.XY, ALU.add).then_inc(v_c, 1)
                    for b in range(2):
                        nc.vector.tensor_copy(ob[:, b, :, :], pm[:, :].unsqueeze(2).broadcast_to([P, 2, DK])).then_inc(v_c, 1)
                    dve.wait_ge(v_c, 5)
                    nc.vector.tensor_scalar(s2[:, 5:8], pw[:, 5:8], 2.0 ** -13, None, ALU.mult).then_inc(v_s2, 1)
                    dve.wait_ge(v_s2, 1)
                    nc.vector.reciprocal(s2[:, 0:3], s2[:, 5:8]).then_inc(v_s2, 1)
                    nc.vector.scalar_tensor_tensor(s2[:, 3:4], pw[:, 5:6], 2.0 ** -14 * DK ** -0.5, pw[:, 6:7],
                                                   ALU.mult, ALU.mult).then_inc(v_s2, 1)
                    nc.vector.tensor_scalar(s2[:, 4:5], pw[:, 7:8], 2.0 ** -13 / S, None, ALU.mult).then_inc(v_s2, 1)
                    dve.wait_ge(v_s2, 4)
                    nc.vector.tensor_scalar(pmv[:, :], pm[:, :], s2[:, 4:5], None, ALU.mult).then_inc(v_s2, 1)
                    nc.vector.tensor_tensor(lo[:, 0:1], m4[:, 2:3], m4[:, 3:4], ALU.add).then_inc(v_c, 1)
                    nc.vector.tensor_tensor(lo[:, 1:2], m4[:, 1:2], m4[:, 3:4], ALU.add).then_inc(v_c, 1)
                    dve.wait_ge(v_c, 7)
                    nc.vector.tensor_scalar(lo[:, :], lo[:, :], DOWN, None, ALU.mult).then_inc(v_s2, 1)
                    for n in range(NPAIR):
                        nc.vector.bn_stats(st6[:, n, :], Xp[:, n, :]).then_inc(v_st, 1)
                    for n in range(NPAIR):
                        dve.wait_ge(v_st, n + 1)
                        nc.vector.bn_aggr(mv[:, n, :], st6[:, n, :]).then_inc(v_st, 1)
                    dve.wait_ge(v_st, 2 * NPAIR)
                    nc.vector.tensor_scalar(sd[:, :], mv[:, :, 1], EPS, None, ALU.add).then_inc(v_st, 1)
                    for a in range(QA + 1):
                        dve.wait_ge(a_w2, a + 1)
                        nc.vector.scalar_tensor_tensor(wst[:, 1, a, :], wrep[:, a, :, :, :].rearrange("p g r d -> p (g r d)"),
                                                       s2[:, a // QA:a // QA + 1], wst[:, 0, a, :],
                                                       ALU.mult, ALU.subtract).then_inc(v_w2, 1)
                    dve.wait_ge(a_w2, QA + 2)
                    nc.vector.scalar_tensor_tensor(wvs[:, 1, :], wv_sb[:, :], s2[:, 2:3], wvs[:, 0, :],
                                                   ALU.mult, ALU.subtract).then_inc(v_w2, 1)
                    dve.wait_ge(a_sd, 1)
                    nc.vector.reciprocal(rs[:, :], sd[:, :]).then_inc(v_rs, 1)
                    dve.wait_ge(v_rs, 1)
                    dve.wait_ge(v_s2, 6)
                    mvf = mv[:, :, :].rearrange("p n k -> p (n k)")

                    def step(i, u):
                        if has(i + 2):
                            n = i + 2
                            dve.wait_ge(a_xh, n + 1)
                            nc.vector.scalar_tensor_tensor(xh[:, u, 1, :], psK[:, 0:P], S, xh[:, u, 0, :],
                                                           ALU.mult, ALU.subtract).then_inc(v_xl, 1)
                        if has(i + 3):
                            n = i + 3
                            wait(dve, p_xt, n - 1)
                            wait(dve, v_x1, i - 1)
                            nc.vector.tensor_scalar(xn[:, 1 - u, :], X[:, bass.ds(n * D, D)], mvf[:, bass.ds(n * 2, 1)],
                                                    rs[:, bass.ds(n, 1)], ALU.subtract, ALU.mult).then_inc(v_xn, 1)
                        if has(i - 2):
                            if not has(i + 3):
                                dve.wait_ge(v_x1, i - 1)
                            nc.vector.bn_stats(x1_stf[:, bass.ds((i - 2) * 6, 6)],
                                               X[:, bass.ds((i - 2) * D, D)]).then_inc(v_x1st, 1)
                        if has(i + 1):
                            n = i + 1
                            dve.wait_ge(p_s, n + 1)
                            if has(i - 1):
                                dve.wait_ge(p_ot, i)
                            sv = psSc[:, :, 0:256].rearrange("p g (a k) -> p g a k", a=QA)
                            mxv = pmx[:, 1 - u, :].rearrange("p (g a) -> p g a", g=4)
                            nc.vector.tensor_reduce(mxv, sv, AX.X, ALU.max).then_inc(v_m, 1)
                        if has(i - 1):
                            n = i - 1
                            dve.wait_ge(p_ot, n + 1)
                            for b in range(2):
                                q = slice(64 * b, 64 * b + 64)
                                nc.vector.reciprocal(
                                    rden[q, :].rearrange("p (k h) -> p k h", h=2),
                                    psSc[q, 1, 256:512].rearrange("p (k b h d) -> p k b h d", b=2, h=2, d=DK)[:, :, b, :, 0]
                                ).then_inc(v_rd, 1)
                            dve.wait_ge(v_rd, 2 * n + 2)
                            for b in range(2):
                                q = slice(64 * b, 64 * b + 64)
                                nc.vector.tensor_tensor(
                                    yv[q, :, :].rearrange("p (k h) d -> p k h d", h=2),
                                    psSc[q, 0, 256:512].rearrange("p (k b h d) -> p k b h d", b=2, h=2, d=DK)[:, :, b, :, :],
                                    rden[q, :].rearrange("p (k h) -> p k h", h=2).unsqueeze(3).broadcast_to([64, 8, 2, DK]),
                                    ALU.mult).then_inc(v_y, 1)
                        if has(i + 1):
                            n = i + 1
                            dve.wait_ge(v_m, n + 1)
                            wait(dve, p_pt, 2 * (n - 1))
                            nc.vector.tensor_tensor(pr[:, 1 - u, :, :].rearrange("p (g a) k -> p g a k", g=4), sv,
                                                    mxv.unsqueeze(3).broadcast_to([P, 4, QA, 64]),
                                                    ALU.subtract).then_inc(v_sub, 1)
                        if has(i + 2):
                            n = i + 2
                            dve.wait_ge(a_hq, 2 * n + 2)
                            nc.vector.scalar_tensor_tensor(KS[:, u, :], psK[:, P:2 * P], DOWN, hk[:, :],
                                                           ALU.mult, ALU.subtract)
                            nc.vector.scalar_tensor_tensor(QS[:, u, :], psQ[:, :], DOWN, hq[:, :],
                                                           ALU.mult, ALU.subtract).then_inc(v_qs, 1)
                        if has(i + 1):
                            n = i + 1
                            dve.wait_ge(p_v, n + 2)
                            wait(dve, p_o, n - 1)
                            nc.vector.tensor_tensor(
                                VB[:, 1 - u, :, :, :],
                                psK[:, 256:272].rearrange("p (b d) -> p b d", b=2).unsqueeze(2).broadcast_to([P, 2, 2, DK]),
                                pmv[:, :].unsqueeze(1).unsqueeze(3).broadcast_to([P, 2, 2, DK]),
                                ALU.mult).then_inc(v_vb, 1)
                        if has(i - 1):
                            n = i - 1
                            dve.wait_ge(v_y, 2 * n + 2)
                            xrow = X[:, bass.ds(n * D, D)].rearrange("p (a g d) -> p a g d", a=QA, g=4)
                            nc.vector.tensor_tensor(xrow, xrow, yv[:, :, :].rearrange("p (g a) d -> p a g d", g=4),
                                                    ALU.add).then_inc(v_x1, 1)
                    run_steps(dve, step)
                    dve.wait_ge(v_x1, NPAIR)
                    nc.vector.bn_stats(x1_st[:, NPAIR - 1, :], Xp[:, NPAIR - 1, :]).then_inc(v_x1st, 1)

        clear_semaphores()

        with ExitStack() as c3:
            def sb(name, shape, dt=F32):
                return c3.enter_context(nc.sbuf_tensor(name, shape, dt))
            mv = sb("mvb", [P, NPAIR, 2])
            sd = sb("sdb", [P, NPAIR])
            rs = sb("rsb", [P, NPAIR])
            xn = sb("xnb", [P, 8, D])
            psX = c3.enter_context(nc.psum_tensor("psX", [P, 2, 512], F32))
            s_x1 = sem("s_x1")
            v_st = sem("v_st3")
            a_sd = sem("a_sd3")
            v_rs = sem("v_rs3")
            v_xn = sem("v_xn3")
            p_xt = sem("p_xt3")
            a_xt = sem("a_xt3")
            v_xt = sem("v_xt3")
            v_st3z = sem("v_st3z")
            NC4 = NPAIR // 4
            with nc.Block() as block:
                @block.sync
                def _(sync):
                    sync.dma_start(x1_dram.rearrange("(n two) t d -> (two t) n d", two=2), Xp).then_inc(s_x1, 16)
                    sync.wait_ge(s_x1, 16)

                @block.tensor
                def _(pe):
                    for c in range(NC4):
                        if c >= 2:
                            pe.wait_ge(v_xt, c - 1)
                        for n in range(4):
                            pe.wait_ge(v_xn, 4 * c + n + 1)
                            mm = nc.tensor.transpose(psX[:, c % 2, n * P:(n + 1) * P], xn[:, (4 * c + n) % 8, :], ident[:, :])
                        mm.then_inc(p_xt, 1)

                def parts(part, c):
                    return XT[:, part, :, 8 * c:8 * c + 8].rearrange("p t b -> p b t")

                @block.scalar
                def _(act):
                    act.wait_ge(v_st3z, 1)
                    nc.scalar.activation(sd[:, :], sd[:, :], ACT.Sqrt).then_inc(a_sd, 1)
                    for c in range(NC4):
                        act.wait_ge(p_xt, c + 1)
                        nc.scalar.activation(parts(0, c), psX[:, c % 2, :].rearrange("p (b t) -> p b t", t=T),
                                             ACT.Copy, scale=S).then_inc(a_xt, 1)

                @block.vector
                def _(dve):
                    for n in range(NPAIR):
                        nc.vector.bn_aggr(mv[:, n, :], x1_st[:, n, :]).then_inc(v_st, 1)
                    dve.wait_ge(v_st, NPAIR)
                    nc.vector.tensor_scalar(sd[:, :], mv[:, :, 1], EPS, None, ALU.add).then_inc(v_st3z, 1)
                    dve.wait_ge(a_sd, 1)
                    nc.vector.reciprocal(rs[:, :], sd[:, :]).then_inc(v_rs, 1)
                    dve.wait_ge(v_rs, 1)
                    for c in range(NC4 + 1):
                        if c < NC4:
                            if c >= 2:
                                dve.wait_ge(p_xt, c - 1)
                            for n in range(4 * c, 4 * c + 4):
                                nc.vector.tensor_scalar(xn[:, n % 8, :], Xp[:, n, :], mv[:, n, 0:1], rs[:, n:n + 1],
                                                        ALU.subtract, ALU.mult).then_inc(v_xn, 1)
                        if c >= 1:
                            k = c - 1
                            dve.wait_ge(a_xt, k + 1)
                            nc.vector.scalar_tensor_tensor(
                                parts(1, k), psX[:, k % 2, :].rearrange("p (b t) -> p b t", t=T), S, parts(0, k),
                                ALU.mult, ALU.subtract).then_inc(v_xt, 1)

        clear_semaphores()

        with ExitStack() as c4:
            def sb(name, shape, dt=F32):
                return c4.enter_context(nc.sbuf_tensor(name, shape, dt))

            class Group:
                pass
            G = []
            for g in range(2):
                q = Group()
                q.g = g
                t = "ab"[g]
                q.xs = sb(f"xs_{t}", [P, 2, GB], F16)
                q.gt = [sb(f"gt{l}_{t}", [P, 4, GB]) for l in range(2)]
                q.u = [sb(f"u{l}_{t}", [P, 2, GB]) for l in range(2)]
                q.c = [sb(f"c{l}_{t}", [P, GB]) for l in range(2)]
                q.tc = [sb(f"tc{l}_{t}", [P, GB]) for l in range(2)]
                q.os = [sb(f"os{l}_{t}", [P, GB]) for l in range(2)]
                q.h32 = [sb(f"h32{l}_{t}", [P, GB]) for l in range(2)]
                q.h = [sb(f"h{l}_{t}", [P, GB + PAD, 2], F16) for l in range(2)]
                q.a = sb(f"a_{t}", [P, GB, 2], F16)
                q.a32 = sb(f"a32_{t}", [P, GB])
                q.sm = sb(f"sm_{t}", [P, GB, 2])
                q.nm = sb(f"nm_{t}", [64, 1])
                q.p = sb(f"p_{t}", [64, 64])
                q.sum = sb(f"sum_{t}", [64, 1])
                q.r = sb(f"r_{t}", [64, 1])
                q.pe = sb(f"pe_{t}", [P, P])
                q.pm = sb(f"pmv_{t}", [P, GB + PAD, 2], F16)
                q.ar = sb(f"ar_{t}", [P, GB])
                ps = lambda n: c4.enter_context(nc.psum_tensor(f"{n}_{t}", [P, 512], F32))
                q.z = [ps("z0"), ps("z1")]
                q.S = ps("sc")
                q.M = ps("mx")
                q.Sv = q.S[:, :].rearrange("p (n w) -> p n w", w=WIDE)[:, :, 0:4]
                q.Mv = q.M[:, :].rearrange("p (n w) -> p n w", w=WIDE)[:, :, 0:4].rearrange(
                    "p n (b k) -> p n b k", k=2)
                q.s_xs = sem(f"xs_{t}")
                q.s_xu = sem(f"xu_{t}")
                q.s_sc = sem(f"sc_{t}")
                q.s_st = sem(f"st_{t}")
                q.s_pt = sem(f"pt_{t}")
                q.s_mx = sem(f"mx_{t}")
                q.s_ex = sem(f"ex_{t}")
                q.s_ta = sem(f"ta_{t}")
                q.s_sm = sem(f"sm_{t}")
                q.s_nm = sem(f"nm_{t}")
                q.s_r = sem(f"r_{t}")
                q.s_pe = sem(f"pe_{t}")
                q.s_pm = sem(f"pm_{t}")
                q.s_ar = sem(f"ar_{t}")
                q.s_ah = sem(f"ah_{t}")
                q.s_ao = sem(f"ao_{t}")
                q.s_z = [sem(f"z{l}_{t}") for l in range(2)]
                q.s_tg = [sem(f"tg{l}_{t}") for l in range(2)]
                q.s_tc = [sem(f"tc{l}_{t}") for l in range(2)]
                q.s_uv = [sem(f"uv{l}_{t}") for l in range(2)]
                q.s_c = [sem(f"c{l}_{t}") for l in range(2)]
                q.s_os = [sem(f"os{l}_{t}") for l in range(2)]
                q.s_h = [sem(f"h{l}_{t}") for l in range(2)]
                q.s_h32 = [sem(f"h32{l}_{t}") for l in range(2)]
                G.append(q)
            s_zero = sem("s_zero")
            zt = sb("zt", [P, 8, ROW])
            v_zt = sem("v_zt")
            d_z = sem("d_z")

            def run_halves(half, eng):
                half(G[0], None, 0, None)
                half(G[1], G[0], 0, 0)
                half(G[0], G[1], 1, 0)
                with eng.Fori(1, T - 1) as t:
                    half(G[1], G[0], t, t)
                    half(G[0], G[1], t + 1, t)
                half(G[1], G[0], T - 1, T - 1)
                half(None, G[1], None, T - 1)

            with nc.Block() as block:
                @block.sync
                def _(sync):
                    sync.wait_ge(v_zt, 2)
                    for k in range(NT // 8):
                        sync.dma_start(xs_dram[k * 8 * P:(k + 1) * 8 * P, :].rearrange("(p j) d -> p j d", j=8),
                                       zt[:, :, :]).then_inc(d_z, 16)
                    sync.wait_ge(d_z, 16 * (NT // 8))

                @block.tensor
                def _(pe):
                    pe.wait_ge(s_zero, 18)

                    def gates(q, layer, blk, mov, parts=((0, 0), (1, 0), (0, 1))):
                        for j in range(4):
                            for w, m in parts:
                                mm = nc.tensor.matmul(q.z[layer][:, j * GB:(j + 1) * GB], WL[:, blk + j, w, :],
                                                      mov[m], start=False, stop=False, skip_group_check=True)
                        return mm

                    def gates_as_ready(q, layer, blk, mov, ready, t):
                        wait(pe, ready, 2 * t - 1)
                        gates(q, layer, blk, mov, ((0, 0), (1, 0)))
                        wait(pe, ready, 2 * t)
                        return gates(q, layer, blk, mov, ((0, 1),))

                    def bias(q, layer):
                        for j in range(4):
                            nc.tensor.matmul(q.z[layer][:, j * GB:(j + 1) * GB], BL[:, layer, j * P:(j + 1) * P],
                                             onesb[:, :], start=(j == 0), stop=False, skip_group_check=True)

                    def early0h(q):
                        bias(q, 0)
                        gates(q, 0, WH0, [q.h[0][:, 0:GB, k] for k in range(2)])

                    def early0x(q, t):
                        pe.wait_ge(q.s_xs, t + 1)
                        gates(q, 0, WX0, [q.xs[:, k, :] for k in range(2)]).then_inc(q.s_xu, 1)

                    def early1(q):
                        bias(q, 1)
                        gates(q, 1, WH1, [q.h[1][:, 0:GB, k] for k in range(2)])

                    def half(L, A, lt, at):
                        last = isinstance(at, int) and at == T - 1
                        def scores(n0, n1):
                            for n in range(n0, n1):
                                pair = A.g * GP + n
                                for k in range(2):
                                    mm = nc.tensor.matmul(A.S[:, WIDE * n:WIDE * (n + 1)],
                                                          KH[:, k, pair * P:(pair + 1) * P],
                                                          A.h[1][:, 2 * n:2 * n + WIDE // 2, :].rearrange("p b k -> p (b k)"),
                                                          start=(k == 0), stop=(k == 1))
                            return mm
                        if A:
                            pe.wait_ge(A.s_h[1], 2 * at + 2)
                            scores(0, NSPLIT)
                        if L:
                            gates_as_ready(L, 0, WA0, [L.a[:, :, k] for k in range(2)], L.s_ah, lt).then_inc(L.s_z[0], 1)
                        if A:
                            scores(NSPLIT, GP).then_inc(A.s_sc, 1)
                            if not last:
                                early0h(A)
                            pe.wait_ge(A.s_sm, at + 1)
                            for k in range(2):
                                mm = nc.tensor.matmul(A.S[0:64, 0:64], A.sm[:, :, k], II[:, :],
                                                      start=(k == 0), stop=(k == 1))
                            mm.then_inc(A.s_st, 1)
                            if not last:
                                early1(A)
                        if L:
                            gates_as_ready(L, 1, WI1, [L.h[0][:, 0:GB, k] for k in range(2)], L.s_h[0],
                                           lt + 1).then_inc(L.s_z[1], 1)
                        if A:
                            pe.wait_ge(A.s_pe, at + 1)
                            nc.tensor.transpose(A.S[:, 128:256], A.pe[:, :], ident[:, :]).then_inc(A.s_pt, 1)
                            if not last:
                                early0x(A, at + 1)
                        if A:
                            for k, (w, m) in enumerate(((0, 0), (1, 0), (0, 1))):
                                nc.tensor.matmul(A.Mv[:, :, :, 0], WO2[:, w, :],
                                                 A.h[1][:, 0:GB, m].rearrange("p (n b) -> p n b", b=2),
                                                 start=(k == 0), stop=False, skip_group_check=True)
                            pe.wait_ge(A.s_pm, 2 * at + 2)
                            for n in range(GP):
                                pair = A.g * GP + n
                                for k in range(2):
                                    mm = nc.tensor.matmul(A.M[:, WIDE * n:WIDE * (n + 1)], VH[:, k, pair, :],
                                                          A.pm[:, 2 * n:2 * n + WIDE // 2, :].rearrange("p b k -> p (b k)"),
                                                          start=False, stop=False, skip_group_check=True)
                            mm.then_inc(A.s_mx, 1)

                    for q in G:
                        early0h(q)
                        early0x(q, 0)
                        early1(q)
                    run_halves(half, pe)

                @block.scalar
                def _(act):
                    def half(L, A, lt, at):
                        def gate_tanh(l):
                            act.wait_ge(L.s_z[l], lt + 1)
                            nc.scalar.activation(L.gt[l][:, :, :].rearrange("p g b -> p (g b)"), L.z[l][:, 0:4 * GB],
                                                 ACT.Tanh, scale=sc[:, I0 + l:I0 + l + 1]).then_inc(L.s_tg[l], 1)

                        def out_gate(l):
                            act.wait_ge(L.s_tg[l], lt + 1)
                            nc.scalar.activation(L.os[l][:, :], L.gt[l][:, 3, :], ACT.Copy, scale=S / 2,
                                                 bias=S / 2).then_inc(L.s_os[l], 1)

                        def cell_tanh(l):
                            act.wait_ge(L.s_c[l], lt + 1)
                            nc.scalar.activation(L.tc[l][:, :], L.c[l][:, :], ACT.Tanh, scale=0.5).then_inc(L.s_tc[l], 1)
                        if L:
                            gate_tanh(0)
                            out_gate(0)
                            cell_tanh(0)
                        if A:
                            act.wait_ge(A.s_nm, at + 1)
                            nc.scalar.activation(A.p[:, :], A.S[0:64, 0:64], ACT.Exp, bias=A.nm[:, 0:1],
                                                 accum_out=A.sum[:, 0:1]).then_inc(A.s_ex, 1)
                        if L:
                            gate_tanh(1)
                            out_gate(1)
                            cell_tanh(1)
                        if A:
                            act.wait_ge(A.s_ar, at + 1)
                            wait(act, A.s_ao, at)
                            nc.scalar.activation(A.a32[:, :], A.ar[:, :], ACT.Tanh, bias=bo_sb[:, 0:1],
                                                 scale=sc[:, IV:IV + 1]).then_inc(A.s_ta, 1)
                    run_halves(half, act)

                @block.gpsimd
                def _(pool):
                    pool.memset(zt[:, :, :], 0.0).then_inc(v_zt, 1)
                    pool.wait_ge(v_zt, 1)
                    pool.memset(zt[:, :, AT_ROW:].bitcast(I32), NOWHERE).then_inc(v_zt, 1)
                    for q in G:
                        for tile in (q.h[0], q.h[1], q.a, q.pm):
                            pool.memset(tile[:, :, :], 0.0).then_inc(s_zero, 1)
                        for tile in (q.c[0], q.c[1]):
                            pool.memset(tile[:, :], 0.0).then_inc(s_zero, 1)
                        for k in range(2):
                            pool.tensor_copy(q.xs[:, k, :], XT[:, k, 0, q.g * GB:(q.g + 1) * GB]).then_inc(s_zero, 1)
                        pool.memset(q.pe[:, :], 0.0).then_inc(s_zero, 1)
                    pool.wait_ge(s_zero, 18)
                    for q in G:
                        pool.sem_inc(q.s_xs, 1)

                    def half(L, A, lt, at):
                        if L:
                            if not (isinstance(lt, int) and lt == T - 1):
                                pool.wait_ge(L.s_xu, lt + 1)
                                pool.tensor_copy(L.xs[:, :, :], XTn(L, lt + 1)).then_inc(L.s_xs, 1)
                        if A:
                            pool.wait_ge(A.s_ta, at + 1)
                            pool.tensor_copy(X[:, bass.ds(at * B + A.g * GB, GB)], A.a32[:, :]).then_inc(A.s_ao, 1)

                    def XTn(L, t):
                        return XTf[:, :, bass.ds(t * B + L.g * GB, GB)]
                    XTf = XT[:, :, :, :].rearrange("p k t b -> p k (t b)")

                    half(G[0], None, 0, None)
                    half(G[1], G[0], 0, 0)
                    half(G[0], G[1], 1, 0)
                    with pool.Fori(1, T - 2) as t:
                        half(G[1], G[0], t, t)
                        half(G[0], G[1], t + 1, t)
                    half(G[1], G[0], T - 2, T - 2)
                    half(G[0], G[1], T - 1, T - 2)
                    half(G[1], G[0], T - 1, T - 1)
                    half(None, G[1], None, T - 1)

                @block.vector
                def _(dve):
                    dve.wait_ge(s_zero, 18)

                    def half(L, A, lt, at):
                        def cell(l):
                            dve.wait_ge(L.s_tg[l], lt + 1)
                            nc.vector.scalar_tensor_tensor(L.u[l][:, 0, :], L.gt[l][:, 1, :], 1.0, L.c[l][:, :],
                                                           ALU.add, ALU.mult).then_inc(L.s_uv[l], 1)
                            nc.vector.scalar_tensor_tensor(L.u[l][:, 1, :], L.gt[l][:, 0, :], 1.0, L.gt[l][:, 2, :],
                                                           ALU.add, ALU.mult).then_inc(L.s_uv[l], 1)
                            dve.wait_ge(L.s_uv[l], 2 * lt + 2)
                            nc.vector.scalar_tensor_tensor(L.c[l][:, :], L.u[l][:, 0, :], 0.5, L.u[l][:, 1, :],
                                                           ALU.mult, ALU.add).then_inc(L.s_c[l], 1)

                        def hidden(l):
                            dve.wait_ge(L.s_tc[l], lt + 1)
                            dve.wait_ge(L.s_os[l], lt + 1)
                            nc.vector.tensor_tensor(L.h[l][:, 0:GB, 0], L.os[l][:, :], L.tc[l][:, :],
                                                    ALU.mult).then_inc(L.s_h[l], 1)
                            nc.vector.tensor_tensor(L.h32[l][:, :], L.os[l][:, :], L.tc[l][:, :],
                                                    ALU.mult).then_inc(L.s_h32[l], 1)

                        def hidden_low(l):
                            dve.wait_ge(L.s_h32[l], lt + 1)
                            dve.wait_ge(L.s_h[l], 2 * lt + 1)
                            nc.vector.tensor_tensor(L.h[l][:, 0:GB, 1], L.h32[l][:, :], L.h[l][:, 0:GB, 0],
                                                    ALU.subtract).then_inc(L.s_h[l], 1)
                        if A:
                            dve.wait_ge(A.s_sc, at + 1)
                            nc.vector.tensor_tensor(A.sm[:, :, :].rearrange("p (n b) k -> p n (b k)", b=2), A.Sv,
                                                    smask[:, :].rearrange("p (n w) -> p n w", w=4), ALU.mult).then_inc(A.s_sm, 1)
                        if L:
                            cell(0)
                        if A:
                            dve.wait_ge(A.s_st, at + 1)
                            nc.vector.tensor_reduce(A.nm[:, :], A.S[0:64, 0:64], AX.X, ALU.max,
                                                    negate=True).then_inc(A.s_nm, 1)
                        if L:
                            hidden(0)
                        if A:
                            dve.wait_ge(A.s_ex, at + 1)
                            nc.vector.reciprocal(A.r[:, :], A.sum[:, :]).then_inc(A.s_r, 1)
                        if L:
                            hidden_low(0)
                        if A:
                            dve.wait_ge(A.s_r, at + 1)
                            nc.vector.scalar_tensor_tensor(
                                A.pe[0:64, :].rearrange("p (h s) -> p h s", h=2),
                                A.p[:, :].unsqueeze(1).broadcast_to([64, 2, 64]), A.r[:, 0:1], pmask[:, :, :],
                                ALU.mult, ALU.mult).then_inc(A.s_pe, 1)
                            dve.wait_ge(A.s_pt, at + 1)
                            nc.vector.tensor_copy(A.pm[:, 0:GB, 0], A.S[:, 128:192]).then_inc(A.s_pm, 1)
                            dve.wait_ge(A.s_pm, 2 * at + 1)
                            nc.vector.tensor_tensor(A.pm[:, 0:GB, 1], A.S[:, 128:192], A.pm[:, 0:GB, 0],
                                                    ALU.subtract).then_inc(A.s_pm, 1)
                        if L:
                            cell(1)
                        if L:
                            hidden(1)
                            hidden_low(1)
                        if A:
                            dve.wait_ge(A.s_mx, at + 1)
                            nc.vector.tensor_reduce(A.ar[:, :].rearrange("p (n b) -> p n b", b=2), A.Mv,
                                                    AX.X, ALU.add).then_inc(A.s_ar, 1)
                        if A:
                            dve.wait_ge(A.s_ta, at + 1)
                            nc.vector.tensor_scalar(A.a[:, :, 0], A.a32[:, :], S, None, ALU.mult).then_inc(A.s_ah, 1)
                            dve.wait_ge(A.s_ah, 2 * at + 1)
                            nc.vector.scalar_tensor_tensor(A.a[:, :, 1], A.a32[:, :], S, A.a[:, :, 0],
                                                           ALU.mult, ALU.subtract).then_inc(A.s_ah, 1)
                    run_halves(half, dve)
        recurrence_ctx.close()

        clear_semaphores()

        with ExitStack() as c5:
            def sb(name, shape, dt=F32):
                return c5.enter_context(nc.sbuf_tensor(name, shape, dt))

            def ps(name, shape, dt=F32):
                return c5.enter_context(nc.psum_tensor(name, shape, dt))
            TOK = sb("TOK", [P, T, ROW])
            XN = TOK[:, :, 0:D]
            X2 = TOK[:, :, AT_X2:AT_GATE]
            w1_sb = sb("w1_sb", [P, NE * FF])
            w2_sb = sb("w2_sb", [P, NE * FC * D])
            b1_sb = sb("b1_sb", [P, NE * FF])
            b2_sb = sb("b2_sb", [P, NE * D])
            rw_sb = sb("rw_sb", [P, NE])
            rbb = sb("rbb", [P, NE])
            wgt = sb("wgt", [P, NE])
            upper = sb("upper", [P, P])
            st6 = sb("st6c", [P, T, 6])
            mv = sb("mvc", [P, T, 2])
            sd = sb("sdc", [P, T])
            rs = sb("rsc", [P, T])
            xT = sb("xTc", [P, 2, 512])
            lg = sb("lg", [P, T, NE])
            m1 = sb("m1", [P, T])
            eg = sb("eg", [P, T, NE])
            one = sb("one", [P, T, NE])
            tot = sb("tot", [P, T, NE])
            cum = sb("cum", [P, NE, T])
            onesT = sb("onesT", [P, T])
            cnt = sb("cnt", [P, NE])
            cnti = sb("cnti", [P, NE], I32)
            pad = sb("pad", [P, NE])
            end = sb("end", [P, NE])
            slotf = sb("slotf", [P, T])
            slot = sb("slot", [P, T], U32)
            tilestart = sb("tilestart", [P, NT])
            past = sb("past", [P, NT, NE])
            tex = sb("tex", [P, NT])
            etab = sb("etab", [P, 2, NT], I32)
            xg = sb("xg", [P, 2, D])
            xgT = sb("xgT", [P, 2, P])
            hb = sb("hb", [P, 2, FF])
            hT = sb("hT", [P, 2, FC, P])
            xr = sb("xr", [P, 4, ROW - AT_X2])
            yb = sb("yb", [P, 2, D])
            ys = sb("ys", [P, 4, D])
            psX = ps("psX5", [P, 2, 512])
            psH = ps("psH", [P, 2, 512])
            psHT = ps("psHT", [P, 2, 512])
            psY = ps("psY", [P, 2, 512])
            psL, psU, psN = psH[:, 0, :], psH[:, 1, :], psHT[:, 0, :]
            NG = 4
            TG = T // NG
            CG = TG // 4
            s_x2 = [sem(f"s_x2{g}") for g in range(NG)]
            s_rw = sem("s_rw")
            s_wf = sem("s_wf")
            p_a = sem("p_a5")
            v_x2 = sem("v_x2")
            v_st = sem("v_st5")
            v_ag = sem("v_ag5")
            v_sd = sem("v_sd5")
            a_sd = sem("a_sd5")
            v_rs = sem("v_rs5")
            v_xn = sem("v_xn5")
            p_t = sem("p_t5")
            a_t = sem("a_t5")
            p_l = sem("p_l5")
            v_r = sem("v_r5")
            v_one = sem("v_one")
            v_sub = sem("v_sub5")
            a_eg = sem("a_eg")
            p_n = sem("p_n5")
            v_slot = sem("v_slot")
            g_c = sem("g_c")
            v_c = sem("v_c5")
            d_sc = sem("d_sc")
            d_xg = [sem(f"d_xg{u}") for u in range(2)]
            p_xt = sem("p_xt5")
            a_xt = sem("a_xt5")
            p_h = sem("p_h")
            v_hb = sem("v_hb")
            p_ht = sem("p_ht")
            a_ht = sem("a_ht")
            p_y = sem("p_y")
            v_ys = sem("v_ys")
            d_xr = [sem(f"d_xr{u}") for u in range(4)]
            v_yb = sem("v_yb")
            g_go = sem("g_go")
            d_ys = [sem(f"d_ys{u}") for u in range(4)]
            NCH = T // 4
            x_rows = xs_dram.rearrange("(j p) d -> p j d", p=P)
            out_rows = out.rearrange("b t d -> (b t) d")

            def run_tiles(eng, step):
                for j in range(6):
                    step(j, j % 4)
                with eng.Fori(6, NT - 5, 4) as j:
                    for k in range(4):
                        step(j + k, (6 + k) % 4)
                for j in range(NT - 2, NT + 1):
                    step(j, j % 4)

            def tile(j):
                return not isinstance(j, int) or 0 <= j < NT

            with nc.Block() as block:
                @block.sync
                def _(sync):
                    sync.dma_start(rw_sb[:, :], rw).then_inc(s_rw, 16)
                    sync.dma_start(rbb[:, :], rb.rearrange("(a n) -> a n", a=1).broadcast_to([P, NE])).then_inc(s_rw, 16)
                    for g in range(NG):
                        sync.dma_start(X2[:, TG * g:TG * (g + 1), :], x1_dram[:, TG * g:TG * (g + 1), :]).then_inc(s_x2[g], 16)
                    sync.dma_start(w1_sb[:, :].rearrange("p (e f) -> p e f", e=NE), w1.rearrange("e p f -> p e f")).then_inc(s_wf, 16)
                    sync.dma_start(w2_sb[:, :].rearrange("p (e c n) -> p e c n", e=NE, c=FC),
                                   w2.rearrange("e (c p) n -> p e c n", p=P)).then_inc(s_wf, 16)
                    sync.dma_start(b1_sb[:, :], b1.rearrange("(a e) f -> a (e f)", a=1).broadcast_to([P, NE * FF])).then_inc(s_wf, 16)
                    sync.dma_start(b2_sb[:, :], b2.rearrange("(a e) f -> a (e f)", a=1).broadcast_to([P, NE * D])).then_inc(s_wf, 16)

                    def load(j, u):
                        wait(sync, p_xt, j - 1)
                        sync.dma_start(xg[:, u % 2, :], x_rows[:, bass.ds(j, 1), 0:D].rearrange("p j d -> p (j d)")).then_inc(d_xg[u % 2], 16)

                    def load_rest(j, u):
                        wait(sync, d_ys[u], 4 * (j - u))
                        sync.dma_start(xr[:, u, :], x_rows[:, bass.ds(j, 1), AT_X2:].rearrange("p j d -> p (j d)")).then_inc(d_xr[u], 16)
                    sync.wait_ge(d_sc, 16 * T)

                    def step(j, u):
                        if tile(j):
                            load(j, u)
                        if tile(j - 2):
                            load_rest(j - 2, (u + 2) % 4)
                    run_tiles(sync, step)
                    load_rest(NT - 1, (NT - 1) % 4)
                    for u in range(4):
                        sync.wait_ge(d_ys[u], 4 * NT)

                @block.gpsimd
                def _(pool):
                    pool.memset(upper[:, :], 1.0).then_inc(g_c, 1)
                    pool.wait_ge(g_c, 1)
                    pool.affine_select(out=upper[:, :], in_=upper[:, :], compare_op=ALU.is_gt, fill=0.0,
                                       base=0, pattern=[[1, P]], channel_multiplier=-1).then_inc(g_c, 1)
                    pool.iota(TOK[:, :, AT_ROW:].bitcast(I32), pattern=[[1, T], [0, 1]], base=0,
                              channel_multiplier=T).then_inc(g_c, 1)
                    pool.wait_ge(g_c, 3)
                    pool.wait_ge(v_sub, 3)
                    for t in range(T):
                        pool.wait_ge(v_slot, 1)
                        pool.indirect_dma_start(xs_dram, bass.IndirectOffsetOnAxis(slot[:, t:t + 1], 0),
                                                TOK[:, t, :], None).then_inc(d_sc, 16)
                    last_row = pool.to_reg(B * T - 1)

                    def store(j, u):
                        pool.wait_ge(v_ys, j + 1)
                        pool.sem_inc(g_go, 1)
                        pool.indirect_dma_start(out_rows, bass.IndirectOffsetOnAxis(
                            xr[:, u, ROW - 1 - AT_X2:].bitcast(U32), 0), ys[:, u, :], None,
                            bounds_check=last_row, oob_is_err=False).then_inc(d_ys[u], 16)

                    def step(j, u):
                        if tile(j):
                            store(j, u)
                    run_tiles(pool, step)

                @block.tensor
                def _(pe):
                    def turn_back(g):
                        for c in range(CG * g, CG * (g + 1)):
                            if c >= 2:
                                pe.wait_ge(v_x2, c - 1)
                            for n in range(4):
                                mm = nc.tensor.transpose(psHT[:, c % 2, n * P:(n + 1) * P], XA[:, 4 * c + n, :], ident[:, :])
                            mm.then_inc(p_a, 1)

                    def logits(c):
                        pe.wait_ge(a_t, c + 1)
                        for n in range(4):
                            t = 4 * c + n
                            mm = nc.tensor.matmul(psL[:, t * NE:(t + 1) * NE], xT[:, c % 2, n * P:(n + 1) * P], rw_sb[:, :],
                                                  start=True, stop=True)
                        mm.then_inc(p_l, 1)
                    turn_back(0)
                    pe.wait_ge(s_rw, 32)
                    for g in range(NG):
                        if g + 1 < NG:
                            turn_back(g + 1)
                        for c in range(CG * g, CG * (g + 1)):
                            if c >= 2:
                                pe.wait_ge(a_t, c - 1)
                            for n in range(4):
                                pe.wait_ge(v_xn, 4 * c + n + 1)
                                mm = nc.tensor.transpose(psX[:, c % 2, n * P:(n + 1) * P], XN[:, 4 * c + n, :], ident[:, :])
                            mm.then_inc(p_t, 1)
                            if c >= 1:
                                logits(c - 1)
                    logits(NCH - 1)
                    pe.wait_ge(g_c, 2)
                    pe.wait_ge(v_one, 1)
                    of = one[:, :, :].rearrange("p t e -> p (t e)")
                    nc.tensor.matmul(psN, ones[:, :], of, start=True, stop=True).then_inc(p_n, 1)
                    nc.tensor.matmul(psU, upper[:, :], of, start=True, stop=True).then_inc(p_n, 1)

                    def turn(j, u):
                        pe.wait_ge(d_xg[u], 8 * (j - u) + 16)
                        wait(pe, a_xt, j - 1)
                        nc.tensor.transpose(psX[:, u, 0:P], xg[:, u, :], ident[:, :]).then_inc(p_xt, 1)

                    def first_column(j):
                        return pe.value_load(etab[0:1, 0, bass.ds(j, 1)], min_val=0, max_val=(NE - 1) * FF)

                    def hidden(j, u, col):
                        pe.wait_ge(a_xt, j + 1)
                        wait(pe, v_hb, j - 1)
                        nc.tensor.matmul(psH[:, u, :], xgT[:, u, :], w1_sb[:, bass.ds(col, FF)],
                                         start=True, stop=True).then_inc(p_h, 1)

                    def turn_hidden(j, u):
                        pe.wait_ge(v_hb, j + 1)
                        wait(pe, a_ht, j - 1)
                        for c in range(FC):
                            mm = nc.tensor.transpose(psHT[:, u, c * P:(c + 1) * P], hb[:, u, c * P:(c + 1) * P], ident[:, :])
                        mm.then_inc(p_ht, 1)

                    def output(j, u, col):
                        pe.wait_ge(a_ht, j + 1)
                        wait(pe, v_yb, j - 1)
                        for c in range(FC):
                            mm = nc.tensor.matmul(psY[:, u, 0:P], hT[:, u, c, :], w2_sb[:, bass.ds(col + c * P, P)],
                                                  start=(c == 0), stop=(c == FC - 1))
                        mm.then_inc(p_y, 1)
                    pe.wait_ge(v_slot, 2)
                    pe.wait_ge(s_wf, 64)
                    turn(0, 0)
                    hidden(0, 0, first_column(0))
                    turn(1, 1)

                    def step(j, u4):
                        u = u4 % 2
                        if tile(j + 1):
                            next_col = first_column(j + 1)
                        if tile(j - 1):
                            before_col = first_column(j - 1)
                        if tile(j + 2):
                            turn(j + 2, u)
                        if tile(j):
                            turn_hidden(j, u)
                        if tile(j + 1):
                            hidden(j + 1, 1 - u, next_col)
                        if tile(j - 1):
                            output(j - 1, 1 - u, before_col)
                    run_tiles(pe, step)

                @block.scalar
                def _(act):
                    for c in range(NCH):
                        if c % CG == 0:
                            g = c // CG
                            act.wait_ge(v_sd, g + 1)
                            gs = slice(TG * g, TG * (g + 1))
                            nc.scalar.activation(sd[:, gs], sd[:, gs], ACT.Sqrt).then_inc(a_sd, 1)
                        act.wait_ge(p_t, c + 1)
                        if c >= 2:
                            act.wait_ge(p_l, c - 1)
                        nc.scalar.activation(xT[:, c % 2, :], psX[:, c % 2, :], ACT.Copy).then_inc(a_t, 1)
                    act.wait_ge(v_sub, 2)
                    nc.scalar.activation(eg[:, :, :], eg[:, :, :], ACT.Exp).then_inc(a_eg, 1)

                    def turned(j, u):
                        act.wait_ge(p_xt, j + 1)
                        wait(act, p_h, j - 1)
                        nc.scalar.activation(xgT[:, u, :], psX[:, u, 0:P], ACT.Copy).then_inc(a_xt, 1)

                    def relu(j, u):
                        act.wait_ge(p_ht, j + 1)
                        wait(act, p_y, j - 1)
                        nc.scalar.activation(hT[:, u, :, :].rearrange("p c n -> p (c n)"), psHT[:, u, :],
                                             ACT.Relu).then_inc(a_ht, 1)
                    turned(0, 0)
                    turned(1, 1)

                    def step(j, u4):
                        u = u4 % 2
                        if tile(j + 2):
                            turned(j + 2, u)
                        if tile(j):
                            relu(j, u)
                    run_tiles(act, step)

                @block.vector
                def _(dve):
                    for e in range(NE):
                        dve.memset(wgt[:, e:e + 1], float(NE - e)).then_inc(v_c, 1)
                    dve.memset(onesT[:, :], 1.0).then_inc(v_c, 1)
                    dve.memset(tilestart[:, :], float(P)).then_inc(v_c, 1)
                    dve.memset(pad[:, :], 1.0).then_inc(v_c, 1)

                    def add_a(g):
                        dve.wait_ge(s_x2[g], 16)
                        for c in range(CG * g, CG * (g + 1)):
                            dve.wait_ge(p_a, c + 1)
                            xc = X2[:, 4 * c:4 * c + 4, :]
                            nc.vector.tensor_tensor(xc, psHT[:, c % 2, :].rearrange("p (t d) -> p t d", d=D), xc,
                                                    ALU.add).then_inc(v_x2, 1)
                    add_a(0)
                    for g in range(NG):
                        gs = slice(TG * g, TG * (g + 1))
                        dve.wait_ge(v_x2, CG * (g + 1))
                        for n in range(TG * g, TG * (g + 1)):
                            nc.vector.bn_stats(st6[:, n, :], X2[:, n, :]).then_inc(v_st, 1)
                        for n in range(TG * g, TG * (g + 1)):
                            dve.wait_ge(v_st, n + 1)
                            nc.vector.bn_aggr(mv[:, n, :], st6[:, n, :]).then_inc(v_ag, 1)
                        dve.wait_ge(v_ag, TG * (g + 1))
                        nc.vector.tensor_scalar(sd[:, gs], mv[:, gs, 1], EPS, None, ALU.add).then_inc(v_sd, 1)
                        if g + 1 < NG:
                            add_a(g + 1)
                        dve.wait_ge(a_sd, g + 1)
                        nc.vector.reciprocal(rs[:, gs], sd[:, gs]).then_inc(v_rs, 1)
                        dve.wait_ge(v_rs, g + 1)
                        for n in range(TG * g, TG * (g + 1)):
                            nc.vector.tensor_scalar(XN[:, n, :], X2[:, n, :], mv[:, n, 0:1], rs[:, n:n + 1],
                                                    ALU.subtract, ALU.mult).then_inc(v_xn, 1)
                    full = [P, T, NE]
                    k = 0

                    def step(ins):
                        nonlocal k
                        k += 1
                        ins.then_inc(v_r, 1)
                        dve.wait_ge(v_r, k)
                    dve.wait_ge(p_l, NCH)
                    dve.wait_ge(s_rw, 32)
                    dve.wait_ge(v_c, NE + 3)
                    step(nc.vector.tensor_tensor(lg[:, :, :], psL.rearrange("p (t e) -> p t e", e=NE),
                                                 rbb[:, :].unsqueeze(1).broadcast_to(full), ALU.add))
                    step(nc.vector.tensor_reduce(m1[:, :], lg[:, :, :], AX.X, ALU.max))
                    nc.vector.tensor_tensor(eg[:, :, :], lg[:, :, :], m1[:, :].unsqueeze(2).broadcast_to(full),
                                            ALU.subtract).then_inc(v_sub, 2)
                    step(nc.vector.tensor_tensor(one[:, :, :], lg[:, :, :], m1[:, :].unsqueeze(2).broadcast_to(full), ALU.is_equal))
                    step(nc.vector.tensor_tensor(one[:, :, :], one[:, :, :], wgt[:, :].unsqueeze(1).broadcast_to(full), ALU.mult))
                    step(nc.vector.tensor_reduce(m1[:, :], one[:, :, :], AX.X, ALU.max))
                    nc.vector.tensor_tensor(one[:, :, :], one[:, :, :], m1[:, :].unsqueeze(2).broadcast_to(full),
                                            ALU.is_equal).then_inc(v_one, 1)
                    dve.wait_ge(p_n, 1)
                    step(nc.vector.tensor_copy(tot[:, :, :], psN.rearrange("p (t e) -> p t e", e=NE)))
                    for e in range(NE - 1):
                        nc.vector.tensor_tensor_scan(cum[:, e, :], onesT[:, :], tot[:, :, e], 0.0, ALU.mult, ALU.add).then_inc(v_c, 1)
                    step(nc.vector.tensor_tensor_scan(cum[:, NE - 1, :], onesT[:, :], tot[:, :, NE - 1], 0.0, ALU.mult, ALU.add))
                    dve.wait_ge(v_c, 2 * NE + 2)
                    step(nc.vector.tensor_scalar(cnt[:, :], cum[:, :, T - 1], float(P - 1), None, ALU.add))
                    step(nc.vector.tensor_copy(cnti[:, :], cnt[:, :]))
                    step(nc.vector.tensor_scalar(cnti[:, :], cnti[:, :], -P, None, ALU.bitwise_and))
                    step(nc.vector.tensor_copy(cnt[:, :], cnti[:, :]))
                    step(nc.vector.tensor_tensor_scan(end[:, :], pad[:, :], cnt[:, :], 0.0, ALU.mult, ALU.add))
                    step(nc.vector.tensor_tensor(pad[:, :], end[:, :], cnt[:, :], ALU.subtract))
                    cumv = cum[:, :, :].rearrange("p e t -> p t e")
                    step(nc.vector.tensor_tensor(tot[:, :, :], cumv, tot[:, :, :], ALU.subtract))
                    dve.wait_ge(p_n, 2)
                    step(nc.vector.tensor_tensor(tot[:, :, :], psU.rearrange("p (t e) -> p t e", e=NE), tot[:, :, :], ALU.add))
                    step(nc.vector.tensor_tensor(tot[:, :, :], tot[:, :, :], pad[:, :].unsqueeze(1).broadcast_to(full), ALU.add))
                    step(nc.vector.tensor_tensor(tot[:, :, :], tot[:, :, :], one[:, :, :], ALU.mult))
                    step(nc.vector.tensor_reduce(slotf[:, :], tot[:, :, :], AX.X, ALU.add))
                    nc.vector.tensor_copy(slot[:, :], slotf[:, :]).then_inc(v_slot, 1)
                    step(nc.vector.tensor_tensor_scan(tex[:, :], ones[:, 0:NT], tilestart[:, :], -float(P), ALU.mult, ALU.add))
                    step(nc.vector.tensor_tensor(past[:, :, :], tex[:, :].unsqueeze(2).broadcast_to([P, NT, NE]),
                                                 end[:, :].unsqueeze(1).broadcast_to([P, NT, NE]), ALU.is_ge))
                    step(nc.vector.tensor_reduce(tex[:, :], past[:, :, :], AX.X, ALU.add))
                    step(nc.vector.tensor_scalar(tex[:, :], tex[:, :], float(NE - 1), None, ALU.min))
                    step(nc.vector.tensor_scalar(etab[:, 0, :], tex[:, :], float(FF), None, ALU.mult))
                    nc.vector.tensor_scalar(etab[:, 1, :], tex[:, :], float(D), None, ALU.mult).then_inc(v_slot, 1)
                    dve.wait_ge(a_eg, 1)
                    step(nc.vector.tensor_reduce(m1[:, :], eg[:, :, :], AX.X, ALU.add))
                    nc.vector.reciprocal(TOK[:, :, AT_GATE], m1[:, :]).then_inc(v_sub, 1)
                    dve.wait_ge(v_slot, 2)

                    def add_b1(j, u):
                        col = dve.value_load(etab[0:1, 0, bass.ds(j, 1)], min_val=0, max_val=(NE - 1) * FF)
                        dve.wait_ge(p_h, j + 1)
                        wait(dve, p_ht, j - 1)
                        nc.vector.tensor_tensor(hb[:, u, :], psH[:, u, :], b1_sb[:, bass.ds(col, FF)], ALU.add).then_inc(v_hb, 1)

                    def add_b2(j, u):
                        col = dve.value_load(etab[0:1, 1, bass.ds(j, 1)], min_val=0, max_val=(NE - 1) * D)
                        dve.wait_ge(p_y, j + 1)
                        nc.vector.tensor_tensor(yb[:, u % 2, :], psY[:, u % 2, 0:P], b2_sb[:, bass.ds(col, D)], ALU.add).then_inc(v_yb, 1)

                    def finish(j, u):
                        dve.wait_ge(v_yb, j + 1)
                        dve.wait_ge(d_xr[u], 4 * (j - u) + 16)
                        wait(dve, d_ys[u], 4 * (j - u))
                        nc.vector.scalar_tensor_tensor(ys[:, u, :], yb[:, u % 2, :], xr[:, u, AT_GATE - AT_X2:AT_GATE - AT_X2 + 1],
                                                       xr[:, u, 0:D], ALU.mult, ALU.add).then_inc(v_ys, 1)
                    dve.wait_ge(s_wf, 64)
                    add_b1(0, 0)

                    def tile_step(j, u4):
                        u = u4 % 2
                        if tile(j + 1):
                            add_b1(j + 1, 1 - u)
                        if tile(j - 1):
                            add_b2(j - 1, 1 - u)
                            finish(j - 1, (u4 + 3) % 4)
                    run_tiles(dve, tile_step)


def kernel(**inputs):
    import numpy as np
    import concourse.bacc as bacc
    from concourse.bass_utils import run_bass_kernel_spmd

    g = {k: np.asarray(v) for k, v in inputs.items()}
    c = np.ascontiguousarray
    ctx = g["ctx_1024"]
    arrays = {
        "x": g["x"], "ctxT": c(ctx.transpose(2, 0, 1).reshape(D, B * T)),
        "wqT": c(g["L0_attn_Wq"].T), "wkT": c(g["L0_attn_Wk"].T), "wvT": c(g["L0_attn_Wv"].T),
        "wi0T": c(g["L0_xattn_Wi0"].T), "wh0T": c(g["L0_xattn_Wh0"].T),
        "bi0": g["L0_xattn_bi0"], "bh0": g["L0_xattn_bh0"],
        "wi1T": c(g["L0_xattn_Wi1"].T), "wh1T": c(g["L0_xattn_Wh1"].T),
        "bi1": g["L0_xattn_bi1"], "bh1": g["L0_xattn_bh1"],
        "xwq": g["L0_xattn_Wq"], "woT": c(g["L0_xattn_Wo"].T), "bo": g["L0_xattn_bo"],
        "rw": g["L0_ffn_router_W"], "rb": g["L0_ffn_router_b"],
        "w1": g["L0_ffn_W1"], "b1": g["L0_ffn_b1"],
        "w2": g["L0_ffn_W2"], "b2": g["L0_ffn_b2"],
    }
    nc = bacc.Bacc("TRN2", target_bir_lowering=False, num_devices=1)
    aps = {}
    feed = {}
    for name, a in arrays.items():
        a = c(a)
        feed[f"in_{name}"] = a
        aps[name] = nc.dram_tensor(f"in_{name}", a.shape, mybir.dt.from_np(a.dtype), kind="ExternalInput").ap()
    o = nc.dram_tensor("out_0", [B, T, D], F32, kind="ExternalOutput").ap()
    decoder_kernel(nc, out=o, **aps)
    r = run_bass_kernel_spmd(nc, [feed], core_ids=[0])
    return r.results[0]["out_0"]
```
